# Optimizing a Trainium2 kernel written in Bass

```python
import numpy as np
import jax
import jax.numpy as jnp

def _softmax(x, axis=-1):
    return jax.nn.softmax(x, axis=axis)

def _gelu(x):
    return jax.nn.gelu(x, approximate=True)

def _silu(x):
    return jax.nn.silu(x)

def _sigmoid(x):
    return jax.nn.sigmoid(x)

def _layernorm(x, axis=-1, eps=1e-05):
    m = jnp.mean(x, axis=axis, keepdims=True)
    v = jnp.var(x, axis=axis, keepdims=True)
    return (x - m) / jnp.sqrt(v + eps)

def _scatter_add(tgt, idx, src, axis=0):
    return tgt.at[idx].add(src)

def _segment_sum(src, seg, n):
    return jax.ops.segment_sum(src, seg, n)
kernel_name = 'mk_recurrent_d4_jaxref_r8_c793d5'

def setup_inputs(seed: int=0):
    np.random.seed(seed)
    _w = jnp.asarray

    def _L0_attn_setup():
        import jax, jax.numpy as jnp
        import numpy as np
        DIM = 128
        HEADS = 16
        HEAD_DIM = DIM // HEADS
        WINDOW = 64
        NEG = -1000000000.0

        def _sliding_window_attn(x, Wq, bq, Wk, bk, Wv, bv, Wo, bo):
            B, S, D = x.shape
            H, hd, W = (HEADS, HEAD_DIM, WINDOW)
            nb = S // W

            def proj(Wp, bp):
                y = x @ Wp.T + bp
                return y.reshape(B, S, H, hd).transpose(0, 2, 1, 3)
            q = proj(Wq, bq)
            k = proj(Wk, bk)
            v = proj(Wv, bv)
            scale = hd ** (-0.5)
            qb = q.reshape(B, H, nb, W, hd)

            def window_kv(t):
                pad = jnp.concatenate([jnp.zeros((B, H, W, hd), t.dtype), t], axis=2)
                prev = pad[:, :, :S].reshape(B, H, nb, W, hd)
                cur = t.reshape(B, H, nb, W, hd)
                return jnp.concatenate([prev, cur], axis=3)
            kw = window_kv(k)
            vw = window_kv(v)
            scores = jnp.einsum('bhnqd,bhnkd->bhnqk', qb, kw) * scale
            t = jnp.arange(2 * W)
            s_ = jnp.arange(W)[:, None]
            n = jnp.arange(nb)[:, None, None]
            valid = (t <= s_ + W) & (t >= s_ + 1) & (n * W - W + t >= 0)
            scores = jnp.where(valid, scores, NEG)
            attn = jax.nn.softmax(scores, axis=-1)
            out = jnp.einsum('bhnqk,bhnkd->bhnqd', attn, vw)
            out = out.reshape(B, H, S, hd).transpose(0, 2, 1, 3).reshape(B, S, D)
            return out @ Wo.T + bo
        key = jax.random.key(seed)
        ks = jax.random.split(key, 9)
        s = 1.0 / np.sqrt(DIM)
        inp = {'x': jax.random.normal(ks[0], (2, 512, DIM), dtype=jnp.float32)}
        for i, name in enumerate(['q', 'k', 'v', 'o']):
            inp[f'W{name}'] = jax.random.uniform(ks[1 + 2 * i], (DIM, DIM), jnp.float32, -s, s)
            inp[f'b{name}'] = jax.random.uniform(ks[2 + 2 * i], (DIM,), jnp.float32, -s, s)
        return inp
    _L0_attn_in = _L0_attn_setup()

    def _L0_ffn_setup():
        import jax, jax.numpy as jnp
        import numpy as np
        GROUP = 16
        EPS = 1e-05

        def _dequant(q, scale):
            w = q.astype(jnp.float32) / 7.5 - 1.0
            return w * jnp.repeat(scale, GROUP, axis=1)

        def _qlora_linear(x, q, scale, bias, la, lb):
            w = _dequant(q, scale)
            base = jnp.einsum('btd,od->bto', x, w) + bias
            lora = jnp.einsum('btr,or->bto', jnp.einsum('btd,rd->btr', x, la), lb)
            return base + lora

        def _layernorm(x, g, b):
            mu = jnp.mean(x, axis=-1, keepdims=True)
            var = jnp.mean(jnp.square(x - mu), axis=-1, keepdims=True)
            return (x - mu) * jax.lax.rsqrt(var + EPS) * g + b
        key = jax.random.key(seed)
        ks = jax.random.split(key, 6)
        D, R, B, T = (128, 32, 8, 512)
        x = jax.random.normal(ks[0], (B, T, D), dtype=jnp.float32)
        qweights = jax.random.randint(ks[1], (6, D, D), 0, 16, dtype=jnp.int32)
        scales = jax.random.uniform(ks[2], (6, D, D // GROUP), dtype=jnp.float32)
        biases = jax.random.normal(ks[3], (6, D), dtype=jnp.float32) * 0.02
        lora_a = jax.random.normal(ks[4], (6, R, D), dtype=jnp.float32) * 0.02
        lora_b = jax.random.normal(ks[5], (6, D, R), dtype=jnp.float32) * 0.02
        ln_gamma = jnp.ones((3, D), dtype=jnp.float32)
        ln_beta = jnp.zeros((3, D), dtype=jnp.float32)
        return {'x': x, 'qweights': qweights, 'scales': scales, 'biases': biases, 'lora_a': lora_a, 'lora_b': lora_b, 'ln_gamma': ln_gamma, 'ln_beta': ln_beta}
    _L0_ffn_in = _L0_ffn_setup()

    def _L1_attn_setup():
        import math
        import jax, jax.numpy as jnp
        import numpy as np
        HIDDEN = 128
        NUM_LAYERS = 24
        LAYER_ID = 4

        def _time_params():
            h = HIDDEN
            ratio_0_to_1 = LAYER_ID / (NUM_LAYERS - 1)
            ratio_1_to_almost_0 = 1.0 - LAYER_ID / NUM_LAYERS
            zigzag = 0.5 * (jnp.arange(1, h + 1) % 3 - 1)
            time_first = jnp.full(h, math.log(0.3)) + zigzag
            idx = jnp.arange(0, h)
            time_decay = -5 + 8 * (idx / (h - 1)) ** (0.7 + 1.3 * ratio_0_to_1)
            x = jnp.arange(h) / h
            time_mix_key = jnp.power(x, ratio_1_to_almost_0)
            time_mix_value = time_mix_key + 0.3 * ratio_0_to_1
            time_mix_receptance = jnp.power(x, 0.5 * ratio_1_to_almost_0)
            return (time_decay.astype(jnp.float32), time_first.astype(jnp.float32), time_mix_key.astype(jnp.float32), time_mix_value.astype(jnp.float32), time_mix_receptance.astype(jnp.float32))

        def _wkv(time_decay, time_first, k, v):
            B, T, H = k.shape
            td = -jnp.exp(time_decay.astype(jnp.float32))
            tf = time_first.astype(jnp.float32)
            kT = jnp.swapaxes(k, 0, 1).astype(jnp.float32)
            vT = jnp.swapaxes(v, 0, 1).astype(jnp.float32)

            def step(carry, kv):
                num, den, mx = carry
                ck, cv = kv
                max_out = jnp.maximum(mx, ck + tf)
                e1 = jnp.exp(mx - max_out)
                e2 = jnp.exp(ck + tf - max_out)
                out = (e1 * num + e2 * cv) / (e1 * den + e2)
                max_st = jnp.maximum(mx + td, ck)
                e1s = jnp.exp(mx + td - max_st)
                e2s = jnp.exp(ck - max_st)
                return ((e1s * num + e2s * cv, e1s * den + e2s, max_st), out)
            init = (jnp.zeros((B, H), jnp.float32), jnp.zeros((B, H), jnp.float32), jnp.full((B, H), -1e+38, jnp.float32))
            _, outT = jax.lax.scan(step, init, (kT, vT))
            return jnp.swapaxes(outT, 0, 1).astype(k.dtype)
        key = jax.random.key(seed)
        k0, k1, k2, k3, k4 = jax.random.split(key, 5)
        B, T, H = (4, 512, HIDDEN)
        td, tf, tmk, tmv, tmr = _time_params()
        scale = 0.02
        return {'hidden': jax.random.normal(k0, (B, T, H), dtype=jnp.float32), 'Wk': jax.random.normal(k1, (H, H), dtype=jnp.float32) * scale, 'Wv': jax.random.normal(k2, (H, H), dtype=jnp.float32) * scale, 'Wr': jax.random.normal(k3, (H, H), dtype=jnp.float32) * scale, 'Wo': jax.random.normal(k4, (H, H), dtype=jnp.float32) * scale, 'time_decay': td, 'time_first': tf, 'time_mix_key': tmk, 'time_mix_value': tmv, 'time_mix_receptance': tmr}
    _L1_attn_in = _L1_attn_setup()

    def _L1_ffn_setup():
        import jax, jax.numpy as jnp
        import numpy as np
        B, S, DIM = (2, 256, 128)
        HID = 256
        E, NSH, TOPK = (8, 2, 2)

        def _ffn(x, w1, w2, w3):
            return jax.nn.silu(x @ w1.T) * (x @ w3.T) @ w2.T
        key = jax.random.key(seed)
        ks = jax.random.split(key, 8)
        sc = 0.02
        return {'x': jax.random.normal(ks[0], (B, S, DIM), jnp.float32), 'router_w': jax.random.normal(ks[1], (E, DIM), jnp.float32) * sc, 'expert_bias': jnp.zeros((E,), jnp.float32), 'w1': jax.random.normal(ks[2], (E, HID, DIM), jnp.float32) * sc, 'w3': jax.random.normal(ks[3], (E, HID, DIM), jnp.float32) * sc, 'w2': jax.random.normal(ks[4], (E, DIM, HID), jnp.float32) * sc, 'sw1': jax.random.normal(ks[5], (NSH, HID, DIM), jnp.float32) * sc, 'sw3': jax.random.normal(ks[6], (NSH, HID, DIM), jnp.float32) * sc, 'sw2': jax.random.normal(ks[7], (NSH, DIM, HID), jnp.float32) * sc}
    _L1_ffn_in = _L1_ffn_setup()

    def _L2_attn_setup():
        import jax, jax.numpy as jnp
        import numpy as np
        D_MODEL = 128
        N_HEADS = 16
        LATENT_HEADS = 8
        LATENT_DIM = 64
        N_LATENTS = 64
        WINDOW = 32
        HEAD_DIM = D_MODEL // N_HEADS
        LAT_HD = LATENT_DIM // LATENT_HEADS
        B, S = (2, 512)

        def _pool_to_latents(x):
            Bx, Sx, C = x.shape
            chunk = max(1, Sx // N_LATENTS)
            return x.reshape(Bx, N_LATENTS, chunk, C).mean(axis=2)

        def _local_window_attn(Q, K, V):
            Bx, H, Sx, D = Q.shape
            W = WINDOW
            nb = Sx // W
            Qb = Q.reshape(Bx, H, nb, W, D)
            Kp = jnp.pad(K, ((0, 0), (0, 0), (W, 0), (0, 0))).reshape(Bx, H, nb + 1, W, D)
            Vp = jnp.pad(V, ((0, 0), (0, 0), (W, 0), (0, 0))).reshape(Bx, H, nb + 1, W, D)
            Kw = jnp.concatenate([Kp[:, :, :-1], Kp[:, :, 1:]], axis=3)
            Vw = jnp.concatenate([Vp[:, :, :-1], Vp[:, :, 1:]], axis=3)
            i = jnp.arange(W)[:, None]
            j = jnp.arange(2 * W)[None, :]
            base = (j > i) & (j <= i + W)
            blk0 = (jnp.arange(nb) > 0)[:, None, None] | (j >= W)[None, :, :]
            mask = base[None, :, :] & blk0
            sc = jnp.einsum('bhnid,bhnjd->bhnij', Qb, Kw) / np.sqrt(D).astype(np.float32)
            sc = jnp.where(mask[None, None], sc, -jnp.inf)
            p = jax.nn.softmax(sc, axis=-1)
            out = jnp.einsum('bhnij,bhnjd->bhnid', p, Vw)
            return out.reshape(Bx, H, Sx, D)
        key = jax.random.key(seed)
        ks = jax.random.split(key, 11)
        std = 0.02
        w = lambda k, shp: jax.random.normal(k, shp, jnp.float32) * std
        return {'x': jax.random.normal(ks[0], (B, S, D_MODEL), jnp.float32), 'wq': w(ks[1], (D_MODEL, D_MODEL)), 'wk': w(ks[2], (D_MODEL, D_MODEL)), 'wv': w(ks[3], (D_MODEL, D_MODEL)), 'wgq': w(ks[4], (D_MODEL, LATENT_DIM)), 'wgk': w(ks[5], (D_MODEL, LATENT_DIM)), 'wgv': w(ks[6], (D_MODEL, LATENT_DIM)), 'r_out_w': w(ks[7], (LATENT_DIM, D_MODEL)), 'gate_local_w': w(ks[8], (N_HEADS, HEAD_DIM)), 'gate_remote_w': w(ks[9], (N_HEADS, HEAD_DIM)), 'w_out': w(ks[10], (D_MODEL, D_MODEL))}
    _L2_attn_in = _L2_attn_setup()

    def _L2_ffn_setup():
        import jax, jax.numpy as jnp
        import numpy as np
        INPUT_SIZE = 128
        OUTPUT_SIZE = 128
        key = jax.random.key(seed)
        kx, kt, kp, ktn, kpn = jax.random.split(key, 5)
        x = jax.random.normal(kx, (8, 256, INPUT_SIZE), dtype=jnp.float32)
        theta = jax.random.normal(kt, (INPUT_SIZE, OUTPUT_SIZE), dtype=jnp.float32) * 0.02
        phi = jax.random.normal(kp, (INPUT_SIZE, OUTPUT_SIZE), dtype=jnp.float32) * 0.02
        theta_noise = jax.random.normal(ktn, (INPUT_SIZE, OUTPUT_SIZE), dtype=jnp.float32) * 0.01
        phi_noise = jax.random.normal(kpn, (INPUT_SIZE, OUTPUT_SIZE), dtype=jnp.float32) * 0.01
        return {'x': x, 'theta': theta, 'phi': phi, 'theta_noise': theta_noise, 'phi_noise': phi_noise}
    _L2_ffn_in = _L2_ffn_setup()

    def _L3_attn_setup():
        import jax, jax.numpy as jnp
        import numpy as np
        B, N, DE, H, DH = (2, 128, 128, 16, 64)
        DK = H * DH
        MIN_EXP = -30.0
        EPS = 0.0001
        key = jax.random.key(seed)
        ks = jax.random.split(key, 8)

        def g(i, shape, sc=1.0):
            return jax.random.normal(ks[i], shape, jnp.float32) * sc
        freqs = 10000.0 ** (-np.arange(DH // 2, dtype=np.float64) / (DH // 2))
        omega = jnp.asarray(np.tile(freqs[None, :], (H, 1)), jnp.float32)
        return {'x': g(0, (B, N, DE)), 'Wq': g(1, (DE, 2 * DK), 1.0 / np.sqrt(DE)), 'Wk': g(2, (DE, 2 * DK), 1.0 / np.sqrt(DE)), 'Wv': g(3, (DE, 2 * DK), 1.0 / np.sqrt(DE)), 'Wo': g(4, (2 * DK, DE), 1.0 / np.sqrt(2 * DK)), 'omega': omega, 'mu_raw': g(5, (H,)) - 2.0, 'sigma_raw': g(6, (H,)), 'eta_raw': jnp.ones((H,), jnp.float32), 'gamma_raw': jnp.ones((H,), jnp.float32), 'tau': jnp.ones((H,), jnp.float32), 'nu_raw': jnp.ones((H,), jnp.float32) * 4.0}
    _L3_attn_in = _L3_attn_setup()

    def _L3_ffn_setup():
        import jax, jax.numpy as jnp
        import numpy as np
        LN_EPS = 1e-05
        NORM_EPS = 1e-12

        def _layernorm(x, gamma, beta):
            mu = x.mean(axis=-1, keepdims=True)
            var = ((x - mu) ** 2).mean(axis=-1, keepdims=True)
            return (x - mu) * jax.lax.rsqrt(var + LN_EPS) * gamma + beta

        def _l2norm(x, axis):
            n = jnp.sqrt((x ** 2).sum(axis=axis, keepdims=True))
            return x / jnp.maximum(n, NORM_EPS)
        key = jax.random.key(seed)
        ks = jax.random.split(key, 4)
        B, N, D, E, S, H = (64, 32, 128, 16, 16, 32)
        x = jax.random.normal(ks[0], (B, N, D), dtype=jnp.float32)
        mu = jax.random.normal(ks[1], (D, E, S), dtype=jnp.float32) / np.sqrt(D)
        w1 = jax.random.normal(ks[2], (E, D, H), dtype=jnp.float32) * np.sqrt(2.0 / D)
        w2 = jax.random.normal(ks[3], (E, H, D), dtype=jnp.float32) * np.sqrt(2.0 / (H + D))
        return {'x': x, 'ln_gamma': jnp.ones((D,), jnp.float32), 'ln_beta': jnp.zeros((D,), jnp.float32), 'mu': mu, 'scale': jnp.ones((1,), jnp.float32), 'w1': w1, 'b1': jnp.zeros((E, H), jnp.float32), 'w2': w2, 'b2': jnp.zeros((E, D), jnp.float32)}
    _L3_ffn_in = _L3_ffn_setup()
    _d = {'L0_attn_x': _L0_attn_in['x'], 'L0_attn_Wq': _L0_attn_in['Wq'], 'L0_attn_bq': _L0_attn_in['bq'], 'L0_attn_Wk': _L0_attn_in['Wk'], 'L0_attn_bk': _L0_attn_in['bk'], 'L0_attn_Wv': _L0_attn_in['Wv'], 'L0_attn_bv': _L0_attn_in['bv'], 'L0_attn_Wo': _L0_attn_in['Wo'], 'L0_attn_bo': _L0_attn_in['bo'], 'L0_ffn_qweights': _L0_ffn_in['qweights'], 'L0_ffn_scales': _L0_ffn_in['scales'], 'L0_ffn_biases': _L0_ffn_in['biases'], 'L0_ffn_lora_a': _L0_ffn_in['lora_a'], 'L0_ffn_lora_b': _L0_ffn_in['lora_b'], 'L0_ffn_ln_gamma': _L0_ffn_in['ln_gamma'], 'L0_ffn_ln_beta': _L0_ffn_in['ln_beta'], 'L1_attn_Wk': _L1_attn_in['Wk'], 'L1_attn_Wv': _L1_attn_in['Wv'], 'L1_attn_Wr': _L1_attn_in['Wr'], 'L1_attn_Wo': _L1_attn_in['Wo'], 'L1_attn_time_decay': _L1_attn_in['time_decay'], 'L1_attn_time_first': _L1_attn_in['time_first'], 'L1_attn_time_mix_key': _L1_attn_in['time_mix_key'], 'L1_attn_time_mix_value': _L1_attn_in['time_mix_value'], 'L1_attn_time_mix_receptance': _L1_attn_in['time_mix_receptance'], 'L1_ffn_router_w': _L1_ffn_in['router_w'], 'L1_ffn_expert_bias': _L1_ffn_in['expert_bias'], 'L1_ffn_w1': _L1_ffn_in['w1'], 'L1_ffn_w3': _L1_ffn_in['w3'], 'L1_ffn_w2': _L1_ffn_in['w2'], 'L1_ffn_sw1': _L1_ffn_in['sw1'], 'L1_ffn_sw3': _L1_ffn_in['sw3'], 'L1_ffn_sw2': _L1_ffn_in['sw2'], 'L2_attn_wq': _L2_attn_in['wq'], 'L2_attn_wk': _L2_attn_in['wk'], 'L2_attn_wv': _L2_attn_in['wv'], 'L2_attn_wgq': _L2_attn_in['wgq'], 'L2_attn_wgk': _L2_attn_in['wgk'], 'L2_attn_wgv': _L2_attn_in['wgv'], 'L2_attn_r_out_w': _L2_attn_in['r_out_w'], 'L2_attn_gate_local_w': _L2_attn_in['gate_local_w'], 'L2_attn_gate_remote_w': _L2_attn_in['gate_remote_w'], 'L2_attn_w_out': _L2_attn_in['w_out'], 'L2_ffn_theta': _L2_ffn_in['theta'], 'L2_ffn_phi': _L2_ffn_in['phi'], 'L2_ffn_theta_noise': _L2_ffn_in['theta_noise'], 'L2_ffn_phi_noise': _L2_ffn_in['phi_noise'], 'L3_attn_Wq': _L3_attn_in['Wq'], 'L3_attn_Wk': _L3_attn_in['Wk'], 'L3_attn_Wv': _L3_attn_in['Wv'], 'L3_attn_Wo': _L3_attn_in['Wo'], 'L3_attn_omega': _L3_attn_in['omega'], 'L3_attn_mu_raw': _L3_attn_in['mu_raw'], 'L3_attn_sigma_raw': _L3_attn_in['sigma_raw'], 'L3_attn_eta_raw': _L3_attn_in['eta_raw'], 'L3_attn_gamma_raw': _L3_attn_in['gamma_raw'], 'L3_attn_tau': _L3_attn_in['tau'], 'L3_attn_nu_raw': _L3_attn_in['nu_raw'], 'L3_ffn_ln_gamma': _L3_ffn_in['ln_gamma'], 'L3_ffn_ln_beta': _L3_ffn_in['ln_beta'], 'L3_ffn_mu': _L3_ffn_in['mu'], 'L3_ffn_scale': _L3_ffn_in['scale'], 'L3_ffn_w1': _L3_ffn_in['w1'], 'L3_ffn_b1': _L3_ffn_in['b1'], 'L3_ffn_w2': _L3_ffn_in['w2'], 'L3_ffn_b2': _L3_ffn_in['b2']}
    _x0 = _d['L0_attn_x']
    _d['L0_attn_x'] = jax.random.normal(jax.random.fold_in(jax.random.key(seed), 1), (8, 512, 128), dtype=_x0.dtype)
    del _x0
    return _d

def reference(L0_attn_x, L0_attn_Wq, L0_attn_bq, L0_attn_Wk, L0_attn_bk, L0_attn_Wv, L0_attn_bv, L0_attn_Wo, L0_attn_bo, L0_ffn_qweights, L0_ffn_scales, L0_ffn_biases, L0_ffn_lora_a, L0_ffn_lora_b, L0_ffn_ln_gamma, L0_ffn_ln_beta, L1_attn_Wk, L1_attn_Wv, L1_attn_Wr, L1_attn_Wo, L1_attn_time_decay, L1_attn_time_first, L1_attn_time_mix_key, L1_attn_time_mix_value, L1_attn_time_mix_receptance, L1_ffn_router_w, L1_ffn_expert_bias, L1_ffn_w1, L1_ffn_w3, L1_ffn_w2, L1_ffn_sw1, L1_ffn_sw3, L1_ffn_sw2, L2_attn_wq, L2_attn_wk, L2_attn_wv, L2_attn_wgq, L2_attn_wgk, L2_attn_wgv, L2_attn_r_out_w, L2_attn_gate_local_w, L2_attn_gate_remote_w, L2_attn_w_out, L2_ffn_theta, L2_ffn_phi, L2_ffn_theta_noise, L2_ffn_phi_noise, L3_attn_Wq, L3_attn_Wk, L3_attn_Wv, L3_attn_Wo, L3_attn_omega, L3_attn_mu_raw, L3_attn_sigma_raw, L3_attn_eta_raw, L3_attn_gamma_raw, L3_attn_tau, L3_attn_nu_raw, L3_ffn_ln_gamma, L3_ffn_ln_beta, L3_ffn_mu, L3_ffn_scale, L3_ffn_w1, L3_ffn_b1, L3_ffn_w2, L3_ffn_b2):

    def _L0_attn_ref(x, Wq, bq, Wk, bk, Wv, bv, Wo, bo):
        import jax, jax.numpy as jnp
        import numpy as np
        DIM = 128
        HEADS = 16
        HEAD_DIM = DIM // HEADS
        WINDOW = 64
        NEG = -1000000000.0

        def _sliding_window_attn(x, Wq, bq, Wk, bk, Wv, bv, Wo, bo):
            B, S, D = x.shape
            H, hd, W = (HEADS, HEAD_DIM, WINDOW)
            nb = S // W

            def proj(Wp, bp):
                y = x @ Wp.T + bp
                return y.reshape(B, S, H, hd).transpose(0, 2, 1, 3)
            q = proj(Wq, bq)
            k = proj(Wk, bk)
            v = proj(Wv, bv)
            scale = hd ** (-0.5)
            qb = q.reshape(B, H, nb, W, hd)

            def window_kv(t):
                pad = jnp.concatenate([jnp.zeros((B, H, W, hd), t.dtype), t], axis=2)
                prev = pad[:, :, :S].reshape(B, H, nb, W, hd)
                cur = t.reshape(B, H, nb, W, hd)
                return jnp.concatenate([prev, cur], axis=3)
            kw = window_kv(k)
            vw = window_kv(v)
            scores = jnp.einsum('bhnqd,bhnkd->bhnqk', qb, kw) * scale
            t = jnp.arange(2 * W)
            s_ = jnp.arange(W)[:, None]
            n = jnp.arange(nb)[:, None, None]
            valid = (t <= s_ + W) & (t >= s_ + 1) & (n * W - W + t >= 0)
            scores = jnp.where(valid, scores, NEG)
            attn = jax.nn.softmax(scores, axis=-1)
            out = jnp.einsum('bhnqk,bhnkd->bhnqd', attn, vw)
            out = out.reshape(B, H, S, hd).transpose(0, 2, 1, 3).reshape(B, S, D)
            return out @ Wo.T + bo
        return _sliding_window_attn(x, Wq, bq, Wk, bk, Wv, bv, Wo, bo)

    def _L0_ffn_ref(x, qweights, scales, biases, lora_a, lora_b, ln_gamma, ln_beta):
        import jax, jax.numpy as jnp
        import numpy as np
        GROUP = 16
        EPS = 1e-05

        def _dequant(q, scale):
            w = q.astype(jnp.float32) / 7.5 - 1.0
            return w * jnp.repeat(scale, GROUP, axis=1)

        def _qlora_linear(x, q, scale, bias, la, lb):
            w = _dequant(q, scale)
            base = jnp.einsum('btd,od->bto', x, w) + bias
            lora = jnp.einsum('btr,or->bto', jnp.einsum('btd,rd->btr', x, la), lb)
            return base + lora

        def _layernorm(x, g, b):
            mu = jnp.mean(x, axis=-1, keepdims=True)
            var = jnp.mean(jnp.square(x - mu), axis=-1, keepdims=True)
            return (x - mu) * jax.lax.rsqrt(var + EPS) * g + b
        h = x
        for blk in range(3):
            i0, i1 = (2 * blk, 2 * blk + 1)
            y = _qlora_linear(h, qweights[i0], scales[i0], biases[i0], lora_a[i0], lora_b[i0])
            y = _layernorm(y, ln_gamma[blk], ln_beta[blk])
            y = jax.nn.gelu(y, approximate=False)
            y = _qlora_linear(y, qweights[i1], scales[i1], biases[i1], lora_a[i1], lora_b[i1])
            h = y + h
        return h

    def _L1_attn_ref(hidden, Wk, Wv, Wr, Wo, time_decay, time_first, time_mix_key, time_mix_value, time_mix_receptance):
        import math
        import jax, jax.numpy as jnp
        import numpy as np
        HIDDEN = 128
        NUM_LAYERS = 24
        LAYER_ID = 4

        def _time_params():
            h = HIDDEN
            ratio_0_to_1 = LAYER_ID / (NUM_LAYERS - 1)
            ratio_1_to_almost_0 = 1.0 - LAYER_ID / NUM_LAYERS
            zigzag = 0.5 * (jnp.arange(1, h + 1) % 3 - 1)
            time_first = jnp.full(h, math.log(0.3)) + zigzag
            idx = jnp.arange(0, h)
            time_decay = -5 + 8 * (idx / (h - 1)) ** (0.7 + 1.3 * ratio_0_to_1)
            x = jnp.arange(h) / h
            time_mix_key = jnp.power(x, ratio_1_to_almost_0)
            time_mix_value = time_mix_key + 0.3 * ratio_0_to_1
            time_mix_receptance = jnp.power(x, 0.5 * ratio_1_to_almost_0)
            return (time_decay.astype(jnp.float32), time_first.astype(jnp.float32), time_mix_key.astype(jnp.float32), time_mix_value.astype(jnp.float32), time_mix_receptance.astype(jnp.float32))

        def _wkv(time_decay, time_first, k, v):
            B, T, H = k.shape
            td = -jnp.exp(time_decay.astype(jnp.float32))
            tf = time_first.astype(jnp.float32)
            kT = jnp.swapaxes(k, 0, 1).astype(jnp.float32)
            vT = jnp.swapaxes(v, 0, 1).astype(jnp.float32)

            def step(carry, kv):
                num, den, mx = carry
                ck, cv = kv
                max_out = jnp.maximum(mx, ck + tf)
                e1 = jnp.exp(mx - max_out)
                e2 = jnp.exp(ck + tf - max_out)
                out = (e1 * num + e2 * cv) / (e1 * den + e2)
                max_st = jnp.maximum(mx + td, ck)
                e1s = jnp.exp(mx + td - max_st)
                e2s = jnp.exp(ck - max_st)
                return ((e1s * num + e2s * cv, e1s * den + e2s, max_st), out)
            init = (jnp.zeros((B, H), jnp.float32), jnp.zeros((B, H), jnp.float32), jnp.full((B, H), -1e+38, jnp.float32))
            _, outT = jax.lax.scan(step, init, (kT, vT))
            return jnp.swapaxes(outT, 0, 1).astype(k.dtype)
        shifted = jnp.pad(hidden, ((0, 0), (1, 0), (0, 0)))[:, :-1]
        k_in = hidden * time_mix_key + shifted * (1 - time_mix_key)
        v_in = hidden * time_mix_value + shifted * (1 - time_mix_value)
        r_in = hidden * time_mix_receptance + shifted * (1 - time_mix_receptance)
        k = k_in @ Wk
        v = v_in @ Wv
        r = jax.nn.sigmoid(r_in @ Wr)
        rwkv = _wkv(time_decay, time_first, k, v)
        return r * rwkv @ Wo

    def _L1_ffn_ref(x, router_w, expert_bias, w1, w3, w2, sw1, sw3, sw2):
        import jax, jax.numpy as jnp
        import numpy as np
        B, S, DIM = (2, 256, 128)
        HID = 256
        E, NSH, TOPK = (8, 2, 2)

        def _ffn(x, w1, w2, w3):
            return jax.nn.silu(x @ w1.T) * (x @ w3.T) @ w2.T
        bs, sl, d = x.shape
        xf = x.reshape(-1, d)
        shared = jnp.zeros_like(xf)
        for i in range(sw1.shape[0]):
            shared = shared + _ffn(xf, sw1[i], sw2[i], sw3[i])
        logits = xf @ router_w.T + expert_bias
        rw, sel = jax.lax.top_k(logits, TOPK)
        rw = jax.nn.softmax(rw.astype(jnp.float32), axis=-1).astype(x.dtype)
        onehot = jax.nn.one_hot(sel, E, dtype=x.dtype)
        combine = jnp.einsum('tk,tke->te', rw, onehot)

        def body(acc, ew):
            e1, e3, e2, cw = ew
            acc = acc + cw[:, None] * _ffn(xf, e1, e2, e3)
            return (acc, None)
        out, _ = jax.lax.scan(body, jnp.zeros_like(xf), (w1, w3, w2, combine.T))
        out = out + shared
        return out.reshape(bs, sl, -1)

    def _L2_attn_ref(x, wq, wk, wv, wgq, wgk, wgv, r_out_w, gate_local_w, gate_remote_w, w_out):
        import jax, jax.numpy as jnp
        import numpy as np
        D_MODEL = 128
        N_HEADS = 16
        LATENT_HEADS = 8
        LATENT_DIM = 64
        N_LATENTS = 64
        WINDOW = 32
        HEAD_DIM = D_MODEL // N_HEADS
        LAT_HD = LATENT_DIM // LATENT_HEADS
        B, S = (2, 512)

        def _pool_to_latents(x):
            Bx, Sx, C = x.shape
            chunk = max(1, Sx // N_LATENTS)
            return x.reshape(Bx, N_LATENTS, chunk, C).mean(axis=2)

        def _local_window_attn(Q, K, V):
            Bx, H, Sx, D = Q.shape
            W = WINDOW
            nb = Sx // W
            Qb = Q.reshape(Bx, H, nb, W, D)
            Kp = jnp.pad(K, ((0, 0), (0, 0), (W, 0), (0, 0))).reshape(Bx, H, nb + 1, W, D)
            Vp = jnp.pad(V, ((0, 0), (0, 0), (W, 0), (0, 0))).reshape(Bx, H, nb + 1, W, D)
            Kw = jnp.concatenate([Kp[:, :, :-1], Kp[:, :, 1:]], axis=3)
            Vw = jnp.concatenate([Vp[:, :, :-1], Vp[:, :, 1:]], axis=3)
            i = jnp.arange(W)[:, None]
            j = jnp.arange(2 * W)[None, :]
            base = (j > i) & (j <= i + W)
            blk0 = (jnp.arange(nb) > 0)[:, None, None] | (j >= W)[None, :, :]
            mask = base[None, :, :] & blk0
            sc = jnp.einsum('bhnid,bhnjd->bhnij', Qb, Kw) / np.sqrt(D).astype(np.float32)
            sc = jnp.where(mask[None, None], sc, -jnp.inf)
            p = jax.nn.softmax(sc, axis=-1)
            out = jnp.einsum('bhnij,bhnjd->bhnid', p, Vw)
            return out.reshape(Bx, H, Sx, D)
        Bx, Sx, _ = x.shape
        chunk = max(1, Sx // N_LATENTS)
        Q = (x @ wq).reshape(Bx, Sx, N_HEADS, HEAD_DIM).transpose(0, 2, 1, 3)
        K = (x @ wk).reshape(Bx, Sx, N_HEADS, HEAD_DIM).transpose(0, 2, 1, 3)
        V = (x @ wv).reshape(Bx, Sx, N_HEADS, HEAD_DIM).transpose(0, 2, 1, 3)
        local = _local_window_attn(Q, K, V)
        GQ = (x @ wgq).reshape(Bx, Sx, LATENT_HEADS, LAT_HD).transpose(0, 2, 1, 3)
        GK = _pool_to_latents(x @ wgk).reshape(Bx, N_LATENTS, LATENT_HEADS, LAT_HD).transpose(0, 2, 1, 3)
        GV = _pool_to_latents(x @ wgv).reshape(Bx, N_LATENTS, LATENT_HEADS, LAT_HD).transpose(0, 2, 1, 3)
        lsc = jnp.einsum('bhsd,bhnd->bhsn', GQ, GK) / np.sqrt(LAT_HD).astype(np.float32)
        lmask = jnp.arange(N_LATENTS)[None, :] <= (jnp.arange(Sx) // chunk)[:, None]
        lsc = jnp.where(lmask[None, None], lsc, -jnp.inf)
        lp = jax.nn.softmax(lsc, axis=-1)
        rem = jnp.einsum('bhsn,bhnd->bhsd', lp, GV)
        rem = rem.transpose(0, 2, 1, 3).reshape(Bx, Sx, LATENT_DIM) @ r_out_w
        rem = rem.reshape(Bx, Sx, N_HEADS, HEAD_DIM).transpose(0, 2, 1, 3)
        gl = jax.nn.sigmoid(jnp.einsum('bhsd,hd->bhs', Q, gate_local_w))[..., None]
        gr = jax.nn.sigmoid(jnp.einsum('bhsd,hd->bhs', Q, gate_remote_w))[..., None]
        out = gl * local + gr * rem
        out = out.transpose(0, 2, 1, 3).reshape(Bx, Sx, D_MODEL)
        return out @ w_out

    def _L2_ffn_ref(x, theta, phi, theta_noise, phi_noise):
        import jax, jax.numpy as jnp
        import numpy as np
        INPUT_SIZE = 128
        OUTPUT_SIZE = 128
        real = jnp.einsum('bti,io->bto', x, jnp.cos(theta + theta_noise))
        imag = jnp.einsum('bti,io->bto', x, jnp.sin(phi + phi_noise))
        return jnp.sqrt(real * real + imag * imag)

    def _L3_attn_ref(x, Wq, Wk, Wv, Wo, omega, mu_raw, sigma_raw, eta_raw, gamma_raw, tau, nu_raw):
        import jax, jax.numpy as jnp
        import numpy as np
        B, N, DE, H, DH = (2, 128, 128, 16, 64)
        DK = H * DH
        MIN_EXP = -30.0
        EPS = 0.0001
        B_, N_, _ = x.shape
        H_, d_half = omega.shape
        DH_ = 2 * d_half
        DKt = H_ * DH_

        def cproj(W):
            z = x @ W
            D = W.shape[1] // 2
            zc = jax.lax.complex(z[..., :D], z[..., D:])
            return zc.reshape(B_, N_, H_, DH_)
        q, k, v = (cproj(Wq), cproj(Wk), cproj(Wv))
        om = jnp.concatenate([omega, -omega], axis=-1)
        t = jnp.arange(N_, dtype=jnp.float32)
        ang = t[:, None, None] * om[None]
        phase = jax.lax.complex(jnp.cos(ang), jnp.sin(ang))
        qr = q * phase[None]
        kr = k * phase[None]
        mu = jax.nn.sigmoid(mu_raw) + EPS
        dt = jnp.abs(t[:, None] - t[None, :])
        E = jnp.exp(jnp.clip(-mu[:, None, None] * dt[None], MIN_EXP, 0.0))
        s = jnp.einsum('bihd,bjhd->bhij', qr, jnp.conj(kr)).real
        qn = (q.real ** 2 + q.imag ** 2).sum(-1).transpose(0, 2, 1)
        kn = (k.real ** 2 + k.imag ** 2).sum(-1).transpose(0, 2, 1)
        sigma_sq = jax.nn.softplus(sigma_raw)
        eta_sq = jax.nn.softplus(eta_raw)
        gamma_sq = jax.nn.softplus(gamma_raw)
        V = (sigma_sq / (2.0 * mu))[:, None, None] * (1.0 - E * E) + (eta_sq + gamma_sq)[:, None, None]
        maha = jnp.maximum(qn[..., None] + (E * E)[None] * kn[:, :, None, :] - 2.0 * E[None] * s, 0.0) / V[None]
        nu = jax.nn.softplus(nu_raw)
        coef = (-0.5 * tau * (nu + DH_))[None, :, None, None]
        logits = coef * jnp.log1p(maha / nu[None, :, None, None]) - 0.5 * DH_ * jnp.log(V)[None]
        causal = t[:, None] >= t[None, :]
        logits = jnp.where(causal[None, None], logits, -jnp.inf)
        A = jax.nn.softmax(logits, axis=-1)
        out = jnp.einsum('bhij,bjhd->bihd', A.astype(v.dtype), v)
        y = jnp.concatenate([out.real.reshape(B_, N_, DKt), out.imag.reshape(B_, N_, DKt)], axis=-1)
        return y @ Wo

    def _L3_ffn_ref(x, ln_gamma, ln_beta, mu, scale, w1, b1, w2, b2):
        import jax, jax.numpy as jnp
        import numpy as np
        LN_EPS = 1e-05
        NORM_EPS = 1e-12

        def _layernorm(x, gamma, beta):
            mu = x.mean(axis=-1, keepdims=True)
            var = ((x - mu) ** 2).mean(axis=-1, keepdims=True)
            return (x - mu) * jax.lax.rsqrt(var + LN_EPS) * gamma + beta

        def _l2norm(x, axis):
            n = jnp.sqrt((x ** 2).sum(axis=axis, keepdims=True))
            return x / jnp.maximum(n, NORM_EPS)
        B, N, D = x.shape
        _, E, S = mu.shape
        xn = _layernorm(x, ln_gamma, ln_beta)
        x_unit = _l2norm(xn, axis=-1)
        mu_unit = _l2norm(mu, axis=0)
        logits = jnp.einsum('bnd,des->bnes', x_unit * scale, mu_unit)
        dispatch = jax.nn.softmax(logits, axis=1)
        combine = jax.nn.softmax(logits.reshape(B, N, E * S), axis=-1).reshape(B, N, E, S)
        slot_in = jnp.einsum('bnd,bnes->besd', xn, dispatch)
        h = jax.nn.gelu(jnp.einsum('besd,edh->besh', slot_in, w1) + b1[None, :, None, :], approximate=False)
        slot_out = jnp.einsum('besh,ehd->besd', h, w2) + b2[None, :, None, :]
        out = jnp.einsum('besd,bnes->bnd', slot_out, combine)
        return out
    x = L0_attn_x
    xn = _layernorm(x, axis=-1)
    s = _L0_attn_ref(xn, L0_attn_Wq, L0_attn_bq, L0_attn_Wk, L0_attn_bk, L0_attn_Wv, L0_attn_bv, L0_attn_Wo, L0_attn_bo)
    g = _silu(_L0_ffn_ref(xn, L0_ffn_qweights, L0_ffn_scales, L0_ffn_biases, L0_ffn_lora_a, L0_ffn_lora_b, L0_ffn_ln_gamma, L0_ffn_ln_beta))
    x = x + s * g
    xn = _layernorm(x, axis=-1)
    s = _L1_attn_ref(xn, L1_attn_Wk, L1_attn_Wv, L1_attn_Wr, L1_attn_Wo, L1_attn_time_decay, L1_attn_time_first, L1_attn_time_mix_key, L1_attn_time_mix_value, L1_attn_time_mix_receptance)
    g = _silu(_L1_ffn_ref(xn, L1_ffn_router_w, L1_ffn_expert_bias, L1_ffn_w1, L1_ffn_w3, L1_ffn_w2, L1_ffn_sw1, L1_ffn_sw3, L1_ffn_sw2))
    x = x + s * g
    xn = _layernorm(x, axis=-1)
    s = _L2_attn_ref(xn, L2_attn_wq, L2_attn_wk, L2_attn_wv, L2_attn_wgq, L2_attn_wgk, L2_attn_wgv, L2_attn_r_out_w, L2_attn_gate_local_w, L2_attn_gate_remote_w, L2_attn_w_out)
    g = _silu(_L2_ffn_ref(xn, L2_ffn_theta, L2_ffn_phi, L2_ffn_theta_noise, L2_ffn_phi_noise))
    x = x + s * g
    xn = _layernorm(x, axis=-1)
    s = _L3_attn_ref(xn, L3_attn_Wq, L3_attn_Wk, L3_attn_Wv, L3_attn_Wo, L3_attn_omega, L3_attn_mu_raw, L3_attn_sigma_raw, L3_attn_eta_raw, L3_attn_gamma_raw, L3_attn_tau, L3_attn_nu_raw)
    g = _silu(_L3_ffn_ref(xn, L3_ffn_ln_gamma, L3_ffn_ln_beta, L3_ffn_mu, L3_ffn_scale, L3_ffn_w1, L3_ffn_b1, L3_ffn_w2, L3_ffn_b2))
    x = x + s * g
    return x

_drawn_inputs = setup_inputs


def setup_inputs(seed=0):
    import zlib

    import numpy as np

    out = dict(_drawn_inputs(seed))
    spreads = {'L0_ffn_ln_gamma': (1.0, 0.2),
     'L0_ffn_ln_beta': (0.0, 0.1),
     'L1_ffn_expert_bias': (0.0, 0.8),
     'L3_attn_eta_raw': (1.0, 0.6),
     'L3_attn_gamma_raw': (1.0, 0.6),
     'L3_attn_tau': (1.0, 0.6),
     'L3_attn_nu_raw': (4.0, 0.6),
     'L3_ffn_ln_gamma': (1.0, 0.6),
     'L3_ffn_ln_beta': (0.0, 0.8),
     'L3_ffn_b1': (0.0, 0.8),
     'L3_ffn_b2': (0.0, 2.0)}
    factors = {'L0_attn_bq': 8.0,
     'L0_attn_bk': 200.0,
     'L0_ffn_biases': 8.0,
     'L0_ffn_lora_a': 8.0,
     'L0_ffn_lora_b': 8.0,
     'L1_attn_Wk': 8.0,
     'L1_attn_Wv': 8.0,
     'L1_attn_Wr': 8.0,
     'L1_attn_Wo': 8.0,
     'L1_attn_time_decay': 8.0,
     'L1_attn_time_first': 8.0,
     'L1_attn_time_mix_key': 8.0,
     'L1_attn_time_mix_value': 8.0,
     'L1_attn_time_mix_receptance': 8.0,
     'L1_ffn_router_w': 8.0,
     'L1_ffn_w1': 8.0,
     'L1_ffn_w3': 8.0,
     'L1_ffn_w2': 8.0,
     'L1_ffn_sw1': 8.0,
     'L1_ffn_sw3': 8.0,
     'L1_ffn_sw2': 8.0,
     'L2_attn_wq': 8.0,
     'L2_attn_wk': 8.0,
     'L2_attn_wv': 8.0,
     'L2_attn_wgq': 32.849,
     'L2_attn_wgk': 31.83,
     'L2_attn_wgv': 8.0,
     'L2_attn_r_out_w': 8.0,
     'L2_attn_gate_local_w': 8.0,
     'L2_attn_gate_remote_w': 34.258,
     'L2_attn_w_out': 8.0,
     'L2_ffn_theta': 64.0,
     'L2_ffn_phi': 8.0,
     'L2_ffn_theta_noise': 64.0,
     'L2_ffn_phi_noise': 25.042,
     'L3_attn_Wq': 8.0,
     'L3_attn_Wk': 8.0,
     'L3_attn_Wv': 8.0,
     'L3_attn_Wo': 8.0,
     'L3_attn_omega': 8.0,
     'L3_attn_mu_raw': 8.0,
     'L3_attn_sigma_raw': 8.0,
     'L3_ffn_mu': 8.0,
     'L3_ffn_w1': 8.0,
     'L3_ffn_w2': 8.0}
    for name, (base, spread) in spreads.items():
        noise = np.random.default_rng([zlib.crc32(name.encode()), seed]).standard_normal(out[name].shape)
        drawn = base * np.exp(spread * noise) if base else spread * noise
        out[name] = jnp.asarray(drawn.astype(out[name].dtype))
    for name, factor in factors.items():
        out[name] = (out[name] * factor).astype(out[name].dtype)
    return out
```

```python
from contextlib import ExitStack

import numpy as np

import concourse.bass as bass
import concourse.mybir as mybir
from concourse.alu_op_type import AluOpType as ALU

F32 = mybir.dt.float32
BF16 = mybir.dt.bfloat16
I32 = mybir.dt.int32
ACT = mybir.ActivationFunctionType
AX = mybir.AxisListType

LAYERS = 4
P = 128
D = 128
SEQS, S = 8, 512
B = 2
CHUNKS = SEQS // B
N = B * S
NT = N // P
TPB = S // P
MASKED = -1e30


class Counter:

    def __init__(self, prog, name, step=1):
        self.prog, self.name, self.step, self.count = prog, name, step, 0
        self.sem = prog.nc.alloc_semaphore(name)
        prog.counters.append(self)

    def mark(self):
        return (self, self.prog.era, self.count)

    def next(self):
        self.count += self.step
        return self.mark()


class Program:

    def __init__(self, nc):
        self.nc, self.era, self.counters, self.engines = nc, 0, [], []

    def new_era(self):
        for e in self.engines:
            for c in self.counters:
                e.wait(c.mark())
        self.nc.all_engine_barrier(sem_only=True)
        for c in self.counters:
            if c.count:
                self.engines[0].e.sem_clear(c.sem)
        self.nc.all_engine_barrier(sem_only=True)
        self.era += 1
        for c in self.counters:
            c.count = 0
        for e in self.engines:
            e.waited = {}

    def loop_over(self, name, n, body):
        self.new_era()
        with self.nc.Fori(0, n) as i:
            body(i)
            self.new_era()


class Engine:

    def __init__(self, prog, eng, name, in_order):
        self.prog, self.e, self.in_order = prog, eng, in_order
        self.done = Counter(prog, name)
        self.waited = {}
        prog.engines.append(self)

    def wait(self, *marks):
        for mark in marks:
            if mark is None:
                continue
            counter, era, count = mark
            if era != self.prog.era or count <= self.waited.get(counter, 0):
                continue
            self.e.wait_ge(counter.sem, count)
            self.waited[counter] = count

    def do(self, need, fn, *args, **kw):
        self.wait(*need)
        if self.in_order:
            self.wait(self.done.mark())
        fn(*args, **kw).then_inc(self.done.sem, 1)
        return self.done.next()

    def quiet(self, need, fn, *args, **kw):
        self.wait(*need)
        fn(*args, **kw)


def interleave(*lanes):
    lanes = [iter(x) for x in lanes]
    while lanes:
        for lane in list(lanes):
            try:
                next(lane)
            except StopIteration:
                lanes.remove(lane)


def view(ap, dims, offset=0):
    return bass.AP(tensor=ap.tensor, offset=ap.offset + offset, ap=[list(ap.ap[0])] + dims)


class Kernel:
    def __init__(self, nc, io):
        self.nc, self.io = nc, io
        self.prog = Program(nc)
        p = self.prog
        self.T = Engine(p, nc.tensor, "pe", False)
        self.V = Engine(p, nc.vector, "dve", True)
        self.A = Engine(p, nc.scalar, "act", True)
        self.G = Engine(p, nc.gpsimd, "pool", True)
        self.Y = Engine(p, nc.sync, "sp", False)
        self.engines = [self.T, self.V, self.A, self.G, self.Y]
        self.ps = nc.alloc_psum_tensor("banks", [P, 8, 512], F32)

    def sb(self, name, shape, dt=F32):
        return self.scope.enter_context(self.nc.sbuf_tensor(name, shape, dt))

    def wide_pair(self, i):
        w = self.scratch
        a = w[:, i, 0, 0:1]
        return bass.AP(tensor=a.tensor, offset=a.offset,
                       ap=[list(a.ap[0]), [N, 2], [1, N]])

    def bank(self, k, n=1):
        return self.ps[:, k, :] if n == 1 else self.ps[:, k:k + n, :]

    def meet(self):
        for e in self.engines:
            for c in self.prog.counters:
                e.wait(c.mark())

    def load(self, group, out, src, need=(), eng=None):
        e = eng or self.Y
        e.wait(*need)
        e.e.dma_start(out, src).then_inc(group.sem, 16)
        return group.next()

    def mm(self, need, out, lhsT, rhs, start=True, stop=True, signal=False, **kw):
        f = self.T.do if signal else self.T.quiet
        return f(need, self.nc.tensor.matmul, out, lhsT, rhs, start=start, stop=stop,
                 skip_group_check=True, **kw)

    def tr(self, need, out, in_, signal=False, start=True, ident=None):
        k = in_.shape[0]
        f = self.T.do if signal else self.T.quiet
        i = self.ident if ident is None else ident
        return f(need, self.nc.tensor.matmul, out, in_, i[0:k, 0:k], start=start, stop=True,
                 is_transpose=True, skip_group_check=True)

    def act(self, need, out, in_, func, **kw):
        return self.A.do(need, self.nc.scalar.activation, out, in_, func, **kw)

    def tt(self, need, out, a, b, op, eng=None):
        e = eng or self.V
        return e.do(need, e.e.tensor_tensor, out, a, b, op)

    def ts(self, need, out, a, s1, s2=None, op0=ALU.mult, op1=None, eng=None):
        e = eng or self.V
        if op1 is None:
            return e.do(need, e.e.tensor_scalar, out, a, s1, None, op0)
        return e.do(need, e.e.tensor_scalar, out, a, s1, s2, op0, op1)

    def stt(self, need, out, a, s, b, op0, op1):
        return self.V.do(need, self.nc.vector.scalar_tensor_tensor, out, a, s, b, op0, op1)

    def copy(self, need, out, in_, eng=None):
        e = eng or self.V
        if e is self.A:
            return self.act(need, out, in_, ACT.Identity)
        return e.do(need, e.e.tensor_copy, out, in_)

    def reduce(self, need, out, in_, op, axis=AX.X):
        return self.V.do(need, self.nc.vector.tensor_reduce, out, in_, axis, op)

    def fill(self, out, value, eng=None):
        e = eng or self.G
        return e.do((), e.e.memset, out, value)

    def keep_where(self, ap, op, fill, base, pattern, mult):
        return self.G.do((), self.nc.gpsimd.affine_select, out=ap, in_=ap, compare_op=op,
                         fill=fill, base=base, pattern=pattern, channel_multiplier=mult)

    def constants(self):
        self.ident = self.sb("ident", [P, P])
        self.identb = self.sb("identb", [P, P], BF16)
        self.ones = self.sb("ones", [P, P])
        self.minus_half = self.sb("minus_half", [P, 16])
        self.fill(self.ident[:, :], 0.0)
        self.keep_where(self.ident[:, :], ALU.not_equal, 1.0, 0, [[-1, P]], 1)
        self.fill(self.identb[:, :], 0.0)
        self.keep_where(self.identb[:, :], ALU.not_equal, 1.0, 0, [[-1, P]], 1)
        self.fill(self.ones[:, :], 1.0)
        self.fill(self.minus_half[:, :], -0.5)

    def rsqrt(self, need, out, in_, eps):
        n = in_.shape[1]
        self.ts(need, out, in_, eps, None, ALU.add, eng=self.G)
        return self.tt((), out, out, self.minus_half[:, 0:n], ALU.pow, eng=self.G)

    def norm_scratch(self):
        self.bn = self.sb("bn", [P, NT, 6])
        self.mv = self.sb("mv", [P, NT, 2])
        self.rstd = self.sb("rstd", [P, NT])
        self.normed = self.sb("normed", [P, NT, D])

    def normalize(self, need, src, out, eps=1e-5):
        v = self.nc.vector
        for t in range(NT):
            self.V.do(need, v.bn_stats, self.bn[:, t, :], src[:, t, :])
        for t in range(NT):
            m = self.V.do((), v.bn_aggr, self.mv[:, t, :], self.bn[:, t, :])
        r = self.rsqrt([m], self.rstd[:, :], self.mv[:, :, 1], eps)
        for t in range(NT):
            m = self.ts([r], out[:, t, :], src[:, t, :], self.mv[:, t, 0:1], self.rstd[:, t:t + 1],
                        ALU.subtract, ALU.mult)
        return m

    def window_mask(self, name, w, heads):
        m = self.sb(name, [P, 2 * w], BF16)
        self.fill(m[:, :], 0.0)
        for h in range(heads):
            q = m[h * w:(h + 1) * w, :]
            self.keep_where(q, ALU.is_ge, MASKED, -1, [[1, 2 * w]], -1)
            self.keep_where(q, ALU.is_ge, MASKED, w, [[-1, 2 * w]], 1)
        first = self.sb(name + "_first", [P, 2 * w], BF16)
        self.copy((), first[:, :], m[:, :], self.G)
        self.fill(first[:, 0:w], MASKED)
        return m, first

    def head_select(self, name, q, scale):
        m = self.sb(name, [P, 4, q])
        self.fill(m[:, :, :], scale)
        for g in range(4):
            part = m[32 * g:32 * g + 32, :, :]
            self.keep_where(part, ALU.is_ge, 0.0, 0, [[-8, 4], [0, q]], 1)
            self.keep_where(part, ALU.is_ge, 0.0, 7, [[8, 4], [0, q]], -1)
        return m

    def l0_load(self):
        io = self.io
        self.c_w0 = Counter(self.prog, "load_w0", 16)
        self.w0 = self.sb("w0", [D, 3, D])
        for i, n in enumerate(("WqT", "WkT", "WvT")):
            self.load(self.c_w0, self.w0[:, i, :], io["L0_" + n])
        self.wo0 = self.sb("wo0", [64, 2, D])
        for hp in range(2):
            src = io["L0_WoT"].rearrange("(g hp d) o -> hp g d o", hp=2, d=8)[hp]
            for g in range(8):
                self.load(self.c_w0, self.wo0[8 * g:8 * g + 8, hp, :], src[g], eng=self.A)
        self.b0 = self.sb("b0", [D, 4])
        self.bv0 = self.sb("bv0", [1, D])
        for i, n in enumerate(("bq", "bk", "bo")):
            self.load(self.c_w0, self.b0[:, i:i + 1], io["L0_" + n].rearrange("(a b) -> a b", b=1))
        self.load(self.c_w0, self.bv0[:, :], io["L0_bv"].rearrange("(a b) -> a b", a=1))

    def l0_attention_prepare(self):
        W = 64
        self.sel0 = self.head_select("sel0", W, 8 ** -0.5)
        self.mask0_rest, self.mask0_first = self.window_mask("mask0_rest", W, 2)
        self.mask0 = self.sb("mask0", [P, 2 * W], BF16)
        self.lanes0 = lanes = []
        for b in range(B):
            t = dict(
                xw=self.sb(f"xw0_{b}", [D, 2 * W]), kt=self.sb(f"kt0_{b}", [D, 2 * W]),
                qx=self.sb(f"qx0_{b}", [D, 4, W]), v=self.sb(f"v0_{b}", [P, 16, 9]),
                mx=self.sb(f"mx0_{b}", [P, 8]), p=self.sb(f"p0_{b}", [P, 8, P]),
                pt=self.sb(f"pt0_{b}", [P, 8, P]), r=self.sb(f"r0_{b}", [P, 8]),
                o=self.sb(f"o0_{b}", [P, 16, 8]), ot=self.sb(f"ot0_{b}", [64, P]))
            self.fill(t["v"][:, :, 8:9], 1.0)
            self.fill(t["o"][:, :, :], 0.0)
            lanes.append(t)

    def l0_attention(self):
        W, k, lanes = 64, self, self.lanes0
        sel, mask = self.sel0, self.mask0
        k.copy((), mask[:, :], k.mask0_first[:, :])
        k.meet()

        def lane(b, i, marks):
            t, base = lanes[b], 4 * b
            proj, sc, tail = k.bank(base), k.bank(base + 1, 2), k.bank(base + 3)
            x = k.copy((), t["xw"][:, :], k.nT0[:, b, bass.ds(i * W, 2 * W)], k.G)
            yield
            k.mm([x], proj[:, 0:P], k.w0[:, 1, :], t["xw"][:, :], start=True)
            k.mm((), proj[:, P:P + W], k.w0[:, 0, :], t["xw"][:, W:2 * W])
            k.mm((), proj[:, 256:384], t["xw"][:, :], k.w0[:, 2, :], stop=False)
            m = k.mm((), proj[:, 256:384], k.ones[0:1, :], k.bv0[:, :], start=False, signal=True)
            kt = k.act([m], t["kt"][:, :], proj[:, 0:P], ACT.Identity, bias=k.b0[:, 1:2])
            v = k.copy([m], t["v"][:, :, 0:8], proj[:, 256:384].rearrange("p (h d) -> p h d", d=8), k.A)
            q = k.stt([m, v], t["qx"][:, :, :], proj[:, P:P + W].unsqueeze(1).broadcast_to([P, 4, W]),
                      k.b0[:, 0:1], sel[:, :, :], ALU.add, ALU.mult)
            yield
            for half in range(2):
                k.mm((), sc[:, half, :], k.identb[:, :],
                     mask[:, :].unsqueeze(1).broadcast_to([P, 4, 2 * W]), stop=False)
            done = {}
            for g in (0, 2, 1, 3):
                rows = slice(32 * g, 32 * g + 32)
                for pair in range(2):
                    c = (g % 2 * 2 + pair) * P
                    m = k.mm([kt, q, done.get(g - 1)], sc[:, g // 2, c:c + P],
                             t["qx"][rows, 2 * pair:2 * pair + 2, :], t["kt"][rows, :],
                             start=False, signal=(pair == 1))
                done[g] = m
            marks["mask"] = m
            s3 = sc.rearrange("p a (g t) -> p (a g) t", t=P)
            mx = k.reduce([m], t["mx"][:, :], s3, ALU.max)
            d = k.tt((), t["p"][:, :, :], s3, t["mx"][:, :].unsqueeze(2).broadcast_to([P, 8, P]),
                     ALU.subtract)
            e = k.act([d], t["p"][:, :, :], t["p"][:, :, :], ACT.Exp)
            yield
            for gp in range(8):
                m = k.tr([e], sc[:, gp // 4, (gp % 4) * P:(gp % 4 + 1) * P], t["p"][:, gp, :],
                         signal=(gp % 4 == 3))
                if gp == 3:
                    c0 = k.copy([m], t["pt"][:, 0:4, :], sc[:, 0, :], k.A)
            c1 = k.copy([m], t["pt"][:, 4:8, :], sc[:, 1, :])
            yield
            for gp in range(8):
                m = k.mm([c0, c1, v], tail[:, gp * 18:gp * 18 + 18], t["pt"][:, gp, :],
                         t["v"][:, 2 * gp:2 * gp + 2, :], signal=(gp == 7))
            for hp in range(2):
                rows = slice(64 * hp, 64 * hp + 64)
                pv = tail[rows, 0:144].rearrange("p (g c) -> p g c", c=18)[:, :, 9 * hp:9 * hp + 9]
                k.V.do([m], k.nc.vector.reciprocal, t["r"][rows, :], pv[:, :, 8])
                o = k.tt((), t["o"][rows, 0:8, :], pv[:, :, 0:8],
                         t["r"][rows, :].unsqueeze(2).broadcast_to([64, 8, 8]), ALU.mult)
            yield
            m = k.tr([o], tail[:, 256:384], t["o"][:, :, :].rearrange("p g d -> p (g d)"),
                     signal=True)
            c = k.copy([m], t["ot"][:, :], tail[0:64, 256:384], k.A)
            k.mm([c], tail[:, 384:448], k.wo0[:, 0, :], t["ot"][:, 0:W], stop=False)
            m = k.mm((), tail[:, 384:448], k.wo0[:, 1, :], t["ot"][:, W:2 * W], start=False,
                     signal=True)
            k.act([m], k.sT[:, bass.ds(i * W + b * S, W)], tail[:, 384:448], ACT.Identity,
                  bias=k.b0[:, 2:3])
            yield

        def body(i):
            marks = {}
            interleave(lane(0, i, marks), lane(1, i, marks))
            k.copy([marks["mask"]], mask[:, :], k.mask0_rest[:, :])

        self.prog.loop_over("l0_attention", S // W, body)

    def l0_ffn_load(self):
        io, p = self.io, self.prog
        self.c_q = Counter(p, "load_q", 16)
        self.c_f0 = Counter(p, "load_f0", 16)
        self.q0 = self.sb("q0", [D, 6, D], I32)
        self.sc0 = self.sb("sc0", [D, 6, D])
        self.la0, self.lb0 = self.sb("la0", [32, 6, D]), self.sb("lb0", [32, 6, D])
        self.load(self.c_q, self.q0[:, :, :], io["L0_qT"].rearrange("i d o -> d i o"), eng=self.A)
        self.load(self.c_q, self.sc0[:, :, :], io["L0_scT"].rearrange("i d o -> d i o"), eng=self.A)
        self.load(self.c_q, self.la0[:, :, :], io["L0_la"].rearrange("i r d -> r i d"), eng=self.A)
        self.load(self.c_q, self.lb0[:, :, :], io["L0_lbT"].rearrange("i r o -> r i o"), eng=self.A)
        self.fb_row = self.sb("fb_row", [1, 3, D])
        self.fb_col = self.sb("fb_col", [D, 6])
        self.ln_g0, self.ln_b0 = self.sb("ln_g0", [D, 3]), self.sb("ln_b0", [D, 3])
        self.load(self.c_f0, self.fb_row[:, :, :],
                  io["L0_fb"].rearrange("(j two) o -> two j o", two=2)[0:1], eng=self.A)
        self.load(self.c_f0, self.fb_col[:, :], io["L0_fbT"], eng=self.A)
        self.load(self.c_f0, self.ln_g0[:, :], io["L0_lngT"], eng=self.A)
        self.load(self.c_f0, self.ln_b0[:, :], io["L0_lnbT"], eng=self.A)

    def l0_ffn_weights(self):
        k = self
        self.wf0 = self.sb("wf0", [D, 6, D])
        k.ts([k.c_q.mark()], k.wf0[:, :, :], k.q0[:, :, :], 1 / 7.5, -1.0, ALU.mult, ALU.add)
        k.tt((), k.wf0[:, :, :], k.wf0[:, :, :], k.sc0[:, :, :], ALU.mult)
        for i in range(6):
            m = k.mm([k.c_q.mark()], k.bank(i // 4)[:, (i % 4) * P:(i % 4 + 1) * P], k.la0[:, i, :],
                     k.lb0[:, i, :], signal=(i in (3, 5)))
            if i == 3:
                k.tt([m], k.wf0[:, 0:4, :], k.wf0[:, 0:4, :],
                     k.bank(0).rearrange("p (i o) -> p i o", o=P), ALU.add)
        return k.tt([m], k.wf0[:, 4:6, :], k.wf0[:, 4:6, :],
                    k.bank(1)[:, 0:256].rearrange("p (i o) -> p i o", o=P), ALU.add)

    def l0_ffn(self):
        k = self
        y = self.bank(0, 2)
        last = [k.c_f0.mark()]
        for blk in range(3):
            def h_of(t):
                if blk:
                    return k.hT[:, t * P:(t + 1) * P]
                return k.nT0[:, t // 4, 64 + (t % 4) * P:64 + (t % 4 + 1) * P]
            w1, w2 = k.wf0[:, 2 * blk, :], k.wf0[:, 2 * blk + 1, :]
            for half in range(2):
                k.mm(last, y[:, half, :], k.ones[0:1, :],
                     k.fb_row[:, blk, :].unsqueeze(1).broadcast_to([1, 4, D]), stop=False)
                for t in range(4 * half, 4 * half + 4):
                    m = k.mm((), y[:, half, (t % 4) * P:(t % 4 + 1) * P], h_of(t), w1, start=False,
                             signal=(t % 4 == 3))
            y8 = y.rearrange("p a (t d) -> p (a t) d", d=D)
            m = k.normalize([m], y8, k.normed)
            halves = []
            for t in range(NT):
                mm = k.tr([m], k.bank(2 + t // 4)[:, (t % 4) * P:(t % 4 + 1) * P],
                          k.normed[:, t, :], signal=(t % 4 == 3))
                if t % 4 == 3:
                    halves.append(mm)
            outs = []
            for half in range(2):
                g = k.act([halves[half]], k.aT[:, half * S:(half + 1) * S], k.bank(2 + half),
                          ACT.Gelu, bias=k.ln_b0[:, blk:blk + 1], scale=k.ln_g0[:, blk:blk + 1])
                outs.append(k.mm([g], k.bank(4 + half), w2, k.aT[:, half * S:(half + 1) * S],
                                 signal=True))
            for half in range(2):
                prev = k.hT[:, half * S:(half + 1) * S] if blk else k.nT0[:, half, 64:64 + S]
                m = k.stt([outs[half]], k.hT[:, half * S:(half + 1) * S], k.bank(4 + half),
                          k.fb_col[:, 2 * blk + 1:2 * blk + 2], prev, ALU.add, ALU.add)
            last = [m]
        return m

    def close_T(self, s, h):
        k = self
        k.meet()
        for half in range(2):
            c = slice(half * S, (half + 1) * S)
            a = k.act((), k.aT[:, c], h[:, c], ACT.Tanh, scale=0.5)
            v = k.stt([a], k.aT[:, c], k.aT[:, c], 1.0, h[:, c], ALU.add, ALU.mult)
            v = k.stt((), k.aT[:, c], k.aT[:, c], 0.5, s[:, c], ALU.mult, ALU.mult)
            for t in range(4):
                m = k.tr([v], k.bank(half)[:, t * P:(t + 1) * P],
                         k.aT[:, half * S + t * P:half * S + (t + 1) * P], signal=(t == 3))
            v = k.tt([m], k.xs[:, bass.ds(k.chunk * NT + 4 * half, 4), :],
                     k.x[:, 4 * half:4 * half + 4, :],
                     k.bank(half).rearrange("p (t d) -> p t d", d=D), ALU.add)
        k.meet()

    def close_R(self, s, f):
        k = self
        k.meet()
        t = k.normed
        a = k.act((), t[:, :, :], f, ACT.Tanh, scale=0.5)
        k.stt([a], t[:, :, :], t[:, :, :], 1.0, f, ALU.add, ALU.mult)
        k.stt((), t[:, :, :], t[:, :, :], 0.5, s, ALU.mult, ALU.mult)
        k.tt((), k.xs[:, bass.ds(k.chunk * NT, NT), :], k.x[:, :, :], t[:, :, :], ALU.add)
        k.meet()

    def open_layer(self, out, pad):
        k = self
        m = k.normalize((), k.x, k.n)
        for b in range(B):
            for t in range(TPB):
                mm = k.tr([m], k.bank(b)[:, t * P:(t + 1) * P], k.n[:, b * TPB + t, :],
                          signal=(t == 3))
            k.copy([mm], out[:, b, pad:pad + S], k.bank(b), k.A if b else k.V)
        k.meet()

    def layer0_prepare(self):
        k = self
        k.l0_load()
        k.l0_ffn_load()
        k.nT0 = k.sb("nT0", [D, B, 64 + S])
        k.fill(k.nT0[:, :, 0:64], 0.0)
        k.l0_attention_prepare()
        k.l0_ffn_weights()

    def layer0(self):
        k = self
        k.open_layer(k.nT0, 64)
        k.l0_ffn()
        k.meet()
        k.l0_attention()
        k.close_T(k.sT, k.hT)

    def layer1_prepare(self):
        k, io = self, self.io
        c = Counter(self.prog, "load_l1", 16)
        k.w1 = k.sb("w1", [D, 10, 256])
        k.w3 = k.sb("w3", [D, 10, 256])
        k.w2 = k.sb("w2", [P, 10, 2, D])
        k.load(c, k.w1[:, :, :], io["L1_w1T"].rearrange("e d h -> d e h"))
        k.load(c, k.w3[:, :, :], io["L1_w3T"].rearrange("e d h -> d e h"), eng=k.A)
        k.load(c, k.w2[:, :, :, :], io["L1_w2T"].rearrange("e (m p) d -> p e m d", p=P))
        k.router = k.sb("router", [D, 8])
        k.router_b = k.sb("router_b", [1, 8])
        k.load(c, k.router[:, :], io["L1_routerT"])
        k.load(c, k.router_b[:, :], io["L1_eb"].rearrange("(a b) -> a b", a=1))
        k.rw = k.sb("rw", [D, 3, D])
        k.rwo = k.sb("rwo", [D, D])
        k.rp = k.sb("rp", [D, 5])
        for i, n in enumerate("kvr"):
            k.load(c, k.rw[:, i, :], io[f"L1_W{n}"], eng=k.A)
        k.load(c, k.rwo[:, :], io["L1_Wo"])
        for i, n in enumerate(("td", "tf", "tmk", "tmv", "tmr")):
            k.load(c, k.rp[:, i:i + 1], io["L1_" + n].rearrange("(a b) -> a b", b=1), eng=k.A)
        k.meet()
        k.td = k.sb("td", [D, 1])
        k.act((), k.td[:, :], k.rp[:, 0:1], ACT.Exp)
        k.ts([k.A.done.mark()], k.td[:, :], k.td[:, :], -1.0)
        k.rw_now, k.rw_before = k.sb("rw_now", [D, 3, D]), k.sb("rw_before", [D, 3, D])
        k.rest = k.sb("rest", [D, 3])
        k.ts((), k.rest[:, :], k.rp[:, 2:5], -1.0, 1.0, ALU.mult, ALU.add)
        for i in range(3):
            k.ts((), k.rw_now[:, i, :], k.rw[:, i, :], k.rp[:, 2 + i:3 + i])
            k.ts((), k.rw_before[:, i, :], k.rw[:, i, :], k.rest[:, i:i + 1])
        k.nT1 = k.sb("nT1", [D, B, 1 + S])
        k.fill(k.nT1[:, :, 0:1], 0.0)
        k.rank = k.sb("rank", [P, NT, 8])
        k.G.do((), k.nc.gpsimd.iota, k.rank[:, :, :], pattern=[[0, NT], [-1, 8]], base=8,
               channel_multiplier=0, allow_small_or_imprecise_dtypes=True)
        k.cw = k.sb("cw", [P, NT, 8])
        k.route_scratch = [k.sb(f"route{i}", [P, NT, 8]) for i in range(4)]
        k.route_top = k.sb("route_top", [P, NT, 4])

    def time_mixing(self):
        k = self
        w = [x[:, :, :] for x in k.wide]
        kT, vT, rT, mx, num, den, mo, e1, e2, f1, f2 = w[:11]
        cols, prev = slice(1, 1 + S), slice(0, S)
        for b in range(B):
            marks = []
            for i in range(3):
                k.mm((), k.bank(2 * i + b), k.rw_now[:, i, :], k.nT1[:, b, cols], stop=False)
                marks.append(k.mm((), k.bank(2 * i + b), k.rw_before[:, i, :], k.nT1[:, b, prev],
                                  start=False, signal=True))
            k.act([marks[0]], kT[:, b, cols], k.bank(b), ACT.Identity)
            k.act([marks[1]], vT[:, b, cols], k.bank(2 + b), ACT.Identity)
            a = k.act([marks[2]], rT[:, b, cols], k.bank(4 + b), ACT.Tanh, scale=0.5)
        K, Vv, R = kT[:, :, cols], vT[:, :, cols], rT[:, :, cols]
        k.V.do((), k.nc.vector.memset, mx[:, :, 0:1], -1e38)
        k.V.do((), k.nc.vector.memset, num[:, :, 0:1], 0.0)
        k.V.do((), k.nc.vector.memset, den[:, :, 0:1], 0.0)
        scan = k.nc.vector.tensor_tensor_scan
        for b in range(B):
            v = k.V.do([a], scan, mx[:, b, cols], k.td[:, 0:1].broadcast_to([D, S]), kT[:, b, cols],
                       -1e38, ALU.add, ALU.max)
        mp, mn = mx[:, :, prev], mx[:, :, cols]
        F1, F2, E1, E2, MO = (x[:, :, cols] for x in (f1, f2, e1, e2, mo))
        g = k.tt([v], F2, K, mn, ALU.subtract, k.G)
        v = k.stt((), F1, mp, k.td[:, 0:1], mn, ALU.add, ALU.subtract)
        x2 = k.act([g], F2, F2, ACT.Exp)
        x1 = k.act([v], F1, F1, ACT.Exp)
        v = k.stt((), MO, K, k.rp[:, 1:2], mp, ALU.add, ALU.max)
        g = k.tt([v, x2], E1, F2, Vv, ALU.mult, k.G)
        v = k.stt((), E2, K, k.rp[:, 1:2], MO, ALU.add, ALU.subtract)
        y2 = k.act([v], E2, E2, ACT.Exp)
        for b in range(B):
            k.V.do([g, x1], scan, num[:, b, cols], f1[:, b, cols], e1[:, b, cols], 0.0,
                   ALU.mult, ALU.add)
            v = k.V.do([x2], scan, den[:, b, cols], f1[:, b, cols], f2[:, b, cols], 0.0,
                       ALU.mult, ALU.add)
        g = k.tt([v], MO, mp, MO, ALU.subtract, k.G)
        y1 = k.act([g], E1, MO, ACT.Exp)
        g = k.tt([y2, v], F2, E2, Vv, ALU.mult, k.G)
        k.tt([y1, g], F1, E1, num[:, :, prev], ALU.mult)
        k.tt((), F1, F1, F2, ALU.add)
        k.tt((), MO, E1, den[:, :, prev], ALU.mult)
        k.tt((), MO, MO, E2, ALU.add)
        k.V.do((), k.nc.vector.reciprocal, MO, MO)
        k.tt((), F1, F1, MO, ALU.mult)
        k.stt((), F1, R, 1.0, F1, ALU.add, ALU.mult)
        v = k.ts((), F1, F1, 0.5)
        for t in range(NT):
            m = k.mm([v], k.bank(6 + t // 4)[:, (t % 4) * P:(t % 4 + 1) * P],
                     f1[:, t // 4, 1 + (t % 4) * P:1 + (t % 4 + 1) * P], k.rwo[:, :],
                     signal=(t == NT - 1))
        k.copy([m], k.sR.rearrange("p (a t) d -> p a (t d)", a=2), k.bank(6, 2), k.A)

    def route(self):
        k = self
        z = k.bank(0)[:, 0:NT * 8]
        k.mm((), z, k.ones[0:1, :], k.router_b[:, :].unsqueeze(1).broadcast_to([1, NT, 8]), stop=False)
        for t in range(NT):
            m = k.mm((), z[:, 8 * t:8 * t + 8], k.nT1[:, t // 4, 1 + (t % 4) * P:1 + (t % 4 + 1) * P],
                     k.router[:, :], start=False, signal=(t == NT - 1))
        top = k.route_top
        l, c, one, two = (x[:, :, :] for x in k.route_scratch)
        full = [P, NT, 8]

        def col(i):
            return top[:, :, i:i + 1].broadcast_to(full)

        def first_largest(out, j):
            k.reduce((), top[:, :, j], l, ALU.max)
            k.tt((), c, l, col(j), ALU.is_ge)
            k.tt((), c, c, k.rank[:, :, :], ALU.mult)
            k.reduce((), top[:, :, 2], c, ALU.max)
            k.tt((), out, c, col(2), ALU.is_equal)

        k.copy([m], l, z.rearrange("p (t e) -> p t e", e=8))
        first_largest(one, 0)
        k.stt((), l, one, -3e38, l, ALU.mult, ALU.add)
        first_largest(two, 1)
        v = k.tt((), top[:, :, 2], top[:, :, 1], top[:, :, 0], ALU.subtract)
        a = k.act([v], top[:, :, 2], top[:, :, 2], ACT.Exp)
        k.ts([a], top[:, :, 3], top[:, :, 2], 1.0, None, ALU.add)
        k.V.do((), k.nc.vector.reciprocal, top[:, :, 3], top[:, :, 3])
        k.tt((), one, one, col(3), ALU.mult)
        k.tt((), top[:, :, 3], top[:, :, 3], top[:, :, 2], ALU.mult)
        k.tt((), two, two, col(3), ALU.mult)
        v = k.tt((), k.cw[:, :, :], one, two, ALU.add)
        return k.ts((), k.cw[:, :, :], k.cw[:, :, :], 0.5)

    def experts(self):
        k = self
        t = [k.wide[i] for i in range(2)]
        g = [k.wide_pair(2), k.wide_pair(4)]
        free = {}
        acc_done, y_done, unit, pending = None, {}, 0, None

        def outputs(e):
            nonlocal acc_done
            marks = []
            for i in range(NT):
                for m in range(2):
                    mk = k.mm([acc_done, g_done[e]], k.bank(6 + i // 4)[:, (i % 4) * P:(i % 4 + 1) * P],
                              g[e % 2][:, m, i * P:(i + 1) * P], k.w2[:, e, m, :], start=(m == 0),
                              stop=(m == 1), signal=(m == 1 and i % 4 == 3))
                if i % 4 == 3:
                    marks.append(mk)
            y_done[e] = marks[1]
            y = k.bank(6, 2).rearrange("p a (t d) -> p (a t) d", d=D)
            if e >= 8:
                acc_done = k.stt([marks[1]], k.moe[:, :, :], y, 0.5, k.moe[:, :, :], ALU.mult, ALU.add)
                return
            for i in range(NT):
                need = [marks[i // 4]]
                if e == 0:
                    acc_done = k.ts(need, k.moe[:, i, :], y[:, i, :], k.cw[:, i, e:e + 1])
                else:
                    acc_done = k.stt(need, k.moe[:, i, :], y[:, i, :], k.cw[:, i, e:e + 1],
                                     k.moe[:, i, :], ALU.mult, ALU.add)

        g_done = {}
        for e in range(10):
            for b in range(B):
                x = k.nT1[:, b, 1:1 + S]
                for m in range(2):
                    p = unit % 3
                    h1, h3, ts_ = k.bank(2 * p), k.bank(2 * p + 1), t[unit % 2][:, 0, 0:S]
                    k.mm([free.get(p)], h1, k.w1[:, e, m * P:(m + 1) * P], x)
                    mk = k.mm((), h3, k.w3[:, e, m * P:(m + 1) * P], x, signal=True)
                    a = k.act([mk, free.get(("t", unit % 2))], ts_, h1, ACT.Tanh, scale=0.5)
                    v = k.stt([a], ts_, ts_, 1.0, h1, ALU.add, ALU.mult)
                    v = k.tt([y_done.get(e - 2)], g[e % 2][:, m, b * S:(b + 1) * S], ts_, h3,
                             ALU.mult)
                    free[p] = free["t", unit % 2] = v
                    unit += 1
            g_done[e] = v
            if e:
                outputs(e - 1)
        outputs(9)

    def layer1(self):
        k = self
        k.open_layer(k.nT1, 1)
        k.time_mixing()
        k.meet()
        k.route()
        k.meet()
        k.experts()
        k.close_R(k.sR[:, :, :], k.moe[:, :, :])

    def sincos(self, ang, sin, cos, turns):
        k = self
        two_pi = 2 * np.pi
        c1 = 6.28125
        c2 = float(np.round((two_pi - c1) * 2.0 ** 20) / 2.0 ** 20)
        c3 = two_pi - c1 - c2
        nearest = 1.5 * 2.0 ** 23
        k.ts((), turns, ang, 1 / two_pi, nearest, ALU.mult, ALU.add)
        k.ts((), turns, turns, nearest, None, ALU.subtract)
        k.stt((), ang, turns, -c1, ang, ALU.mult, ALU.add)
        k.stt((), ang, turns, -c2, ang, ALU.mult, ALU.add)
        k.stt((), ang, turns, -c3, ang, ALU.mult, ALU.add)
        pi = float(np.nextafter(np.float32(np.pi), np.float32(0)))
        v = k.ts((), ang, ang, pi, -pi, ALU.min, ALU.max)
        k.act([v], sin, ang, ACT.Sin)
        a = k.act((), cos, ang, ACT.Sin, scale=0.5)
        k.tt([a], cos, cos, cos, ALU.mult)
        return k.ts((), cos, cos, -2.0, 1.0, ALU.mult, ALU.add)

    def layer2_prepare(self):
        k, io = self, self.io
        c = Counter(self.prog, "load_l2", 16)
        W = 32
        k.wqkv2 = k.sb("wqkv2", [D, 3, D])
        for i, n in enumerate("qkv"):
            k.load(c, k.wqkv2[:, i, :], io["L2_w" + n])
        k.wg2 = k.sb("wg2", [D, 3, 64])
        for i, n in enumerate("qkv"):
            k.load(c, k.wg2[:, i, :], io["L2_wg" + n], eng=k.A)
        k.rout2 = k.sb("rout2", [64, D])
        k.load(c, k.rout2[:, :], io["L2_rout"])
        k.wout2 = k.sb("wout2", [D, D])
        k.load(c, k.wout2[:, :], io["L2_wout"])
        k.wout2_hp = k.sb("wout2_hp", [32, 4, D])
        src = io["L2_wout"].rearrange("(g hp d) o -> g hp d o", hp=4, d=8)
        for g in range(4):
            k.load(c, k.wout2_hp[8 * g:8 * g + 8, :, :], src[g].rearrange("hp d o -> d hp o"), eng=k.A)
        k.gate_w = k.sb("gate_w", [D, 2])
        k.load(c, k.gate_w[:, 0:1], io["L2_gl"].rearrange("(a b) -> a b", b=1))
        k.load(c, k.gate_w[:, 1:2], io["L2_gr"].rearrange("(a b) -> a b", b=1))
        k.trig = k.sb("trig", [D, 2, D])
        noise = k.scratch[:, 0, 0, 0:256].rearrange("p (i o) -> p i o", i=2)
        k.load(c, k.trig[:, 0, :], io["L2_theta"])
        k.load(c, k.trig[:, 1, :], io["L2_phi"])
        k.load(c, noise[:, 0, :], io["L2_thetan"])
        k.load(c, noise[:, 1, :], io["L2_phin"])
        k.meet()
        k.tt((), k.trig[:, :, :], k.trig[:, :, :], noise, ALU.add)
        s, co, tu, an = (k.scratch[:, i, 0, 0:256] for i in range(1, 5))
        k.copy((), an, k.trig.rearrange("p i o -> p (i o)"))
        k.sincos(an, s, co, tu)
        k.copy((), k.trig[:, 0, :], co[:, 0:D])
        k.copy((), k.trig[:, 1, :], s[:, D:2 * D])
        k.ts((), k.wout2[:, :], k.wout2[:, :], 0.5)
        k.ts((), k.wout2_hp[:, :, :], k.wout2_hp[:, :, :], 0.5)
        k.sel2 = k.head_select("sel2", W, 8 ** -0.5)
        rest, first = k.window_mask("mask2w", W, 4)
        k.mask2, k.mask2_rest, k.mask2_first = (k.sb("mask2" + n, [P, 4, 2 * W], BF16)
                                                for n in ("", "_all", "_one"))
        k.copy((), k.mask2_rest[:, :, :], rest[:, :].unsqueeze(1).broadcast_to([P, 4, 2 * W]), k.G)
        k.copy((), k.mask2_first[:, :, :], k.mask2_rest[:, :, :], k.G)
        k.copy((), k.mask2_first[:, 0, :], first[:, :], k.G)
        k.glw = k.sb("glw", [D, 4])
        k.fill(k.glw[:, :], 1.0)
        k.keep_where(k.glw[:, :], ALU.is_ge, 0.0, 0, [[-32, 4]], 1)
        k.keep_where(k.glw[:, :], ALU.is_ge, 0.0, 31, [[32, 4]], -1)
        k.ts((), k.glw[:, :], k.glw[:, :], k.gate_w[:, 0:1], eng=k.G)
        k.grw = k.sb("grw", [D, 16, 8])
        k.fill(k.grw[:, :, :], 1.0)
        k.keep_where(k.grw[:, :, :], ALU.is_ge, 0.0, 0, [[-8, 16], [0, 8]], 1)
        k.keep_where(k.grw[:, :, :], ALU.is_ge, 0.0, 7, [[8, 16], [0, 8]], -1)
        k.ts((), k.grw[:, :, :], k.grw[:, :, :], k.gate_w[:, 1:2], eng=k.G)
        k.selg = k.sb("selg", [64, 8, 64])
        k.fill(k.selg[:, :, :], 1.0)
        k.keep_where(k.selg[:, :, :], ALU.is_ge, 0.0, 0, [[-8, 8], [0, 64]], 1)
        k.keep_where(k.selg[:, :, :], ALU.is_ge, 0.0, 7, [[8, 8], [0, 64]], -1)
        k.maskg = k.sb("maskg", [P, TPB, 64], BF16)
        k.fill(k.maskg[:, :, :], 0.0)
        k.keep_where(k.maskg[:, :, :], ALU.is_ge, MASKED, 0, [[P, TPB], [-8, 64]], 1)
        k.half2 = k.sb("half2", [P, 2, 9])
        k.fill(k.half2[:, :, :], 1.0)
        k.keep_where(k.half2[:, :, :], ALU.is_ge, 0.0, 0, [[-64, 2], [0, 9]], 1)
        k.keep_where(k.half2[:, :, :], ALU.is_ge, 0.0, 63, [[64, 2], [0, 9]], -1)
        k.quad2 = k.sb("quad2", [P, 4, 9])
        k.fill(k.quad2[:, :, :], 1.0)
        k.keep_where(k.quad2[:, :, :], ALU.is_ge, 0.0, 0, [[-32, 4], [0, 9]], 1)
        k.keep_where(k.quad2[:, :, :], ALU.is_ge, 0.0, 31, [[32, 4], [0, 9]], -1)
        k.nT2 = k.sb("nT2", [D, B, W + S])
        k.fill(k.nT2[:, :, 0:W], 0.0)
        k.pool2 = k.sb("pool2", [D, B, 2, 64])
        k.gk2 = k.sb("gk2", [64, B, 8, 64])
        k.gv2 = k.sb("gv2", [P, B, 4, 2, 9])
        for b in range(B):
            k.copy((), k.gv2[:, b, :, :, 8:9], k.half2[:, :, 8:9].unsqueeze(1)
                   .broadcast_to([P, 4, 2, 1]), k.G)
        k.lanes2g = [dict(mx=k.sb(f"mx2g_{b}", [P, 8]), p=k.sb(f"p2g_{b}", [P, 8, 64]),
                          pt=k.sb(f"pt2g_{b}", [P, 4, P]), o=k.sb(f"o2g_{b}", [P, 8, 8]))
                     for b in range(2)]
        k.lanes2 = []
        for b in range(B):
            t = dict(xw=k.sb(f"xw2_{b}", [D, 160]), xv=k.sb(f"xv2_{b}", [D, 2, 2, 64]), kt=k.sb(f"kt2_{b}", [D, 160]),
                     qx=k.sb(f"qx2_{b}", [D, 4, 4, W]), v=k.sb(f"v2_{b}", [P, 2, 16, 9]),
                     mx=k.sb(f"mx2_{b}", [P, 16]), p=k.sb(f"p2_{b}", [P, 8, P]), pt=k.sb(f"pt2_{b}", [P, 8, P]),
                     gate=k.sb(f"gate2_{b}", [P, 16]), ox=k.sb(f"ox2_{b}", [P, 16, 36]),
                     os=k.sb(f"os2_{b}", [P, 16, 9]), o=k.sb(f"o2_{b}", [P, 4, 4, 8]),
                     ot=k.sb(f"ot2_{b}", [32, 4, P]))
            k.fill(t["v"][:, :, :, 8:9], 1.0)
            k.lanes2.append(t)

    def latent_attention(self):
        k = self
        qT, gr, gq, rem = (k.wide[i] for i in range(4))
        for b in range(B):
            x = k.nT2[:, b, 32:32 + S]
            m = k.mm((), k.bank(b), k.wqkv2[:, 0, :], x, signal=True)
            a = k.copy([m], qT[:, b, 0:S], k.bank(b), k.A)
            m = k.mm([a], k.bank(b), k.grw.rearrange("p h d -> p (h d)"), qT[:, b, 0:S], signal=True)
            k.act([m], gr[:, b, 0:S], k.bank(b), ACT.Tanh, scale=0.5)
            m = k.mm((), k.bank(2 + b)[0:64, :], k.wg2[:, 0, :], x, signal=True)
            k.act([m], gq[0:64, b, 0:S], k.bank(2 + b)[0:64, :], ACT.Identity, scale=8 ** -0.5)
            k.reduce((), k.pool2[:, b, 0, :], x.rearrange("p (n c) -> p n c", c=8), ALU.add)
        v = k.ts((), k.pool2[:, :, 0, :], k.pool2[:, :, 0, :], 1 / 8)
        v = k.copy((), k.pool2[:, :, 1, :], k.pool2[:, :, 0, :])
        for b in range(B):
            m = k.mm([v], k.bank(4)[0:64, b * 64:b * 64 + 64], k.wg2[:, 1, :], k.pool2[:, b, 0, :])
            m = k.mm((), k.bank(4)[:, 256 + b * 64:320 + b * 64],
                     k.pool2[:, b, :, :].rearrange("p i n -> p (i n)"), k.wg2[:, 2, :],
                     signal=True)
        for b in range(B):
            k.tt([m], k.gk2[:, b, :, :], k.bank(4)[0:64, b * 64:b * 64 + 64].unsqueeze(1)
                 .broadcast_to([64, 8, 64]), k.selg[:, :, :], ALU.mult)
            gv = k.tt((), k.gv2[:, b, :, :, 0:8], k.bank(4)[:, 256 + b * 64:320 + b * 64]
                      .rearrange("p (a h d) -> p a h d", a=4, h=2),
                      k.half2[:, :, 0:8].unsqueeze(1).broadcast_to([P, 4, 2, 8]), ALU.mult)
        k.meet()

        def lane(b, tiles):
            t = k.lanes2g[b]
            sc, pt, small = (k.bank(4 * b + i) for i in range(3))
            for tile in tiles:
                cols = slice((tile % 4) * P, (tile % 4 + 1) * P)
                bb = tile // 4
                k.mm([k.V.done.mark()], sc, k.identb[:, :], k.maskg[:, tile % 4, :].unsqueeze(1)
                     .broadcast_to([P, 8, 64]), stop=False)
                m = k.mm((), sc, gq[0:64, bb, cols], k.gk2[:, bb, :, :].rearrange("p h n -> p (h n)"),
                         start=False, signal=True)
                s3 = sc.rearrange("p (h n) -> p h n", n=64)
                k.reduce([m], t["mx"][:, :], s3, ALU.max)
                v = k.tt((), t["p"][:, :, :], s3, t["mx"][:, :].unsqueeze(2).broadcast_to([P, 8, 64]),
                         ALU.subtract)
                a = k.act([v], t["p"][:, :, :], t["p"][:, :, :], ACT.Exp)
                yield
                for pair in range(4):
                    m = k.tr([a], pt[:, pair * P:(pair + 1) * P],
                             t["p"][:, 2 * pair:2 * pair + 2, :].rearrange("p h n -> p (h n)"),
                             signal=(pair == 3))
                a = k.copy([m], t["pt"].rearrange("p a n -> p (a n)"), pt, k.A)
                yield
                for pair in range(4):
                    m = k.mm([a], small[:, pair * 18:pair * 18 + 18], t["pt"][:, pair, :],
                             k.gv2[:, bb, pair, :, :].rearrange("p h c -> p (h c)"),
                             signal=(pair == 3))
                o = small[:, 0:72].rearrange("p (h c) -> p h c", c=9)
                k.V.do([m], k.nc.vector.reciprocal, t["mx"][:, :], o[:, :, 8])
                v = k.tt((), t["o"][:, :, :], o[:, :, 0:8],
                         t["mx"][:, :].unsqueeze(2).broadcast_to([P, 8, 8]), ALU.mult)
                yield
                m = k.tr([v], small[0:64, 128:256], t["o"][:, :, :].rearrange("p h d -> p (h d)"),
                         signal=True)
                k.copy([m], rem[0:64, bb, cols], small[0:64, 128:256])
                yield

        interleave(lane(0, range(4)), lane(1, range(4, 8)))
        k.meet()
        for b in range(B):
            m = k.mm((), k.bank(b), k.rout2[:, :], rem[0:64, b, 0:S], signal=True)
            v = k.stt([m], gr[:, b, 0:S], gr[:, b, 0:S], 1.0, k.bank(b), ALU.add, ALU.mult)
            m = k.mm([v], k.bank(2 + b), k.wout2[:, :], gr[:, b, 0:S], signal=True)
            k.copy([m], k.sT[:, b * S:(b + 1) * S], k.bank(2 + b), k.A)

    def local_attention(self):
        k, W, mask = self, 32, self.mask2
        k.copy((), mask[:, :, :], k.mask2_first[:, :, :])

        def lane(b, i, marks):
            t, base = k.lanes2[b], 4 * b
            proj, sc, tail = k.bank(base), k.bank(base + 1, 2), k.bank(base + 3)
            x = k.copy((), t["xw"][:, :], k.nT2[:, b, bass.ds(i * P, 160)], k.G)
            xv = k.copy((), t["xv"][:, :, :, :], view(t["xw"][:, 0:1], [[64, 2], [W, 2], [1, 64]]), k.G)
            yield
            k.mm([x], proj[:, 0:160], k.wqkv2[:, 1, :], t["xw"][:, :])
            m = k.mm((), proj[:, 160:288], k.wqkv2[:, 0, :], t["xw"][:, W:160], signal=True)
            for jp in range(2):
                mv = k.mm([xv], tail[:, jp * P:(jp + 1) * P],
                          t["xv"][:, jp, :, :].rearrange("p a t -> p (a t)"),
                          k.wqkv2[:, 2, :], signal=(jp == 1))
            kt = k.copy([m], t["kt"][:, :], proj[:, 0:160], k.A)
            v = k.copy([mv], t["v"][:, :, :, 0:8],
                       tail[:, 0:256].rearrange("p (j h d) -> p j h d", j=2, d=8), k.A)
            q = k.tt([m, kt], t["qx"][:, :, :, :],
                     proj[:, 160:288].rearrange("p (j q) -> p j q", j=4).unsqueeze(2)
                     .broadcast_to([P, 4, 4, W]),
                     k.sel2[:, :, :].unsqueeze(1).broadcast_to([P, 4, 4, W]), ALU.mult)
            yield
            for j in range(4):
                off = 288 + (j % 2) * 8 + j // 2
                m = k.mm([q], proj[:, off:off + 7:2], t["qx"][:, j, :, :].rearrange("p h q -> p (h q)"),
                         k.glw[:, :], signal=(j == 3))
            ga = k.act([m], t["gate"][:, :], proj[:, 288:304], ACT.Tanh, scale=0.5 * 8 ** 0.5)
            for half in range(2):
                k.mm((), sc[:, half, :], k.identb[:, :], mask.rearrange("p j t -> p (j t)")
                     .unsqueeze(1).broadcast_to([P, 2, 8 * W]), stop=False)
            done = {}
            for g in (0, 2, 1, 3):
                rows = slice(32 * g, 32 * g + 32)
                for j in range(4):
                    cc = (g % 2 * 4 + j) * 2 * W
                    m = k.mm([kt, q, done.get(g - 1)], sc[:, g // 2, cc:cc + 2 * W],
                             t["qx"][rows, j, :, :].rearrange("p h q -> p (h q)"),
                             t["kt"][rows, j * W:(j + 2) * W], start=False, signal=(j == 3))
                done[g] = m
            marks["mask"] = m
            s3 = sc.rearrange("p a (g t) -> p (a g) t", t=2 * W)
            k.reduce([m], t["mx"][:, :], s3, ALU.max)
            p3 = t["p"].rearrange("p a (g t) -> p (a g) t", t=2 * W)
            d = k.tt((), p3, s3, t["mx"][:, :].unsqueeze(2).broadcast_to([P, 16, 2 * W]), ALU.subtract)
            e = k.act([d], t["p"][:, :, :], t["p"][:, :, :], ACT.Exp)
            yield
            for gj in range(8):
                m = k.tr([e], sc[:, gj // 4, (gj % 4) * P:(gj % 4 + 1) * P], t["p"][:, gj, :],
                         signal=(gj % 4 == 3))
                if gj == 3:
                    c0 = k.copy([m], t["pt"][:, 0:4, :], sc[:, 0, :], k.A)
            c1 = k.copy([m], t["pt"][:, 4:8, :], sc[:, 1, :])
            yield
            for par, bank in ((0, proj), (1, tail)):
                rows = slice(64 * par, 64 * par + 64)
                for gj in range(8):
                    g, jp = gj // 2, gj % 2
                    m = k.mm([c0, c1, v, ga], bank[:, gj * 36:gj * 36 + 36], t["pt"][rows, gj, :],
                             t["v"][rows, jp, 4 * g:4 * g + 4, :].rearrange("p h c -> p (h c)"),
                             signal=(gj == 7))
                k.tt([m], t["ox"][:, 8 * par:8 * par + 8, :], bank[:, 0:288]
                     .rearrange("p (g c) -> p g c", c=36),
                     k.quad2.rearrange("p h c -> p (h c)").unsqueeze(1).broadcast_to([P, 8, 36]),
                     ALU.mult)
            k.reduce((), t["os"][:, :, :], t["ox"].rearrange("p g (h c) -> p g c h", c=9), ALU.add)
            k.V.do((), k.nc.vector.reciprocal, t["mx"][:, :], t["os"][:, :, 8])
            k.stt([ga], t["mx"][:, :], t["gate"][:, :], 1.0, t["mx"][:, :], ALU.add, ALU.mult)
            for par in range(2):
                gs = slice(8 * par, 8 * par + 8)
                o = k.tt((), t["o"].rearrange("p (jp par) g d -> p par g jp d", par=2)[:, par],
                         t["os"][:, gs, 0:8].rearrange("p (g jp) d -> p g jp d", jp=2),
                         t["mx"][:, gs].rearrange("p (g jp) -> p g jp", jp=2).unsqueeze(3)
                         .broadcast_to([P, 4, 2, 8]), ALU.mult)
            yield
            for j in range(4):
                m = k.tr([o], tail[0:32, j * P:(j + 1) * P],
                         t["o"][:, j, :, :].rearrange("p g d -> p (g d)"), signal=(j == 3))
            a = k.copy([m], t["ot"].rearrange("p j q -> p (j q)"), tail[0:32, :], k.A)
            for hp in range(4):
                m = k.mm([a], proj[:, 0:P], k.wout2_hp[:, hp, :], t["ot"][:, :, hp * W:(hp + 1) * W],
                         start=(hp == 0), stop=(hp == 3), signal=(hp == 3))
            dst = k.sT[:, bass.ds(i * P + b * S, P)]
            k.tt([m], dst, dst, proj[:, 0:P], ALU.add)
            yield

        def body(i):
            marks = {}
            interleave(lane(0, i, marks), lane(1, i, marks))
            k.copy([marks["mask"]], mask[:, :, :], k.mask2_rest[:, :, :])

        k.prog.loop_over("l2_local", TPB, body)

    def magnitude(self):
        k = self
        for t in range(NT):
            m = k.mm((), k.bank(t // 2)[:, (t % 2) * 256:(t % 2 + 1) * 256],
                     k.nT2[:, t // 4, 32 + (t % 4) * P:32 + (t % 4 + 1) * P],
                     k.trig.rearrange("p i o -> p (i o)"), signal=(t == NT - 1))
        sq = k.wide_pair(0)
        flat = sq.rearrange("p a n -> p (a n)")
        k.act([m], flat, k.bank(0, 4).rearrange("p a n -> p (a n)"), ACT.Square)
        s4 = flat.rearrange("p (t i d) -> p t i d", t=NT, i=2)
        v = k.tt([k.A.done.mark()], k.moe[:, :, :], s4[:, :, 0, :], s4[:, :, 1, :], ALU.add)
        k.act([v], k.moe[:, :, :], k.moe[:, :, :], ACT.Sqrt)

    def layer2(self):
        k = self
        k.open_layer(k.nT2, 32)
        k.latent_attention()
        k.local_attention()
        k.magnitude()
        k.meet()
        for t in range(NT):
            m = k.tr((), k.bank(t // 4)[:, (t % 4) * P:(t % 4 + 1) * P], k.sT[:, t * P:(t + 1) * P],
                     signal=(t == NT - 1))
        k.close_R(k.bank(0, 2).rearrange("p a (t d) -> p (a t) d", d=D), k.moe[:, :, :])

    HEADS, DH = 16, 64

    def layer3_prepare(self):
        k, io, nc = self, self.io, self.nc
        H = k.HEADS
        c = Counter(self.prog, "load_l3", 16)

        k.gam, k.bet = k.sb("gam", [P, D]), k.sb("bet", [P, D])
        k.load(c, k.gam[:, :], io["L3_g"].partition_broadcast(P))
        k.load(c, k.bet[:, :], io["L3_b"].partition_broadcast(P))
        k.mscale = k.sb("mscale", [P, 1])
        k.load(c, k.mscale[:, :], io["L3_scale"].partition_broadcast(P))
        k.mu3 = k.sb("mu3", [D, 256])
        k.load(c, k.mu3[:, :], io["L3_mu"].rearrange("d e s -> d (e s)"))
        k.w1s, k.w2s = k.sb("w1s", [D, H, 32]), k.sb("w2s", [32, H, D])
        k.load(c, k.w1s[:, :, :], io["L3_w1"].rearrange("e d h -> d e h"), eng=k.A)
        k.load(c, k.w2s[:, :, :], io["L3_w2"].rearrange("e h d -> h e d"), eng=k.A)
        k.b1s, k.b2s = k.sb("b1s", [32, H]), k.sb("b2s", [D, H])
        k.load(c, k.b1s[:, :], io["L3_b1T"])
        k.load(c, k.b2s[:, :], io["L3_b2T"])
        par = k.sb("par", [H, 6])
        k.load(c, par[:, :], io["L3_par"])
        om = k.scratch[:, 0, 0, 0:512]
        k.load(c, om, io["L3_omega"].rearrange("h d -> (h d)").partition_broadcast(P))
        k.meet()
        sq, nrm = k.scratch[:, 1, 0, 0:256], k.scratch[:, 2, 0, 0:256]
        v = k.tt((), sq, k.mu3[:, :], k.mu3[:, :], ALU.mult)
        m = k.mm([v], k.bank(0)[:, 0:256], k.ones[:, :], sq, signal=True)
        v = k.ts([m], nrm, k.bank(0)[:, 0:256], 1e-24, None, ALU.max)
        a = k.act([v], nrm, nrm, ACT.Sqrt)
        k.V.do([a], nc.vector.reciprocal, nrm, nrm)
        k.tt((), k.mu3[:, :], k.mu3[:, :], nrm, ALU.mult)

        k.cosT = k.sb("cosT", [P, TPB, H, 32])
        k.sinT = k.sb("sinT", [P, TPB, H, 3, 32])
        tok = k.sb("tok", [P, TPB])
        g = k.G.do((), nc.gpsimd.iota, tok[:, :], pattern=[[P, TPB]], base=0, channel_multiplier=1,
                   allow_small_or_imprecise_dtypes=True)
        ang, turns = k.scratch[:, 1, 0, 0:512], k.scratch[:, 2, 0, 0:512]
        s, co = k.scratch[:, 3, 0, 0:512], k.scratch[:, 4, 0, 0:512]
        for t in range(TPB):
            k.ts([g], ang, om, tok[:, t:t + 1])
            k.sincos(ang, s, co, turns)
            k.copy((), k.cosT[:, t, :, :], co.rearrange("p (h d) -> p h d", d=32))
            s3 = s.rearrange("p (h d) -> p h d", d=32)
            for i, f in enumerate((1.0, -1.0, 1.0)):
                last = k.ts([k.A.done.mark()], k.sinT[:, t, :, i, :], s3, f)
            k.A.wait(last)

        k.coef = k.sb("coef", [P, H])
        layer = k.scope
        with ExitStack() as k.scope:
            k.head_tables(par)
        k.scope = layer
        k.ident_b0 = k.sb("zero", [P, 512], BF16)
        k.fill(k.ident_b0[:, :], 0.0)
        k.backwards = k.sb("backwards", [P, P])
        k.fill(k.backwards[:, :], 0.0)
        k.keep_where(k.backwards[:, :], ALU.not_equal, 1.0, 1 - P, [[1, P]], 1)
        k.nT3 = k.sb("nT3", [D, B, S])
        k.slotT = k.sb("slotT", [D, B, 256])
        k.hs = k.sb("hs", [32, H, 32])
        k.so = k.sb("so", [P, B, 2, D])
        k.small3 = [k.sb(f"small3_{i}", [P, NT, 16]) for i in range(3)]
        k.one3 = [k.sb(f"one3_{i}", [P, NT]) for i in range(3)]
        sizes = dict(qkv=1536, a=1024, b=1024, sq=1024, qT=512, kT=512, dk=512, y=1280, pt=1280,
                     oT=512)
        spare = dict(a=k.sT[:, :], b=k.aT[:, :], sq=k.sR.rearrange("p t d -> p (t d)"))
        other = k.sb("lane3", [P, sum(w for n, w in sizes.items() if n not in spare)])
        flat = k.scratch.rearrange("p i b s -> p (i b s)")
        k.lanes3 = []
        for b, mem in enumerate((flat, other)):
            t, at = {}, 0
            for n, w in sizes.items():
                if b == 1 and n in spare:
                    t[n] = spare[n]
                    continue
                t[n] = mem[:, at:at + w]
                at += w
            t["nn"] = k.sb(f"nn3_{b}", [P, 4, 2])
            for n in ("mx", "sum", "qn"):
                t[n] = k.sb(f"{n}3_{b}", [P, 4])
            k.lanes3.append(t)
        k.head = []
        for j in range(2):
            k.head.append(dict(w=k.sb(f"w3_{j}", [D, 3, 2, 64]), wo=k.sb(f"wo3_{j}", [P, D]),
                               tb=k.sb(f"tb3_{j}", [P, 4, 512]),
                               landed=Counter(self.prog, f"head{j}", 16)))
            k.prog.counters.remove(k.head[j]["landed"])
        for j in range(2):
            k.load_head(j, j)

    def head_tables(self, par):
        k, nc, H, X = self, self.nc, self.HEADS, 640
        a, e, v, w = (k.sb(f"ht{i}", [H, X]) for i in range(4))
        ar, er, vr, wr = (t[:, :] for t in (a, e, v, w))
        sp = k.sb("sp", [H, 4])
        u, o = k.sb("spu", [H, 4]), k.sb("spo", [H, 4])
        hp = k.sb("hp", [H, 8])
        mu, vs, nu, coef, icoef, rvn, half, tmp = (hp[:, i:i + 1] for i in range(8))
        raw = par[:, 1:5]
        q = k.stt((), u[:, :], raw, -1.0, raw, ALU.mult, ALU.max)
        q = k.act([q], u[:, :], u[:, :], ACT.Exp, scale=-1.0)
        k.ts([q], o[:, :], u[:, :], 1.0, None, ALU.add)
        q = k.act([k.V.done.mark()], sp[:, :], o[:, :], ACT.Ln)
        k.ts([q], o[:, :], o[:, :], 1.0, None, ALU.subtract)
        z = k.sb("spz", [H, 4])
        k.ts((), z[:, :], o[:, :], 0.0, None, ALU.is_equal)
        k.tt((), sp[:, :], sp[:, :], z[:, :], ALU.add)
        k.tt((), o[:, :], o[:, :], z[:, :], ALU.add)
        k.V.do((), nc.vector.reciprocal, o[:, :], o[:, :])
        k.tt((), sp[:, :], sp[:, :], o[:, :], ALU.mult)
        k.tt((), sp[:, :], sp[:, :], u[:, :], ALU.mult)
        q = k.stt((), sp[:, :], raw, 0.0, sp[:, :], ALU.max, ALU.add)
        q = k.act([q], mu, par[:, 0:1], ACT.Exp, scale=-1.0)
        k.ts([q], mu, mu, 1.0, None, ALU.add)
        k.V.do((), nc.vector.reciprocal, mu, mu)
        k.ts((), mu, mu, 1e-4, None, ALU.add)
        k.ts((), tmp, mu, 2.0)
        k.V.do((), nc.vector.reciprocal, tmp, tmp)
        k.tt((), vs, sp[:, 0:1], tmp, ALU.mult)
        k.tt((), half, sp[:, 1:2], sp[:, 2:3], ALU.add)
        k.copy((), nu, sp[:, 3:4])
        k.ts((), coef, nu, float(k.DH), -0.5, ALU.add, ALU.mult)
        k.tt((), coef, coef, par[:, 5:6], ALU.mult)
        k.stt((), tmp, coef, -1.0, coef, ALU.mult, ALU.max)
        k.ts((), tmp, tmp, 1e-8, None, ALU.is_lt)
        k.stt((), icoef, tmp, -1.0, coef, ALU.mult, ALU.mult)
        k.tt((), coef, coef, icoef, ALU.add)
        k.stt((), coef, tmp, 1e-8, coef, ALU.mult, ALU.add)
        k.V.do((), nc.vector.reciprocal, icoef, coef)
        q = k.G.do((), nc.gpsimd.iota, ar, pattern=[[-1, X]], base=512, channel_multiplier=0,
                   allow_small_or_imprecise_dtypes=True)
        q = k.stt([q], vr, ar, -1.0, ar, ALU.mult, ALU.max)
        k.ts([q], vr, vr, mu, -1.0, ALU.mult, ALU.mult)
        k.ts((), vr, vr, -30.0, None, ALU.max)
        future = k.sb("future", [H, X])
        k.ts((), future[:, :], ar, 0.0, -1e28, ALU.is_lt, ALU.mult)
        q = k.act([k.V.done.mark()], er, vr, ACT.Exp)
        k.ts([q], wr, vr, 1 / 8, 1.0, ALU.mult, ALU.add)
        for n in range(7, 1, -1):
            k.tt((), wr, wr, vr, ALU.mult)
            k.ts((), wr, wr, 1 / n, 1.0, ALU.mult, ALU.add)
        k.tt((), wr, wr, vr, ALU.mult)
        near = ar
        k.ts((), near, vr, -0.25, None, ALU.is_gt)
        k.ts((), vr, er, 1.0, None, ALU.subtract)
        k.tt((), wr, wr, vr, ALU.subtract)
        k.tt((), wr, wr, near, ALU.mult)
        k.tt((), er, er, wr, ALU.add)
        k.tt((), wr, wr, vr, ALU.add)
        k.stt((), vr, wr, 2.0, wr, ALU.add, ALU.mult)
        k.ts((), vr, vr, -1.0)
        k.ts((), vr, vr, vs, half, ALU.mult, ALU.add)
        k.V.do((), nc.vector.reciprocal, wr, er)
        k.ts((), ar, vr, nu)
        k.V.do((), nc.vector.reciprocal, ar, ar)
        k.tt((), ar, ar, er, ALU.mult)
        q = k.act([k.V.done.mark()], vr, vr, ACT.Ln)
        k.stt([q], vr, vr, -0.5 * k.DH, future[:, :], ALU.mult, ALU.add)
        k.ts((), vr, vr, icoef)
        q = k.V.done.mark()
        rows = nc.dram_tensor("head_rows", (H + 2, 4, X), F32).ap()
        cf = nc.dram_tensor("head_coef", (1, H + 2), F32).ap()
        k.c_rows = Counter(k.prog, "store_rows", 16)
        for i, t in enumerate((w, a, v, e)):
            k.load(k.c_rows, rows[0:H, i, :], t[:, :], need=[q])
            k.load(k.c_rows, rows[H:H + 2, i, :], t[0:2, :])
        k.load(k.c_rows, cf[0, 0:H], coef)
        k.load(k.c_rows, cf[0, H:H + 2], hp[0:2, 3:4])
        k.meet()
        k.rows = rows
        c = Counter(k.prog, "load_coef", 16)
        k.load(c, k.coef[:, :], cf[0, 0:H].partition_broadcast(P))
        k.meet()

    def load_head(self, j, h):
        k, t = self, self.head[j]
        X = 640
        R = k.HEADS + 2
        k.load(t["landed"], t["w"][:, :, :, :], k.io["L3_W"][bass.ds(h, 1)]
               .rearrange("a d i j c -> d (a i) j c"))
        k.load(t["landed"], t["wo"][:, :], k.io["L3_Wo"][bass.ds(h, 1)].rearrange("a r c -> r (a c)"))
        row = k.rows[bass.ds(h, 1), 0, 1:2]
        k.load(t["landed"], t["tb"][:, :, :], bass.AP(tensor=row.tensor, offset=row.offset,
                                                      ap=[[1, P], [X, 4], [1, 512]]))
        t["landed"].count = 0

    HEAD_LOADS = 3

    def soft_mixture(self):
        k, H = self, self.HEADS
        xn = k.normed
        k.normalize((), k.n, xn)
        g8 = [P, NT, D]
        k.tt((), xn[:, :, :], xn[:, :, :], k.gam[:, :].unsqueeze(1).broadcast_to(g8), ALU.mult)
        v = k.tt((), xn[:, :, :], xn[:, :, :], k.bet[:, :].unsqueeze(1).broadcast_to(g8), ALU.add)
        ss, r, tot = (t[:, :] for t in k.one3)
        xu = k.moe
        a = k.act([v], xu[:, :, :], xn[:, :, :], ACT.Square)
        v = k.reduce([a], ss, xu[:, :, :], ALU.add)
        k.ts([v], r, ss, 1e-24, None, ALU.max, eng=k.G)
        k.tt((), r, r, k.minus_half[:, 0:NT], ALU.pow, eng=k.G)
        q = k.ts((), r, r, k.mscale[:, 0:1], eng=k.G)
        for t in range(NT):
            v = k.ts([q], xu[:, t, :], xn[:, t, :], r[:, t:t + 1])
        xuT = k.hT
        for t in range(NT):
            m = k.tr([v], k.bank(6 + t // 4)[:, (t % 4) * P:(t % 4 + 1) * P], xu[:, t, :],
                     signal=(t % 4 == 3))
            if t % 4 == 3:
                a = k.copy([m], xuT[:, (t // 4) * S:(t // 4 + 1) * S], k.bank(6 + t // 4), k.A)
        for t in range(NT):
            m = k.mm([a], k.bank(t // 2)[:, (t % 2) * 256:(t % 2 + 1) * 256],
                     xuT[:, t * P:(t + 1) * P], k.mu3[:, :], signal=(t == NT - 1))
        combine, dsp, dspT, cT = (k.wide_pair(2 * i) for i in range(4))
        cmb = combine.rearrange("p a (t c) -> p (a t) c", c=256)
        lg = k.bank(0, 4).rearrange("p a (t c) -> p (a t) c", t=2)
        v = k.reduce([m], ss, lg, ALU.max)
        v = k.ts((), ss, ss, -1.0)
        for t in range(NT):
            c = k.act([v], cmb[:, t, :], lg[:, t, :], ACT.Exp, bias=ss[:, t:t + 1],
                      accum_out=tot[:, t:t + 1])
        v = k.V.do([c], k.nc.vector.reciprocal, tot, tot)
        for t in range(NT):
            v = k.ts((), cmb[:, t, :], cmb[:, t, :], tot[:, t:t + 1])
        for h in range(2):
            for b in range(B):
                m = k.mm([a, k.A.done.mark()], k.bank(4 + 2 * h + b),
                         k.mu3[:, h * P:(h + 1) * P], xuT[:, b * S:(b + 1) * S], signal=True)
        smx, ssum = (t[:, 0, 0:4] for t in k.small3[0:2])
        k.reduce([m], smx, k.bank(4, 4), ALU.max)
        v = k.ts((), smx, smx, -1.0)
        for h in range(2):
            for b in range(B):
                i = 2 * h + b
                w = k.act([v], dspT[:, h, b * S:(b + 1) * S], k.bank(4 + i), ACT.Exp,
                          bias=smx[:, i:i + 1], accum_out=ssum[:, i:i + 1])
        k.V.do([w], k.nc.vector.reciprocal, ssum, ssum)
        for h in range(2):
            for b in range(B):
                i = 2 * h + b
                v = k.ts((), dspT[:, h, b * S:(b + 1) * S], dspT[:, h, b * S:(b + 1) * S],
                         ssum[:, i:i + 1])
        dsp = dsp.rearrange("p a (t c) -> p (a t) c", c=256)
        d = [k.A.done.mark(), v]
        for t in range(NT):
            bank = k.bank(t // 2)
            for h in range(2):
                m = k.tr(d, bank[:, (t % 2) * 256 + h * P:(t % 2) * 256 + (h + 1) * P],
                         dspT[:, h, t * P:(t + 1) * P], signal=(h == 1 and t % 2 == 1))
            if t % 2:
                v = k.copy([m], dsp[:, t - 1:t + 1, :].rearrange("p t c -> p (t c)"), bank,
                           k.A if t // 2 % 2 else k.V)
        for b in range(B):
            for t in range(TPB):
                m = k.mm([k.V.done.mark(), k.A.done.mark()], k.bank(4)[:, b * 256:(b + 1) * 256],
                         xn[:, b * TPB + t, :], dsp[:, b * TPB + t, :], start=(t == 0), stop=(t == TPB - 1),
                         signal=(t == TPB - 1))
        a = k.copy([m], k.slotT.rearrange("p b s -> p (b s)"), k.bank(4), k.A)
        for e in range(H):
            m = k.mm([a], k.bank(5)[0:32, e * 32:(e + 1) * 32], k.w1s[:, e, :],
                     k.slotT[:, :, e * 16:(e + 1) * 16], signal=(e == H - 1))
        v = k.tt([m], k.hs[:, :, :], k.bank(5)[0:32, :].rearrange("p (e c) -> p e c", c=32),
                 k.b1s[:, :].unsqueeze(2).broadcast_to([32, H, 32]), ALU.add)
        a = k.act([v], k.hs[:, :, :], k.hs[:, :, :], ACT.Gelu)
        for e in range(H):
            m = k.mm([a], k.bank(4)[:, e * 32:(e + 1) * 32], k.w2s[:, e, :], k.hs[:, e, :],
                     signal=(e == H - 1))
        for b in range(B):
            v = k.tt([m], k.slotT[:, b, :].rearrange("p (e s) -> p e s", s=16),
                     k.bank(4).rearrange("p (e b s) -> p b e s", b=B, s=16)[:, b],
                     k.b2s[:, :].unsqueeze(2).broadcast_to([D, H, 16]), ALU.add)
        for b in range(B):
            for h in range(2):
                m = k.tr([v], k.bank(5)[:, (2 * b + h) * P:(2 * b + h + 1) * P],
                         k.slotT[:, b, h * P:(h + 1) * P], signal=(b == 1 and h == 1))
        a = k.copy([m], k.so.rearrange("p b h d -> p (b h d)"), k.bank(5), k.A)
        for h in range(2):
            for t in range(NT):
                m = k.tr([v], k.bank(2 * h + t // 4)[:, (t % 4) * P:(t % 4 + 1) * P],
                         cmb[:, t, h * P:(h + 1) * P], signal=(t % 4 == 3))
                if t % 4 == 3:
                    w = k.copy([m], cT[:, h, (t // 4) * S:(t // 4 + 1) * S], k.bank(2 * h + t // 4),
                               k.A if t // 4 else k.V)
        for t in range(NT):
            for h in range(2):
                m = k.mm([a, w, k.A.done.mark(), k.V.done.mark()],
                         k.bank(6 + t // 4)[:, (t % 4) * P:(t % 4 + 1) * P],
                         cT[:, h, t * P:(t + 1) * P], k.so[:, t // 4, h, :], start=(h == 0),
                         stop=(h == 1), signal=(t == NT - 1 and h == 1))
        k.copy([m], k.moe.rearrange("p (a t) d -> p a (t d)", a=2), k.bank(6, 2), k.A)

    def attention_unit(self, b, j, h, free):
        k, t, hd, nc = self, self.lanes3[b], self.head[j], self.nc
        bk = [k.bank(3 * b + i) for i in range(3)]
        w = hd["w"].rearrange("d i j c -> d (i j c)")
        tb = hd["tb"]
        v4 = t["qkv"].rearrange("p (t c) -> p t c", t=4)
        for i in range(4):
            m = k.mm([k.A.done.mark() if i > 1 else None], bk[i % 2][:, 0:384],
                     k.nT3[:, b, i * P:(i + 1) * P], w, signal=True)
            a = k.copy([m], v4[:, i, :], bk[i % 2][:, 0:384], k.A)
        yield
        a4, b4 = (t[n].rearrange("p (t c) -> p t c", t=4) for n in "ab")
        sq = t["sq"].rearrange("p (t c) -> p t c", t=4)
        g = k.tt([a], sq, v4[:, :, 0:256], v4[:, :, 0:256], ALU.mult, k.G)
        cs = k.cosT[:, :, bass.ds(h, 1), :].rearrange("p t a d -> p t (a d)")
        k.tt([a], a4.rearrange("p t (r d) -> p t r d", d=32),
             v4[:, :, 0:256].rearrange("p t (r d) -> p t r d", d=32),
             cs.unsqueeze(2).broadcast_to([P, 4, 8, 32]), ALU.mult)
        sn = k.sinT[:, :, bass.ds(h, 1), :, :].rearrange("p t a i d -> p t (a i d)")
        for i in range(2):
            k.tt((), b4[:, :, 128 * i:128 * i + 64], v4[:, :, 128 * i + 64:128 * i + 128],
                 sn[:, :, 32:96], ALU.mult)
            v = k.tt((), b4[:, :, 128 * i + 64:128 * i + 128], v4[:, :, 128 * i:128 * i + 64],
                     sn[:, :, 0:64], ALU.mult)
        nn = k.reduce([g], t["nn"][:, :, :], sq.rearrange("p t (i c) -> p t i c", i=2), ALU.add)
        m = k.mm([nn], bk[2][:, 0:4], k.backwards[:, :], t["nn"][:, :, 0], signal=True)
        k.copy([m], t["qn"][:, :], bk[2][:, 0:4], k.A)
        for i in range(4):
            dk = k.ts([nn], t["dk"][:, i * P:(i + 1) * P], k.ident[:, :], t["nn"][:, i, 1:2])
        yield
        for i, (n, f) in enumerate((("qT", -2.0), ("kT", 1.0))):
            for tt in range(4):
                k.tr([v], bk[i][:, tt * P:(tt + 1) * P], a4[:, tt, i * P:(i + 1) * P])
                m = k.tr((), bk[i][:, tt * P:(tt + 1) * P], b4[:, tt, i * P:(i + 1) * P],
                         start=False, signal=(tt == 3))
            out = t[n].rearrange("p (t c) -> p t c", t=4)
            if n == "qT":
                out = view(out[:, 0, P - 1:P], [[P, 4], [-1, P]])
            a = k.act([m], out, bk[i].rearrange("p (t c) -> p t c", t=4), ACT.Identity, scale=f)
        yield
        at = [0, 128, 384, 768, 1280]
        mks = [a, a, a]
        ys = []
        for i in range(4):
            wd = (i + 1) * P
            ps = bk[i % 2][:, 0:wd]
            k.mm([a, dk, mks[i % 2]], ps, t["qT"][:, i * P:(i + 1) * P], t["kT"][:, 0:wd], stop=False)
            for jj in range(i + 1):
                m = k.mm((), ps[:, jj * P:(jj + 1) * P], tb[:, 3, (3 - i + jj) * P:(4 - i + jj) * P],
                         t["dk"][:, jj * P:(jj + 1) * P], start=False, signal=(jj == i))
            y = t["y"][:, at[i]:at[i + 1]]
            cols = slice(512 - wd, 512)
            mks[i % 2] = k.stt([m], y, tb[:, 0, cols], t["qn"][:, i:i + 1], ps, ALU.mult, ALU.add)
            v = k.stt((), y, y, 0.0, tb[:, 1, cols], ALU.max, ALU.mult)
            ys.append(k.act([v], y, y, ACT.Ln, bias=1.0))
            if i % 2:
                yield
        cf = k.coef_h[j]
        for i in range(4):
            y = t["y"][:, at[i]:at[i + 1]]
            cols = slice(512 - (i + 1) * P, 512)
            v = k.V.do([ys[i]], nc.vector.tensor_tensor_reduce, y, y, tb[:, 2, cols], cf[:, 0:1],
                       -3e38, ALU.add, ALU.max, t["mx"][:, i:i + 1])
        v = k.ts((), t["mx"][:, :], t["mx"][:, :], -1.0)
        for i in range(4):
            y = t["y"][:, at[i]:at[i + 1]]
            a = k.act([v], y, y, ACT.Exp, bias=t["mx"][:, i:i + 1], accum_out=t["sum"][:, i:i + 1])
        k.V.do([a], nc.vector.reciprocal, t["sum"][:, :], t["sum"][:, :])
        for i in range(4):
            y = t["y"][:, at[i]:at[i + 1]]
            v = k.ts((), y, y, t["sum"][:, i:i + 1])
        yield
        pat = [0, 512, 896, 1152, 1280]
        cp = [None] * 4
        for jj in range(4):
            bank = bk[jj % 2]
            for i in range(jj, 4):
                m = k.tr([v, cp[jj - 2] if jj > 1 else None],
                         bank[:, (i - jj) * P:(i - jj + 1) * P],
                         t["y"][:, at[i] + jj * P:at[i] + (jj + 1) * P], signal=(i == 3))
            cp[jj] = k.copy([m], t["pt"][:, pat[jj]:pat[jj + 1]], bank[:, 0:(4 - jj) * P],
                            k.A if jj % 2 else k.V)
        yield
        for jj in range(4):
            m = k.mm([cp[jj]], bk[2][:, jj * P:512], v4[:, jj, 256:384],
                     t["pt"][:, pat[jj]:pat[jj + 1]], start=(jj == 0), stop=(jj == 3),
                     signal=(jj == 3))
        o = view(t["oT"][:, P - 1:P], [[P, 4], [-1, P]])
        a = k.copy([m], o, bk[2].rearrange("p (t c) -> p t c", t=4), k.A)
        yield
        for i in range(4):
            free[b] = k.mm([a], k.bank(6 + b)[:, i * P:(i + 1) * P], t["oT"][:, i * P:(i + 1) * P],
                           hd["wo"][:, :], start=False, signal=(i == 3))

    def attention(self):
        k = self
        k.coef_h = [k.small3[j][:, 0, 0:1] for j in range(2)]
        k.meet()
        k.A.do((), k.nc.scalar.preload_act_table_set, "natural_log_exp_and_others")
        for b in range(B):
            k.mm((), k.bank(6 + b), k.ident_b0[:, 0:P], k.ident_b0[:, :], signal=(b == 1))

        def body(i):
            for j in range(2):
                k.copy((), k.coef_h[j], k.coef[:, bass.ds(2 * i + j, 1)])
            for j in range(2):
                free = {}
                landed = k.head[j]["landed"]
                for e in (k.T, k.V):
                    e.e.wait_ge(landed.sem, 16 * k.HEAD_LOADS)
                interleave(*(k.attention_unit(b, j, 2 * i + j, free) for b in range(B)))
                k.Y.wait(free[0], free[1], k.V.done.mark(), k.A.done.mark())
                k.Y.e.sem_clear(landed.sem)
                k.load_head(j, 2 * i + j + 2)

        k.prog.loop_over("heads", k.HEADS // 2, body)

    def layer3(self):
        k = self
        k.open_layer(k.nT3, 0)
        k.soft_mixture()
        k.attention()
        k.close_R(k.bank(6, 2).rearrange("p a (t d) -> p (a t) d", d=D), k.moe[:, :, :])

    def run(self, layers):
        k, p = self, self.prog
        with ExitStack() as k.scope:
            k.constants()
            k.norm_scratch()
            k.xs = k.sb("xs", [P, SEQS * TPB, D])
            load_x, store_x = Counter(p, "load_x", 16), Counter(p, "store_x", 16)
            for b in range(SEQS):
                k.load(load_x, k.xs[:, b * TPB:(b + 1) * TPB, :],
                       k.io["x"][b].rearrange("(t p) d -> p t d", p=P))
            k.x, k.n, k.sR, k.moe = (k.sb(n, [P, NT, D]) for n in ("x", "n", "sR", "moe"))
            k.sT, k.hT, k.aT = (k.sb(n, [D, N]) for n in ("sT", "hT", "aT"))
            k.scratch = k.sb("scratch", [D, 11, B, 1 + S])
            k.wide = [k.scratch[:, i, :, :] for i in range(11)]
            whole = k.scope
            for i in range(layers):
                with ExitStack() as k.scope:
                    prepare, layer = ((k.layer0_prepare, k.layer0), (k.layer1_prepare, k.layer1),
                                      (k.layer2_prepare, k.layer2), (k.layer3_prepare, k.layer3))[i]
                    prepare()

                    def chunk(c):
                        k.chunk = c
                        k.copy((), k.x[:, :, :], k.xs[:, bass.ds(c * NT, NT), :], k.A)
                        k.meet()
                        layer()

                    p.loop_over(f"layer{i}", CHUNKS, chunk)
                    if i == 3:
                        for head in k.head:
                            k.Y.e.wait_ge(head["landed"].sem, 16 * k.HEAD_LOADS)
                k.scope = whole
            for b in range(SEQS):
                k.load(store_x, k.io["out"][b].rearrange("(t p) d -> p t d", p=P),
                       k.xs[:, b * TPB:(b + 1) * TPB, :])
            k.Y.wait(store_x.mark())


def build(nc, inputs):
    io = {n: nc.dram_tensor("in_" + n, a.shape, mybir.dt.from_np(a.dtype), kind="ExternalInput").ap()
          for n, a in inputs.items()}
    io["out"] = nc.dram_tensor("out_0", (SEQS, S, D), F32, kind="ExternalOutput").ap()
    k = Kernel(nc, io)
    k.run(LAYERS)


def lay_out_more(a, r, c):
    for i in (1, 3, 2):
        w = np.concatenate([a[f"L1_ffn_w{i}"], a[f"L1_ffn_sw{i}"]])
        r[f"L1_w{i}T"] = w.transpose(0, 2, 1)
    r["L1_routerT"] = a["L1_ffn_router_w"].T
    r["L1_eb"] = a["L1_ffn_expert_bias"]
    for n in ("Wk", "Wv", "Wr", "Wo"):
        r["L1_" + n] = a["L1_attn_" + n]
    for n, m in (("td", "time_decay"), ("tf", "time_first"), ("tmk", "time_mix_key"),
                 ("tmv", "time_mix_value"), ("tmr", "time_mix_receptance")):
        r["L1_" + n] = a["L1_attn_" + m]
    for n in ("wq", "wk", "wv", "wgq", "wgk", "wgv"):
        r["L2_" + n] = a["L2_attn_" + n]
    r["L2_rout"] = a["L2_attn_r_out_w"]
    r["L2_wout"] = a["L2_attn_w_out"]
    r["L2_gl"] = a["L2_attn_gate_local_w"].reshape(-1)
    r["L2_gr"] = a["L2_attn_gate_remote_w"].reshape(-1)
    for n, m in (("theta", "theta"), ("phi", "phi"), ("thetan", "theta_noise"), ("phin", "phi_noise")):
        r["L2_" + n] = a["L2_ffn_" + m]
    w = np.stack([a[f"L3_attn_W{n}"].reshape(D, 2, 16, 64) for n in "qkv"])
    w = w.transpose(3, 1, 0, 2, 4)
    r["L3_W"] = np.concatenate([w, w[:2]])
    w = a["L3_attn_Wo"].reshape(2, 16, 64, D).transpose(1, 0, 2, 3).reshape(16, P, D)
    r["L3_Wo"] = np.concatenate([w, w[:2]])
    r["L3_par"] = np.stack([a["L3_attn_" + n] for n in (
        "mu_raw", "sigma_raw", "eta_raw", "gamma_raw", "nu_raw", "tau")], axis=1)
    r["L3_omega"] = a["L3_attn_omega"]
    r["L3_g"], r["L3_b"] = a["L3_ffn_ln_gamma"], a["L3_ffn_ln_beta"]
    r["L3_scale"] = a["L3_ffn_scale"]
    r["L3_mu"], r["L3_w1"], r["L3_w2"] = (a["L3_ffn_" + n] for n in ("mu", "w1", "w2"))
    r["L3_b1T"], r["L3_b2T"] = a["L3_ffn_b1"].T, a["L3_ffn_b2"].T


def lay_out(a):
    c = np.ascontiguousarray
    r = {"x": a["L0_attn_x"]}
    for n in "qkvo":
        r[f"L0_W{n}T"] = c(a[f"L0_attn_W{n}"].T)
        r[f"L0_b{n}"] = a[f"L0_attn_b{n}"]
    r["L0_qT"] = c(a["L0_ffn_qweights"].transpose(0, 2, 1))
    r["L0_scT"] = c(np.repeat(a["L0_ffn_scales"], 16, axis=2).transpose(0, 2, 1))
    r["L0_la"] = a["L0_ffn_lora_a"]
    r["L0_lbT"] = c(a["L0_ffn_lora_b"].transpose(0, 2, 1))
    r["L0_fb"] = a["L0_ffn_biases"]
    r["L0_fbT"] = c(a["L0_ffn_biases"].T)
    r["L0_lngT"] = c(a["L0_ffn_ln_gamma"].T)
    r["L0_lnbT"] = c(a["L0_ffn_ln_beta"].T)
    lay_out_more(a, r, c)
    return {k: c(v) for k, v in r.items()}


def kernel(**inputs):
    import concourse.bacc as bacc
    from concourse.bass_utils import run_bass_kernel_spmd as run

    nc = bacc.Bacc("TRN2", target_bir_lowering=False, num_devices=1)
    arrays = lay_out({k: np.asarray(v) for k, v in inputs.items()})
    build(nc, arrays)
    r = run(nc, [{"in_" + n: v for n, v in arrays.items()}], core_ids=[0])
    return r.results[0]["out_0"]
```

```python
from contextlib import ExitStack

import numpy as np

import concourse.bass as bass
import concourse.mybir as mybir
from concourse.alu_op_type import AluOpType as ALU

F32 = mybir.dt.float32
BF16 = mybir.dt.bfloat16
I32 = mybir.dt.int32
ACT = mybir.ActivationFunctionType
AX = mybir.AxisListType

LAYERS = 4
P = 128
D = 128
SEQS, S = 8, 512
B = 2
CHUNKS = SEQS // B
N = B * S
NT = N // P
TPB = S // P
ASIDE = "aside"
MASKED = -1e30


class Counter:

    def __init__(self, prog, name, step=1):
        self.prog, self.name, self.step, self.count = prog, name, step, 0
        self.sem = prog.nc.alloc_semaphore(name)
        prog.counters.append(self)

    def mark(self):
        return (self, self.prog.era, self.count)

    def next(self):
        self.count += self.step
        return self.mark()


class Program:

    def __init__(self, nc):
        self.nc, self.era, self.counters, self.engines = nc, 0, [], []

    def new_era(self):
        for e in self.engines:
            for c in self.counters:
                e.wait(c.mark())
        self.nc.all_engine_barrier(sem_only=True)
        for c in self.counters:
            if c.count:
                self.engines[0].e.sem_clear(c.sem)
        self.nc.all_engine_barrier(sem_only=True)
        self.era += 1
        for c in self.counters:
            c.count = 0
        for e in self.engines:
            e.waited = {}

    def loop_over(self, name, n, body):
        self.new_era()
        with self.nc.Fori(0, n) as i:
            body(i)
            self.new_era()


class Engine:

    def __init__(self, prog, eng, name, in_order):
        self.prog, self.e, self.in_order = prog, eng, in_order
        self.done = Counter(prog, name)
        self.waited = {}
        prog.engines.append(self)

    def wait(self, *marks):
        for mark in marks:
            if mark is None or mark is ASIDE:
                continue
            counter, era, count = mark
            if era != self.prog.era or count <= self.waited.get(counter, 0):
                continue
            self.e.wait_ge(counter.sem, count)
            self.waited[counter] = count

    def do(self, need, fn, *args, **kw):
        self.wait(*need)
        if self.in_order and ASIDE not in need:
            self.wait(self.done.mark())
        fn(*args, **kw).then_inc(self.done.sem, 1)
        return self.done.next()

    def quiet(self, need, fn, *args, **kw):
        self.wait(*need)
        fn(*args, **kw)


def interleave(*lanes):
    lanes = [iter(x) for x in lanes]
    while lanes:
        for lane in list(lanes):
            try:
                next(lane)
            except StopIteration:
                lanes.remove(lane)


def pipeline(order, units, front, back, passed=None, lead=0, first_stages=1,
             offset=0):
    marks = [[{} for _ in range(units)] for _ in range(B)]
    free = [{} for _ in range(B)]
    through = {"front": [0] * B, "back": [0] * B}
    stage, running = {}, {}

    def may_go(kind, b):
        u, key = through[kind][b], (kind, b)
        if kind == "back":
            return u < through["front"][b]
        if key not in running:
            ahead = passed is not None and u - 2 >= min(through["front"])
            return u < units and u - 1 <= through["back"][b] and not ahead
        return (u == 0 or through["back"][b] == u or stage[key] < first_stages
                or stage.get(("back", b), 0) >= lead)

    while min(through["back"]) < units:
        for c in order:
            kind, b = ("front" if c in "fF" else "back"), int(c in "FB")
            if b and offset > 0:
                offset -= 1
                continue
            if not may_go(kind, b):
                continue
            key, u = (kind, b), through[kind][b]
            if key not in running:
                running[key] = (front if kind == "front" else back)(b, u, marks[b][u], free[b])
                stage[key] = 0
            stage[key] += 1
            if next(running[key], "end") != "end":
                continue
            del running[key], stage[key]
            through[kind][b] += 1
            if passed and min(through[kind]) == u + 1:
                passed(kind, u, [m[u] for m in marks])


def view(ap, dims, offset=0):
    return bass.AP(tensor=ap.tensor, offset=ap.offset + offset, ap=[list(ap.ap[0])] + dims)


class Kernel:
    def __init__(self, nc, io):
        self.nc, self.io = nc, io
        self.prog = Program(nc)
        p = self.prog
        self.T = Engine(p, nc.tensor, "pe", False)
        self.V = Engine(p, nc.vector, "dve", True)
        self.A = Engine(p, nc.scalar, "act", True)
        self.G = Engine(p, nc.gpsimd, "pool", True)
        self.Y = Engine(p, nc.sync, "sp", False)
        self.engines = [self.T, self.V, self.A, self.G, self.Y]
        self.ps = nc.alloc_psum_tensor("banks", [P, 8, 512], F32)

    def sb(self, name, shape, dt=F32):
        return self.scope.enter_context(self.nc.sbuf_tensor(name, shape, dt))

    def wide_pair(self, i):
        w = self.scratch
        a = w[:, i, 0, 0:1]
        return bass.AP(tensor=a.tensor, offset=a.offset,
                       ap=[list(a.ap[0]), [N, 2], [1, N]])

    def bank(self, k, n=1):
        return self.ps[:, k, :] if n == 1 else self.ps[:, k:k + n, :]

    def meet(self):
        for e in self.engines:
            for c in self.prog.counters:
                e.wait(c.mark())

    def load(self, group, out, src, need=(), eng=None):
        e = eng or self.Y
        e.wait(*need)
        e.e.dma_start(out, src).then_inc(group.sem, 16)
        return group.next()

    def mm(self, need, out, lhsT, rhs, start=True, stop=True, signal=False, **kw):
        f = self.T.do if signal else self.T.quiet
        return f(need, self.nc.tensor.matmul, out, lhsT, rhs, start=start, stop=stop,
                 skip_group_check=True, **kw)

    def tr(self, need, out, in_, signal=False, start=True, ident=None):
        k = in_.shape[0]
        f = self.T.do if signal else self.T.quiet
        i = self.ident if ident is None else ident
        return f(need, self.nc.tensor.matmul, out, in_, i[0:k, 0:k], start=start, stop=True,
                 is_transpose=True, skip_group_check=True)

    def act(self, need, out, in_, func, **kw):
        return self.A.do(need, self.nc.scalar.activation, out, in_, func, **kw)

    def tt(self, need, out, a, b, op, eng=None):
        e = eng or self.V
        return e.do(need, e.e.tensor_tensor, out, a, b, op)

    def ts(self, need, out, a, s1, s2=None, op0=ALU.mult, op1=None, eng=None):
        e = eng or self.V
        if op1 is None:
            return e.do(need, e.e.tensor_scalar, out, a, s1, None, op0)
        return e.do(need, e.e.tensor_scalar, out, a, s1, s2, op0, op1)

    def stt(self, need, out, a, s, b, op0, op1):
        return self.V.do(need, self.nc.vector.scalar_tensor_tensor, out, a, s, b, op0, op1)

    def copy(self, need, out, in_, eng=None):
        e = eng or self.V
        if e is self.A:
            return self.act(need, out, in_, ACT.Identity)
        return e.do(need, e.e.tensor_copy, out, in_)

    def reduce(self, need, out, in_, op, axis=AX.X):
        return self.V.do(need, self.nc.vector.tensor_reduce, out, in_, axis, op)

    def fill(self, out, value, eng=None):
        e = eng or self.G
        return e.do((), e.e.memset, out, value)

    def keep_where(self, ap, op, fill, base, pattern, mult):
        return self.G.do((), self.nc.gpsimd.affine_select, out=ap, in_=ap, compare_op=op,
                         fill=fill, base=base, pattern=pattern, channel_multiplier=mult)

    def constants(self):
        self.ident = self.sb("ident", [P, P])
        self.identb = self.sb("identb", [P, P], BF16)
        self.ones = self.sb("ones", [P, P])
        self.minus_half = self.sb("minus_half", [P, 16])
        self.fill(self.ident[:, :], 0.0)
        self.keep_where(self.ident[:, :], ALU.not_equal, 1.0, 0, [[-1, P]], 1)
        self.fill(self.identb[:, :], 0.0)
        self.keep_where(self.identb[:, :], ALU.not_equal, 1.0, 0, [[-1, P]], 1)
        self.fill(self.ones[:, :], 1.0)
        self.fill(self.minus_half[:, :], -0.5)

    def rsqrt(self, need, out, in_, eps):
        n = in_.shape[1]
        self.ts(need, out, in_, eps, None, ALU.add, eng=self.G)
        return self.tt((), out, out, self.minus_half[:, 0:n], ALU.pow, eng=self.G)

    def norm_scratch(self):
        self.bn = self.sb("bn", [P, NT, 6])
        self.mv = self.sb("mv", [P, NT, 2])
        self.rstd = self.sb("rstd", [P, NT])
        self.normed = self.sb("normed", [P, NT, D])

    def normalize(self, need, src, out, eps=1e-5):
        v = self.nc.vector
        for t in range(NT):
            self.V.do(need, v.bn_stats, self.bn[:, t, :], src[:, t, :])
        for t in range(NT):
            m = self.V.do((), v.bn_aggr, self.mv[:, t, :], self.bn[:, t, :])
        r = self.rsqrt([m], self.rstd[:, :], self.mv[:, :, 1], eps)
        for t in range(NT):
            m = self.ts([r], out[:, t, :], src[:, t, :], self.mv[:, t, 0:1], self.rstd[:, t:t + 1],
                        ALU.subtract, ALU.mult)
        return m

    def window_mask(self, name, w, heads):
        m = self.sb(name, [P, 2 * w], BF16)
        self.fill(m[:, :], 0.0)
        for h in range(heads):
            q = m[h * w:(h + 1) * w, :]
            self.keep_where(q, ALU.is_ge, MASKED, -1, [[1, 2 * w]], -1)
            self.keep_where(q, ALU.is_ge, MASKED, w, [[-1, 2 * w]], 1)
        first = self.sb(name + "_first", [P, 2 * w], BF16)
        self.copy((), first[:, :], m[:, :], self.G)
        self.fill(first[:, 0:w], MASKED)
        return m, first

    def head_select(self, name, q, scale):
        m = self.sb(name, [P, 4, q])
        self.fill(m[:, :, :], scale)
        for g in range(4):
            part = m[32 * g:32 * g + 32, :, :]
            self.keep_where(part, ALU.is_ge, 0.0, 0, [[-8, 4], [0, q]], 1)
            self.keep_where(part, ALU.is_ge, 0.0, 7, [[8, 4], [0, q]], -1)
        return m

    def l0_load(self):
        io = self.io
        self.c_w0 = Counter(self.prog, "load_w0", 16)
        self.w0 = self.sb("w0", [D, 3, D])
        for i, n in enumerate(("WqT", "WkT", "WvT")):
            self.load(self.c_w0, self.w0[:, i, :], io["L0_" + n])
        self.wo0 = self.sb("wo0", [64, 2, D])
        for hp in range(2):
            src = io["L0_WoT"].rearrange("(g hp d) o -> hp g d o", hp=2, d=8)[hp]
            for g in range(8):
                self.load(self.c_w0, self.wo0[8 * g:8 * g + 8, hp, :], src[g], eng=self.A)
        self.b0 = self.sb("b0", [D, 4])
        self.bv0 = self.sb("bv0", [P, D])
        for i, n in enumerate(("bq", "bk", "bo")):
            self.load(self.c_w0, self.b0[:, i:i + 1], io["L0_" + n].rearrange("(a b) -> a b", b=1))
        self.load(self.c_w0, self.bv0[:, :], io["L0_bv"].partition_broadcast(P))

    def l0_attention_prepare(self):
        W = 64
        self.sel0 = self.head_select("sel0", W, 8 ** -0.5)
        self.mask0_rest, self.mask0_first = self.window_mask("mask0_rest", W, 2)
        self.mask0 = self.sb("mask0", [P, 2 * W], BF16)
        self.kT0 = self.sb("kT0", [D, B, W + S])
        self.fill(self.kT0[:, :, 0:W], 0.0)
        self.qT0 = self.sb("qT0", [D, B, S])
        self.v0 = self.sb("v0", [P, B, S // W, 16, 9])
        self.fill(self.v0[:, :, :, :, 8:9], 1.0)
        self.oT0 = self.sb("oT0", [64, B, 2, S])
        self.lanes0 = lanes = []
        for b in range(B):
            t = dict(
                kt=self.sb(f"kt0_{b}", [D, 2 * W]), qx=self.sb(f"qx0_{b}", [D, 4, W]),
                mx=self.sb(f"mx0_{b}", [P, 8]), p=self.sb(f"p0_{b}", [P, 2, 8, P]),
                pt=self.sb(f"pt0_{b}", [P, 8, P]), r=self.sb(f"r0_{b}", [P, 8]),
                o=self.sb(f"o0_{b}", [P, 16, 8]))
            self.fill(t["o"][:, :, :], 0.0)
            lanes.append(t)

    ORDER0 = "fbFB"
    WINDOWS = 4

    def l0_window_front(self, b, u, i, m, free):
        k, W, t = self, 64, self.lanes0[b]
        mask = k.mask0 if u == 0 else k.mask0_rest
        sc = k.bank(4 * b, 2)
        kt = k.copy([free.get("scores")], t["kt"][:, :], k.kT0[:, b, bass.ds(i * W, 2 * W)], k.G)
        q = k.tt([free.get("scores"), ASIDE], t["qx"][:, :, :],
                 k.qT0[:, b, bass.ds(i * W, W)].unsqueeze(1).broadcast_to([P, 4, W]),
                 k.sel0[:, :, :], ALU.mult)
        yield
        for half in range(2):
            k.mm([free.get("sub")], sc[:, half, :], k.identb[:, :],
                 mask[:, :].unsqueeze(1).broadcast_to([P, 4, 2 * W]), stop=False)
        done = {}
        for g in (0, 2, 1, 3):
            rows = slice(32 * g, 32 * g + 32)
            for pair in range(2):
                c = (g % 2 * 2 + pair) * P
                mm = k.mm([kt, q, done.get(g - 1)], sc[:, g // 2, c:c + P],
                          t["qx"][rows, 2 * pair:2 * pair + 2, :], t["kt"][rows, :],
                          start=False, signal=(pair == 1))
            done[g] = mm
        m["mask"] = free["scores"] = mm
        yield
        s3 = sc.rearrange("p a (g t) -> p (a g) t", t=P)
        p = t["p"][:, u % 2, :, :]
        k.reduce([mm, ASIDE], t["mx"][:, :], s3, ALU.max)
        d = free["sub"] = k.tt((), p, s3, t["mx"][:, :].unsqueeze(2).broadcast_to([P, 8, P]),
                               ALU.subtract)
        m["exp"] = k.act([d, ASIDE], p, p, ACT.Exp)

    def l0_window_back(self, b, u, i, m, free):
        k, W, t = self, 64, self.lanes0[b]
        bk = [k.bank(4 * b + 2 + j) for j in range(2)]
        c = []
        for gp in range(8):
            mm = k.tr([m["exp"], free.get("oT")], bk[gp // 4][:, (gp % 4) * P:(gp % 4 + 1) * P],
                      t["p"][:, u % 2, gp, :], signal=(gp % 4 == 3))
            if gp % 4 == 3:
                c.append(k.copy([mm, ASIDE], t["pt"][:, gp - 3:gp + 1, :], bk[gp // 4],
                                k.V if gp == 7 else k.A))
        yield
        tail = bk[0]
        for gp in range(8):
            mm = k.mm(c, tail[:, gp * 18:gp * 18 + 18], t["pt"][:, gp, :],
                      k.v0[:, b, bass.ds(i, 1), 2 * gp:2 * gp + 2, :]
                      .rearrange("p w h c -> p (w h c)"), signal=(gp == 7))
        for hp in range(2):
            rows = slice(64 * hp, 64 * hp + 64)
            pv = tail[rows, 0:144].rearrange("p (g c) -> p g c", c=18)[:, :, 9 * hp:9 * hp + 9]
            k.V.do([mm, ASIDE], k.nc.vector.reciprocal, t["r"][rows, :], pv[:, :, 8])
        for hp in range(2):
            rows = slice(64 * hp, 64 * hp + 64)
            pv = tail[rows, 0:144].rearrange("p (g c) -> p g c", c=18)[:, :, 9 * hp:9 * hp + 9]
            o = k.tt([ASIDE] if hp else (), t["o"][rows, 0:8, :], pv[:, :, 0:8],
                     t["r"][rows, :].unsqueeze(2).broadcast_to([64, 8, 8]), ALU.mult)
        yield
        mm = k.tr([o], bk[1][:, 0:P], t["o"][:, :, :].rearrange("p g d -> p (g d)"), signal=True)
        free["oT"] = k.copy([mm, ASIDE], k.oT0[:, b, :, bass.ds(i * W, W)],
                            bk[1][0:64, 0:P].rearrange("p (h q) -> p h q", h=2), k.A)

    def l0_attention(self):
        W, k = 64, self
        k.copy((), k.mask0[:, :], k.mask0_first[:, :])
        for b in range(B):
            x = k.nT0[:, b, W:W + S]
            for i, out in enumerate((k.qT0[:, b, :], k.kT0[:, b, W:W + S])):
                m = k.mm((), k.bank(4 * b + i), k.w0[:, i, :], x, signal=True)
                k.act([m], out, k.bank(4 * b + i), ACT.Identity, bias=k.b0[:, i:i + 1])
            for w in range(S // W):
                m = k.mm((), k.bank(4 * b + 2 + w // 4)[:, (w % 4) * P:(w % 4 + 1) * P],
                         k.nT0[:, b, w * W:w * W + 2 * W], k.w0[:, 2, :], signal=(w % 4 == 3))
                if w % 4 == 3:
                    k.tt([m, ASIDE], k.v0[:, b, w - 3:w + 1, :, 0:8],
                         k.bank(4 * b + 2 + w // 4).rearrange("p (w h d) -> p w h d", w=4, d=8),
                         k.bv0.rearrange("p (h d) -> p h d", d=8).unsqueeze(1)
                         .broadcast_to([P, 4, 16, 8]), ALU.add)
        k.meet()

        def body(i):
            at = i * k.WINDOWS

            def passed(kind, u, marks):
                if kind == "front" and u == 0:
                    k.copy([m["mask"] for m in marks], k.mask0[:, :], k.mask0_rest[:, :])

            pipeline(k.ORDER0, k.WINDOWS,
                     lambda b, u, m, free: k.l0_window_front(b, u, at + u, m, free),
                     lambda b, u, m, free: k.l0_window_back(b, u, at + u, m, free), passed)

        k.prog.loop_over("l0_attention", S // W // k.WINDOWS, body)
        for b in range(B):
            for hp in range(2):
                m = k.mm((), k.bank(b), k.wo0[:, hp, :], k.oT0[:, b, hp, :], start=(hp == 0),
                         stop=(hp == 1), signal=(hp == 1))
            k.act([m], k.sT[:, b * S:(b + 1) * S], k.bank(b), ACT.Identity, bias=k.b0[:, 2:3])

    def l0_ffn_load(self):
        io, p = self.io, self.prog
        self.c_q = Counter(p, "load_q", 16)
        self.c_f0 = Counter(p, "load_f0", 16)
        self.q0 = self.sb("q0", [D, 6, D], I32)
        self.sc0 = self.sb("sc0", [D, 6, D])
        self.la0, self.lb0 = self.sb("la0", [32, 6, D]), self.sb("lb0", [32, 6, D])
        self.load(self.c_q, self.q0[:, :, :], io["L0_qT"].rearrange("i d o -> d i o"), eng=self.A)
        self.load(self.c_q, self.sc0[:, :, :], io["L0_scT"].rearrange("i d o -> d i o"), eng=self.A)
        self.load(self.c_q, self.la0[:, :, :], io["L0_la"].rearrange("i r d -> r i d"), eng=self.A)
        self.load(self.c_q, self.lb0[:, :, :], io["L0_lbT"].rearrange("i r o -> r i o"), eng=self.A)
        self.fb_row = self.sb("fb_row", [1, 3, D])
        self.fb_col = self.sb("fb_col", [D, 6])
        self.ln_g0, self.ln_b0 = self.sb("ln_g0", [D, 3]), self.sb("ln_b0", [D, 3])
        self.load(self.c_f0, self.fb_row[:, :, :],
                  io["L0_fb"].rearrange("(j two) o -> two j o", two=2)[0:1], eng=self.A)
        self.load(self.c_f0, self.fb_col[:, :], io["L0_fbT"], eng=self.A)
        self.load(self.c_f0, self.ln_g0[:, :], io["L0_lngT"], eng=self.A)
        self.load(self.c_f0, self.ln_b0[:, :], io["L0_lnbT"], eng=self.A)

    def l0_ffn_weights(self):
        k = self
        self.wf0 = self.sb("wf0", [D, 6, D])
        k.ts([k.c_q.mark()], k.wf0[:, :, :], k.q0[:, :, :], 1 / 7.5, -1.0, ALU.mult, ALU.add)
        k.tt((), k.wf0[:, :, :], k.wf0[:, :, :], k.sc0[:, :, :], ALU.mult)
        for i in range(6):
            m = k.mm([k.c_q.mark()], k.bank(i // 4)[:, (i % 4) * P:(i % 4 + 1) * P], k.la0[:, i, :],
                     k.lb0[:, i, :], signal=(i in (3, 5)))
            if i == 3:
                k.tt([m], k.wf0[:, 0:4, :], k.wf0[:, 0:4, :],
                     k.bank(0).rearrange("p (i o) -> p i o", o=P), ALU.add)
        return k.tt([m], k.wf0[:, 4:6, :], k.wf0[:, 4:6, :],
                    k.bank(1)[:, 0:256].rearrange("p (i o) -> p i o", o=P), ALU.add)

    def l0_ffn(self):
        k = self
        y = self.bank(0, 2)
        last = [k.c_f0.mark()]
        for blk in range(3):
            def h_of(t):
                if blk:
                    return k.hT[:, t * P:(t + 1) * P]
                return k.nT0[:, t // 4, 64 + (t % 4) * P:64 + (t % 4 + 1) * P]
            w1, w2 = k.wf0[:, 2 * blk, :], k.wf0[:, 2 * blk + 1, :]
            for half in range(2):
                k.mm(last, y[:, half, :], k.ones[0:1, :],
                     k.fb_row[:, blk, :].unsqueeze(1).broadcast_to([1, 4, D]), stop=False)
                for t in range(4 * half, 4 * half + 4):
                    m = k.mm((), y[:, half, (t % 4) * P:(t % 4 + 1) * P], h_of(t), w1, start=False,
                             signal=(t % 4 == 3))
            y8 = y.rearrange("p a (t d) -> p (a t) d", d=D)
            m = k.normalize([m], y8, k.normed)
            halves = []
            for t in range(NT):
                mm = k.tr([m], k.bank(2 + t // 4)[:, (t % 4) * P:(t % 4 + 1) * P],
                          k.normed[:, t, :], signal=(t % 4 == 3))
                if t % 4 == 3:
                    halves.append(mm)
            outs = []
            for half in range(2):
                g = k.act([halves[half]], k.aT[:, half * S:(half + 1) * S], k.bank(2 + half),
                          ACT.Gelu, bias=k.ln_b0[:, blk:blk + 1], scale=k.ln_g0[:, blk:blk + 1])
                outs.append(k.mm([g], k.bank(4 + half), w2, k.aT[:, half * S:(half + 1) * S],
                                 signal=True))
            for half in range(2):
                prev = k.hT[:, half * S:(half + 1) * S] if blk else k.nT0[:, half, 64:64 + S]
                m = k.stt([outs[half]], k.hT[:, half * S:(half + 1) * S], k.bank(4 + half),
                          k.fb_col[:, 2 * blk + 1:2 * blk + 2], prev, ALU.add, ALU.add)
            last = [m]
        return m

    def close_T(self, s, h):
        k = self
        k.meet()
        for half in range(2):
            c = slice(half * S, (half + 1) * S)
            a = k.act((), k.aT[:, c], h[:, c], ACT.Tanh, scale=0.5)
            v = k.stt([a], k.aT[:, c], k.aT[:, c], 1.0, h[:, c], ALU.add, ALU.mult)
            v = k.stt((), k.aT[:, c], k.aT[:, c], 0.5, s[:, c], ALU.mult, ALU.mult)
            for t in range(4):
                m = k.tr([v], k.bank(half)[:, t * P:(t + 1) * P],
                         k.aT[:, half * S + t * P:half * S + (t + 1) * P], signal=(t == 3))
            v = k.tt([m], k.xs[:, bass.ds(k.chunk * NT + 4 * half, 4), :],
                     k.x[:, 4 * half:4 * half + 4, :],
                     k.bank(half).rearrange("p (t d) -> p t d", d=D), ALU.add)
        k.meet()

    def close_R(self, s, f):
        k = self
        k.meet()
        t = k.normed
        a = k.act((), t[:, :, :], f, ACT.Tanh, scale=0.5)
        k.stt([a], t[:, :, :], t[:, :, :], 1.0, f, ALU.add, ALU.mult)
        k.stt((), t[:, :, :], t[:, :, :], 0.5, s, ALU.mult, ALU.mult)
        k.tt((), k.xs[:, bass.ds(k.chunk * NT, NT), :], k.x[:, :, :], t[:, :, :], ALU.add)
        k.meet()

    def open_layer(self, out, pad):
        k = self
        m = k.normalize((), k.x, k.n)
        for b in range(B):
            for t in range(TPB):
                mm = k.tr([m], k.bank(b)[:, t * P:(t + 1) * P], k.n[:, b * TPB + t, :],
                          signal=(t == 3))
            k.copy([mm], out[:, b, pad:pad + S], k.bank(b), k.A if b else k.V)
        k.meet()

    def layer0_prepare(self):
        k = self
        k.l0_load()
        k.l0_ffn_load()
        k.nT0 = k.sb("nT0", [D, B, 64 + S])
        k.fill(k.nT0[:, :, 0:64], 0.0)
        k.l0_attention_prepare()
        k.l0_ffn_weights()

    def layer0(self):
        k = self
        k.open_layer(k.nT0, 64)
        k.l0_ffn()
        k.meet()
        k.l0_attention()
        k.close_T(k.sT, k.hT)

    def layer1_prepare(self):
        k, io = self, self.io
        c = Counter(self.prog, "load_l1", 16)
        k.w1 = k.sb("w1", [D, 10, 256])
        k.w3 = k.sb("w3", [D, 10, 256])
        k.w2 = k.sb("w2", [P, 10, 2, D])
        k.load(c, k.w1[:, :, :], io["L1_w1T"].rearrange("e d h -> d e h"))
        k.load(c, k.w3[:, :, :], io["L1_w3T"].rearrange("e d h -> d e h"), eng=k.A)
        k.load(c, k.w2[:, :, :, :], io["L1_w2T"].rearrange("e (m p) d -> p e m d", p=P))
        k.router = k.sb("router", [D, 8])
        k.router_b = k.sb("router_b", [1, 8])
        k.load(c, k.router[:, :], io["L1_routerT"])
        k.load(c, k.router_b[:, :], io["L1_eb"].rearrange("(a b) -> a b", a=1))
        k.rw = k.sb("rw", [D, 3, D])
        k.rwo = k.sb("rwo", [D, D])
        k.rp = k.sb("rp", [D, 5])
        for i, n in enumerate("kvr"):
            k.load(c, k.rw[:, i, :], io[f"L1_W{n}"], eng=k.A)
        k.load(c, k.rwo[:, :], io["L1_Wo"])
        for i, n in enumerate(("td", "tf", "tmk", "tmv", "tmr")):
            k.load(c, k.rp[:, i:i + 1], io["L1_" + n].rearrange("(a b) -> a b", b=1), eng=k.A)
        k.meet()
        k.td = k.sb("td", [D, 1])
        k.act((), k.td[:, :], k.rp[:, 0:1], ACT.Exp)
        k.ts([k.A.done.mark()], k.td[:, :], k.td[:, :], -1.0)
        k.rw_now, k.rw_before = k.sb("rw_now", [D, 3, D]), k.sb("rw_before", [D, 3, D])
        k.rest = k.sb("rest", [D, 3])
        k.ts((), k.rest[:, :], k.rp[:, 2:5], -1.0, 1.0, ALU.mult, ALU.add)
        for i in range(3):
            k.ts((), k.rw_now[:, i, :], k.rw[:, i, :], k.rp[:, 2 + i:3 + i])
            k.ts((), k.rw_before[:, i, :], k.rw[:, i, :], k.rest[:, i:i + 1])
        k.nT1 = k.sb("nT1", [D, B, 1 + S])
        k.fill(k.nT1[:, :, 0:1], 0.0)
        k.rank = k.sb("rank", [P, NT, 8])
        k.G.do((), k.nc.gpsimd.iota, k.rank[:, :, :], pattern=[[0, NT], [-1, 8]], base=8,
               channel_multiplier=0, allow_small_or_imprecise_dtypes=True)
        k.cw = k.sb("cw", [P, NT, 8])
        k.route_scratch = [k.sb(f"route{i}", [P, NT, 8]) for i in range(4)]
        k.route_top = k.sb("route_top", [P, NT, 4])

    def time_mixing(self):
        k = self
        w = [x[:, :, :] for x in k.wide]
        kT, vT, rT, mx, num, den, mo, e1, e2, f1, f2 = w[:11]
        cols, prev = slice(1, 1 + S), slice(0, S)
        for b in range(B):
            marks = []
            for i in range(3):
                k.mm((), k.bank(2 * i + b), k.rw_now[:, i, :], k.nT1[:, b, cols], stop=False)
                marks.append(k.mm((), k.bank(2 * i + b), k.rw_before[:, i, :], k.nT1[:, b, prev],
                                  start=False, signal=True))
            k.act([marks[0]], kT[:, b, cols], k.bank(b), ACT.Identity)
            k.act([marks[1]], vT[:, b, cols], k.bank(2 + b), ACT.Identity)
            a = k.act([marks[2]], rT[:, b, cols], k.bank(4 + b), ACT.Tanh, scale=0.5)
        K, Vv, R = kT[:, :, cols], vT[:, :, cols], rT[:, :, cols]
        k.V.do((), k.nc.vector.memset, mx[:, :, 0:1], -1e38)
        k.V.do((), k.nc.vector.memset, num[:, :, 0:1], 0.0)
        k.V.do((), k.nc.vector.memset, den[:, :, 0:1], 0.0)
        scan = k.nc.vector.tensor_tensor_scan
        for b in range(B):
            v = k.V.do([a], scan, mx[:, b, cols], k.td[:, 0:1].broadcast_to([D, S]), kT[:, b, cols],
                       -1e38, ALU.add, ALU.max)
        mp, mn = mx[:, :, prev], mx[:, :, cols]
        F1, F2, E1, E2, MO = (x[:, :, cols] for x in (f1, f2, e1, e2, mo))
        g = k.tt([v], F2, K, mn, ALU.subtract, k.G)
        v = k.stt((), F1, mp, k.td[:, 0:1], mn, ALU.add, ALU.subtract)
        x2 = k.act([g], F2, F2, ACT.Exp)
        x1 = k.act([v], F1, F1, ACT.Exp)
        v = k.stt((), MO, K, k.rp[:, 1:2], mp, ALU.add, ALU.max)
        g = k.tt([v, x2], E1, F2, Vv, ALU.mult, k.G)
        v = k.stt((), E2, K, k.rp[:, 1:2], MO, ALU.add, ALU.subtract)
        y2 = k.act([v], E2, E2, ACT.Exp)
        for b in range(B):
            k.V.do([g, x1], scan, num[:, b, cols], f1[:, b, cols], e1[:, b, cols], 0.0,
                   ALU.mult, ALU.add)
            v = k.V.do([x2], scan, den[:, b, cols], f1[:, b, cols], f2[:, b, cols], 0.0,
                       ALU.mult, ALU.add)
        g = k.tt([v], MO, mp, MO, ALU.subtract, k.G)
        y1 = k.act([g], E1, MO, ACT.Exp)
        g = k.tt([y2, v], F2, E2, Vv, ALU.mult, k.G)
        k.tt([y1, g], F1, E1, num[:, :, prev], ALU.mult)
        k.tt((), F1, F1, F2, ALU.add)
        k.tt((), MO, E1, den[:, :, prev], ALU.mult)
        k.tt((), MO, MO, E2, ALU.add)
        k.V.do((), k.nc.vector.reciprocal, MO, MO)
        k.tt((), F1, F1, MO, ALU.mult)
        k.stt((), F1, R, 1.0, F1, ALU.add, ALU.mult)
        v = k.ts((), F1, F1, 0.5)
        for t in range(NT):
            m = k.mm([v], k.bank(6 + t // 4)[:, (t % 4) * P:(t % 4 + 1) * P],
                     f1[:, t // 4, 1 + (t % 4) * P:1 + (t % 4 + 1) * P], k.rwo[:, :],
                     signal=(t == NT - 1))
        k.copy([m], k.sR.rearrange("p (a t) d -> p a (t d)", a=2), k.bank(6, 2), k.A)

    def route(self):
        k = self
        z = k.bank(0)[:, 0:NT * 8]
        k.mm((), z, k.ones[0:1, :], k.router_b[:, :].unsqueeze(1).broadcast_to([1, NT, 8]), stop=False)
        for t in range(NT):
            m = k.mm((), z[:, 8 * t:8 * t + 8], k.nT1[:, t // 4, 1 + (t % 4) * P:1 + (t % 4 + 1) * P],
                     k.router[:, :], start=False, signal=(t == NT - 1))
        top = k.route_top
        l, c, one, two = (x[:, :, :] for x in k.route_scratch)
        full = [P, NT, 8]

        def col(i):
            return top[:, :, i:i + 1].broadcast_to(full)

        def first_largest(out, j):
            k.reduce((), top[:, :, j], l, ALU.max)
            k.tt((), c, l, col(j), ALU.is_ge)
            k.tt((), c, c, k.rank[:, :, :], ALU.mult)
            k.reduce((), top[:, :, 2], c, ALU.max)
            k.tt((), out, c, col(2), ALU.is_equal)

        k.copy([m], l, z.rearrange("p (t e) -> p t e", e=8))
        first_largest(one, 0)
        k.stt((), l, one, -3e38, l, ALU.mult, ALU.add)
        first_largest(two, 1)
        v = k.tt((), top[:, :, 2], top[:, :, 1], top[:, :, 0], ALU.subtract)
        a = k.act([v], top[:, :, 2], top[:, :, 2], ACT.Exp)
        k.ts([a], top[:, :, 3], top[:, :, 2], 1.0, None, ALU.add)
        k.V.do((), k.nc.vector.reciprocal, top[:, :, 3], top[:, :, 3])
        k.tt((), one, one, col(3), ALU.mult)
        k.tt((), top[:, :, 3], top[:, :, 3], top[:, :, 2], ALU.mult)
        k.tt((), two, two, col(3), ALU.mult)
        v = k.tt((), k.cw[:, :, :], one, two, ALU.add)
        return k.ts((), k.cw[:, :, :], k.cw[:, :, :], 0.5)

    def experts(self):
        k = self
        t = [k.wide[i] for i in range(2)]
        g = [k.wide_pair(2), k.wide_pair(4)]
        free = {}
        acc_done, y_done, unit, pending = None, {}, 0, None

        def outputs(e):
            nonlocal acc_done
            marks = []
            for i in range(NT):
                for m in range(2):
                    mk = k.mm([acc_done, g_done[e]], k.bank(6 + i // 4)[:, (i % 4) * P:(i % 4 + 1) * P],
                              g[e % 2][:, m, i * P:(i + 1) * P], k.w2[:, e, m, :], start=(m == 0),
                              stop=(m == 1), signal=(m == 1 and i % 4 == 3))
                if i % 4 == 3:
                    marks.append(mk)
            y_done[e] = marks[1]
            y = k.bank(6, 2).rearrange("p a (t d) -> p (a t) d", d=D)
            if e >= 8:
                acc_done = k.stt([marks[1]], k.moe[:, :, :], y, 0.5, k.moe[:, :, :], ALU.mult, ALU.add)
                return
            for i in range(NT):
                need = [marks[i // 4]]
                if e == 0:
                    acc_done = k.ts(need, k.moe[:, i, :], y[:, i, :], k.cw[:, i, e:e + 1])
                else:
                    acc_done = k.stt(need, k.moe[:, i, :], y[:, i, :], k.cw[:, i, e:e + 1],
                                     k.moe[:, i, :], ALU.mult, ALU.add)

        g_done = {}
        for e in range(10):
            for b in range(B):
                x = k.nT1[:, b, 1:1 + S]
                for m in range(2):
                    p = unit % 3
                    h1, h3, ts_ = k.bank(2 * p), k.bank(2 * p + 1), t[unit % 2][:, 0, 0:S]
                    k.mm([free.get(p)], h1, k.w1[:, e, m * P:(m + 1) * P], x)
                    mk = k.mm((), h3, k.w3[:, e, m * P:(m + 1) * P], x, signal=True)
                    a = k.act([mk, free.get(("t", unit % 2))], ts_, h1, ACT.Tanh, scale=0.5)
                    v = k.stt([a], ts_, ts_, 1.0, h1, ALU.add, ALU.mult)
                    v = k.tt([y_done.get(e - 2)], g[e % 2][:, m, b * S:(b + 1) * S], ts_, h3,
                             ALU.mult)
                    free[p] = free["t", unit % 2] = v
                    unit += 1
            g_done[e] = v
            if e:
                outputs(e - 1)
        outputs(9)

    def layer1(self):
        k = self
        k.open_layer(k.nT1, 1)
        k.time_mixing()
        k.meet()
        k.route()
        k.meet()
        k.experts()
        k.close_R(k.sR[:, :, :], k.moe[:, :, :])

    def sincos(self, ang, sin, cos, turns):
        k = self
        two_pi = 2 * np.pi
        c1 = 6.28125
        c2 = float(np.round((two_pi - c1) * 2.0 ** 20) / 2.0 ** 20)
        c3 = two_pi - c1 - c2
        nearest = 1.5 * 2.0 ** 23
        k.ts((), turns, ang, 1 / two_pi, nearest, ALU.mult, ALU.add)
        k.ts((), turns, turns, nearest, None, ALU.subtract)
        k.stt((), ang, turns, -c1, ang, ALU.mult, ALU.add)
        k.stt((), ang, turns, -c2, ang, ALU.mult, ALU.add)
        k.stt((), ang, turns, -c3, ang, ALU.mult, ALU.add)
        pi = float(np.nextafter(np.float32(np.pi), np.float32(0)))
        v = k.ts((), ang, ang, pi, -pi, ALU.min, ALU.max)
        k.act([v], sin, ang, ACT.Sin)
        a = k.act((), cos, ang, ACT.Sin, scale=0.5)
        k.tt([a], cos, cos, cos, ALU.mult)
        return k.ts((), cos, cos, -2.0, 1.0, ALU.mult, ALU.add)

    def layer2_prepare(self):
        k, io = self, self.io
        c = Counter(self.prog, "load_l2", 16)
        W = 32
        k.wqkv2 = k.sb("wqkv2", [D, 3, D])
        for i, n in enumerate("qkv"):
            k.load(c, k.wqkv2[:, i, :], io["L2_w" + n])
        k.wg2 = k.sb("wg2", [D, 3, 64])
        for i, n in enumerate("qkv"):
            k.load(c, k.wg2[:, i, :], io["L2_wg" + n], eng=k.A)
        k.rout2 = k.sb("rout2", [64, D])
        k.load(c, k.rout2[:, :], io["L2_rout"])
        k.wout2 = k.sb("wout2", [D, D])
        k.load(c, k.wout2[:, :], io["L2_wout"])
        k.wout2_hp = k.sb("wout2_hp", [32, 4, D])
        src = io["L2_wout"].rearrange("(g hp d) o -> g hp d o", hp=4, d=8)
        for g in range(4):
            k.load(c, k.wout2_hp[8 * g:8 * g + 8, :, :], src[g].rearrange("hp d o -> d hp o"), eng=k.A)
        k.gate_w = k.sb("gate_w", [D, 2])
        k.load(c, k.gate_w[:, 0:1], io["L2_gl"].rearrange("(a b) -> a b", b=1))
        k.load(c, k.gate_w[:, 1:2], io["L2_gr"].rearrange("(a b) -> a b", b=1))
        k.trig = k.sb("trig", [D, 2, D])
        noise = k.scratch[:, 0, 0, 0:256].rearrange("p (i o) -> p i o", i=2)
        k.load(c, k.trig[:, 0, :], io["L2_theta"])
        k.load(c, k.trig[:, 1, :], io["L2_phi"])
        k.load(c, noise[:, 0, :], io["L2_thetan"])
        k.load(c, noise[:, 1, :], io["L2_phin"])
        k.meet()
        k.tt((), k.trig[:, :, :], k.trig[:, :, :], noise, ALU.add)
        s, co, tu, an = (k.scratch[:, i, 0, 0:256] for i in range(1, 5))
        k.copy((), an, k.trig.rearrange("p i o -> p (i o)"))
        k.sincos(an, s, co, tu)
        k.copy((), k.trig[:, 0, :], co[:, 0:D])
        k.copy((), k.trig[:, 1, :], s[:, D:2 * D])
        k.ts((), k.wout2[:, :], k.wout2[:, :], 0.5)
        k.ts((), k.wout2_hp[:, :, :], k.wout2_hp[:, :, :], 0.5)
        k.sel2 = k.head_select("sel2", W, 8 ** -0.5)
        rest, first = k.window_mask("mask2w", W, 4)
        k.mask2_rest, k.mask2_first = (k.sb("mask2" + n, [P, 4, 2 * W], BF16)
                                       for n in ("_rest", "_first"))
        k.copy((), k.mask2_rest[:, :, :], rest[:, :].unsqueeze(1).broadcast_to([P, 4, 2 * W]), k.G)
        k.copy((), k.mask2_first[:, :, :], k.mask2_rest[:, :, :], k.G)
        k.copy((), k.mask2_first[:, 0, :], first[:, :], k.G)
        k.glw = k.sb("glw", [D, 4])
        k.fill(k.glw[:, :], 1.0)
        k.keep_where(k.glw[:, :], ALU.is_ge, 0.0, 0, [[-32, 4]], 1)
        k.keep_where(k.glw[:, :], ALU.is_ge, 0.0, 31, [[32, 4]], -1)
        k.ts((), k.glw[:, :], k.glw[:, :], k.gate_w[:, 0:1], eng=k.G)
        k.grw = k.sb("grw", [D, 16, 8])
        k.fill(k.grw[:, :, :], 1.0)
        k.keep_where(k.grw[:, :, :], ALU.is_ge, 0.0, 0, [[-8, 16], [0, 8]], 1)
        k.keep_where(k.grw[:, :, :], ALU.is_ge, 0.0, 7, [[8, 16], [0, 8]], -1)
        k.ts((), k.grw[:, :, :], k.grw[:, :, :], k.gate_w[:, 1:2], eng=k.G)
        k.selg = k.sb("selg", [64, 8, 64])
        k.fill(k.selg[:, :, :], 1.0)
        k.keep_where(k.selg[:, :, :], ALU.is_ge, 0.0, 0, [[-8, 8], [0, 64]], 1)
        k.keep_where(k.selg[:, :, :], ALU.is_ge, 0.0, 7, [[8, 8], [0, 64]], -1)
        k.maskg = k.sb("maskg", [P, TPB, 64], BF16)
        k.fill(k.maskg[:, :, :], 0.0)
        k.keep_where(k.maskg[:, :, :], ALU.is_ge, MASKED, 0, [[P, TPB], [-8, 64]], 1)
        k.half2 = k.sb("half2", [P, 2, 9])
        k.fill(k.half2[:, :, :], 1.0)
        k.keep_where(k.half2[:, :, :], ALU.is_ge, 0.0, 0, [[-64, 2], [0, 9]], 1)
        k.keep_where(k.half2[:, :, :], ALU.is_ge, 0.0, 63, [[64, 2], [0, 9]], -1)
        k.quad2 = k.sb("quad2", [P, 4, 9])
        k.fill(k.quad2[:, :, :], 1.0)
        k.keep_where(k.quad2[:, :, :], ALU.is_ge, 0.0, 0, [[-32, 4], [0, 9]], 1)
        k.keep_where(k.quad2[:, :, :], ALU.is_ge, 0.0, 31, [[32, 4], [0, 9]], -1)
        k.nT2 = k.sb("nT2", [D, B, W + S])
        k.fill(k.nT2[:, :, 0:W], 0.0)
        k.pool2 = k.sb("pool2", [D, B, 2, 64])
        k.gk2 = k.sb("gk2", [64, B, 8, 64])
        k.gv2 = k.sb("gv2", [P, B, 4, 2, 9])
        for b in range(B):
            k.copy((), k.gv2[:, b, :, :, 8:9], k.half2[:, :, 8:9].unsqueeze(1)
                   .broadcast_to([P, 4, 2, 1]), k.G)
        k.lanes2g = [dict(mx=k.sb(f"mx2g_{b}", [P, 8]), p=k.sb(f"p2g_{b}", [P, 8, 64]),
                          pt=k.sb(f"pt2g_{b}", [P, 4, P]), o=k.sb(f"o2g_{b}", [P, 8, 8]))
                     for b in range(4)]
        k.kT2 = k.sb("kT2", [D, B, W + S])
        k.fill(k.kT2[:, :, 0:W], 0.0)
        k.v2 = k.sb("v2", [P, B, 2 * TPB, 16, 9])
        k.fill(k.v2[:, :, :, :, 8:9], 1.0)
        k.oT2 = k.sb("oT2", [32, B, 4, S])
        k.lanes2 = []
        for b in range(B):
            t = dict(qx=k.sb(f"qx2_{b}", [D, 2, 4, 4, W]),
                     mx=k.sb(f"mx2_{b}", [P, 16]), r=k.sb(f"r2_{b}", [P, 16]),
                     p=k.sb(f"p2_{b}", [P, 2, 8, P]), pt=k.sb(f"pt2_{b}", [P, 8, P]),
                     gate=k.sb(f"gate2_{b}", [P, 16]), ox=k.sb(f"ox2_{b}", [P, 16, 36]),
                     os=k.sb(f"os2_{b}", [P, 16, 9]), o=k.sb(f"o2_{b}", [P, 4, 4, 8]))
            k.lanes2.append(t)

    def latent_attention(self):
        k = self
        qT, gr, gq, rem = (k.wide[i] for i in range(4))
        for b in range(B):
            x = k.nT2[:, b, 32:32 + S]
            m = k.mm((), k.bank(b), k.wqkv2[:, 0, :], x, signal=True)
            a = k.copy([m], qT[:, b, 0:S], k.bank(b), k.A)
            m = k.mm([a], k.bank(b), k.grw.rearrange("p h d -> p (h d)"), qT[:, b, 0:S], signal=True)
            k.act([m], gr[:, b, 0:S], k.bank(b), ACT.Tanh, scale=0.5)
            m = k.mm((), k.bank(2 + b)[0:64, :], k.wg2[:, 0, :], x, signal=True)
            k.act([m], gq[0:64, b, 0:S], k.bank(2 + b)[0:64, :], ACT.Identity, scale=8 ** -0.5)
            k.reduce((), k.pool2[:, b, 0, :], x.rearrange("p (n c) -> p n c", c=8), ALU.add)
        v = k.ts((), k.pool2[:, :, 0, :], k.pool2[:, :, 0, :], 1 / 8)
        v = k.copy((), k.pool2[:, :, 1, :], k.pool2[:, :, 0, :])
        for b in range(B):
            m = k.mm([v], k.bank(4)[0:64, b * 64:b * 64 + 64], k.wg2[:, 1, :], k.pool2[:, b, 0, :])
            m = k.mm((), k.bank(4)[:, 256 + b * 64:320 + b * 64],
                     k.pool2[:, b, :, :].rearrange("p i n -> p (i n)"), k.wg2[:, 2, :],
                     signal=True)
        for b in range(B):
            k.tt([m], k.gk2[:, b, :, :], k.bank(4)[0:64, b * 64:b * 64 + 64].unsqueeze(1)
                 .broadcast_to([64, 8, 64]), k.selg[:, :, :], ALU.mult)
            gv = k.tt((), k.gv2[:, b, :, :, 0:8], k.bank(4)[:, 256 + b * 64:320 + b * 64]
                      .rearrange("p (a h d) -> p a h d", a=4, h=2),
                      k.half2[:, :, 0:8].unsqueeze(1).broadcast_to([P, 4, 2, 8]), ALU.mult)
        k.meet()

        def lane(n, tiles):
            t = k.lanes2g[n]
            sc, small = k.bank(2 * n), k.bank(2 * n + 1)
            free = None
            for tile in tiles:
                cols = slice((tile % 4) * P, (tile % 4 + 1) * P)
                b = tile // 4
                k.mm([free], sc, k.identb[:, :], k.maskg[:, tile % 4, :].unsqueeze(1)
                     .broadcast_to([P, 8, 64]), stop=False)
                m = k.mm((), sc, gq[0:64, b, cols], k.gk2[:, b, :, :].rearrange("p h n -> p (h n)"),
                         start=False, signal=True)
                s3 = sc.rearrange("p (h n) -> p h n", n=64)
                k.reduce([m, ASIDE], t["mx"][:, :], s3, ALU.max)
                v = k.tt((), t["p"][:, :, :], s3, t["mx"][:, :].unsqueeze(2).broadcast_to([P, 8, 64]),
                         ALU.subtract)
                a = k.act([v, ASIDE], t["p"][:, :, :], t["p"][:, :, :], ACT.Exp)
                yield
                for pair in range(4):
                    m = k.tr([a], sc[:, pair * P:(pair + 1) * P],
                             t["p"][:, 2 * pair:2 * pair + 2, :].rearrange("p h n -> p (h n)"),
                             signal=(pair == 3))
                a = k.copy([m, ASIDE], t["pt"].rearrange("p a n -> p (a n)"), sc, k.A)
                yield
                for pair in range(4):
                    m = k.mm([a], small[:, pair * 18:pair * 18 + 18], t["pt"][:, pair, :],
                             k.gv2[:, b, pair, :, :].rearrange("p h c -> p (h c)"),
                             signal=(pair == 3))
                o = small[:, 0:72].rearrange("p (h c) -> p h c", c=9)
                k.V.do([m, ASIDE], k.nc.vector.reciprocal, t["mx"][:, :], o[:, :, 8])
                v = k.tt((), t["o"][:, :, :], o[:, :, 0:8],
                         t["mx"][:, :].unsqueeze(2).broadcast_to([P, 8, 8]), ALU.mult)
                yield
                m = k.tr([v], small[0:64, 128:256], t["o"][:, :, :].rearrange("p h d -> p (h d)"),
                         signal=True)
                free = k.copy([m, ASIDE], rem[0:64, b, cols], small[0:64, 128:256], k.A)
                yield

        interleave(*(lane(n, (2 * n, 2 * n + 1)) for n in range(4)))
        k.meet()
        for b in range(B):
            m = k.mm((), k.bank(b), k.rout2[:, :], rem[0:64, b, 0:S], signal=True)
            v = k.stt([m], gr[:, b, 0:S], gr[:, b, 0:S], 1.0, k.bank(b), ALU.add, ALU.mult)
            m = k.mm([v], k.bank(2 + b), k.wout2[:, :], gr[:, b, 0:S], signal=True)
            k.copy([m], k.sT[:, b * S:(b + 1) * S], k.bank(2 + b), k.A)

    ORDER2 = "fbFB"
    def l2_tile_front(self, b, i, m, free):
        k, W, t = self, 32, self.lanes2[b]
        mask = k.mask2_rest if i else k.mask2_first
        sc, qx = k.bank(4 * b, 2), t["qx"][:, i % 2]
        q = k.tt([free.get("gate"), ASIDE], qx, k.wide[0][:, b, i * P:(i + 1) * P]
                 .rearrange("p (j q) -> p j q", j=4).unsqueeze(2).broadcast_to([P, 4, 4, W]),
                 k.sel2[:, :, :].unsqueeze(1).broadcast_to([P, 4, 4, W]), ALU.mult)
        m["q"] = q
        yield
        for half in range(2):
            k.mm([free.get("sub")], sc[:, half, :], k.identb[:, :],
                 mask.rearrange("p j t -> p (j t)").unsqueeze(1).broadcast_to([P, 2, 8 * W]),
                 stop=False)
        done = {}
        for g in (0, 2, 1, 3):
            rows = slice(32 * g, 32 * g + 32)
            for j in range(4):
                c = (g % 2 * 4 + j) * 2 * W
                mm = k.mm([q, done.get(g - 1)], sc[:, g // 2, c:c + 2 * W],
                          qx[rows, j, :, :].rearrange("p h q -> p (h q)"),
                          k.kT2[rows, b, i * P + j * W:i * P + (j + 2) * W], start=False, signal=(j == 3))
            done[g] = mm
        yield
        s3 = sc.rearrange("p a (g t) -> p (a g) t", t=2 * W)
        k.reduce([mm, ASIDE], t["mx"][:, :], s3, ALU.max)
        p = t["p"][:, i % 2, :, :]
        d = free["sub"] = k.tt((), p.rearrange("p a (g t) -> p (a g) t", t=2 * W), s3,
                               t["mx"][:, :].unsqueeze(2).broadcast_to([P, 16, 2 * W]),
                               ALU.subtract)
        m["exp"] = k.act([d, ASIDE], p, p, ACT.Exp)

    def l2_tile_back(self, b, i, m, free):
        k, W, t = self, 32, self.lanes2[b]
        bk = [k.bank(4 * b + 2 + j) for j in range(2)]
        c = []
        for gj in range(8):
            mm = k.tr([m["exp"], free.get("oT"), free.get("banks")],
                      bk[gj // 4][:, (gj % 4) * P:(gj % 4 + 1) * P], t["p"][:, i % 2, gj, :],
                      signal=(gj % 4 == 3))
            if gj % 4 == 3:
                c.append(k.copy([mm, ASIDE], t["pt"][:, gj - 3:gj + 1, :], bk[gj // 4],
                                k.V if gj == 7 else k.A))
        yield
        for j in range(4):
            off = 288 + (j % 2) * 8 + j // 2
            mm = k.mm([m["q"], c[0]], bk[0][:, off:off + 7:2],
                      t["qx"][:, i % 2, j, :, :].rearrange("p h q -> p (h q)"), k.glw[:, :],
                      signal=(j == 3))
        ga = k.act([mm, ASIDE], t["gate"][:, :], bk[0][:, 288:304], ACT.Tanh,
                   scale=0.5 * 8 ** 0.5)
        for par, bank in ((1, bk[1]), (0, bk[0])):
            rows = slice(64 * par, 64 * par + 64)
            for gj in range(8):
                g, jp = gj // 2, gj % 2
                mm = k.mm([*c, ga if par == 0 else None], bank[:, gj * 36:gj * 36 + 36],
                          t["pt"][rows, gj, :],
                          k.v2[rows, b, 2 * i + jp, 4 * g:4 * g + 4, :].rearrange("p h c -> p (h c)"),
                          signal=(gj == 7))
            x = k.tt([mm, ASIDE], t["ox"][:, 8 * par:8 * par + 8, :], bank[:, 0:288]
                     .rearrange("p (g c) -> p g c", c=36),
                     k.quad2.rearrange("p h c -> p (h c)").unsqueeze(1).broadcast_to([P, 8, 36]),
                     ALU.mult)
        yield
        k.reduce((), t["os"][:, :, :], t["ox"].rearrange("p g (h c) -> p g c h", c=9), ALU.add)
        k.V.do((), k.nc.vector.reciprocal, t["r"][:, :], t["os"][:, :, 8])
        k.stt([ga], t["r"][:, :], t["gate"][:, :], 1.0, t["r"][:, :], ALU.add, ALU.mult)
        for par in range(2):
            gs = slice(8 * par, 8 * par + 8)
            o = k.tt([ASIDE] if par else (),
                     t["o"].rearrange("p (jp par) g d -> p par g jp d", par=2)[:, par],
                     t["os"][:, gs, 0:8].rearrange("p (g jp) d -> p g jp d", jp=2),
                     t["r"][:, gs].rearrange("p (g jp) -> p g jp", jp=2).unsqueeze(3)
                     .broadcast_to([P, 4, 2, 8]), ALU.mult)
        yield
        for j in range(4):
            mm = k.tr([o], bk[1][0:32, j * P:(j + 1) * P],
                      t["o"][:, j, :, :].rearrange("p g d -> p (g d)"), signal=(j == 3))
        free["banks"] = x
        free["oT"] = k.copy([mm, ASIDE], k.oT2[:, b, :, i * P:(i + 1) * P]
                            .rearrange("p h (j q) -> p h j q", j=4),
                            bk[1][0:32, :].rearrange("p (j h q) -> p h j q", j=4, h=4), k.A)

    def local_attention(self):
        k, W = self, 32
        k.meet()
        xv = k.scratch[:, 1:3, :, :].rearrange("p i b s -> p (i b s)")[:, 0:B * 1024]
        for b in range(B):
            n = k.nT2[:, b, 0:1]
            x = k.copy((), xv[:, b * 1024:(b + 1) * 1024].rearrange("p (j t) -> p j t", t=2 * W),
                       view(n, [[W, 4 * TPB], [1, 2 * W]]), (k.V, k.A)[b])
            m = k.mm((), k.bank(4 * b), k.wqkv2[:, 1, :], k.nT2[:, b, W:W + S], signal=True)
            k.copy([m], k.kT2[:, b, W:W + S], k.bank(4 * b), k.A)
            for j in range(2 * TPB):
                c = b * 1024 + j * P
                bank = k.bank(4 * b + 2 + j // 4)
                m = k.mm([x], bank[:, (j % 4) * P:(j % 4 + 1) * P], xv[:, c:c + P],
                         k.wqkv2[:, 2, :], signal=(j % 4 == 3))
                if j % 4 == 3:
                    k.copy([m], k.v2[:, b, j - 3:j + 1, :, 0:8],
                           bank.rearrange("p (w h d) -> p w h d", w=4, d=8), (k.V, k.A)[b])
        k.meet()

        pipeline(k.ORDER2, TPB, k.l2_tile_front, k.l2_tile_back)
        for b in range(B):
            for h in range(4):
                m = k.mm([k.A.done.mark(), k.V.done.mark()], k.bank(b), k.wout2_hp[:, h, :], k.oT2[:, b, h, :], start=(h == 0),
                         stop=(h == 3), signal=(h == 3))
            dst = k.sT[:, b * S:(b + 1) * S]
            k.tt([m], dst, dst, k.bank(b), ALU.add)

    def magnitude(self):
        k = self
        for t in range(NT):
            m = k.mm([k.V.done.mark()], k.bank(t // 2)[:, (t % 2) * 256:(t % 2 + 1) * 256],
                     k.nT2[:, t // 4, 32 + (t % 4) * P:32 + (t % 4 + 1) * P],
                     k.trig.rearrange("p i o -> p (i o)"), signal=(t == NT - 1))
        sq = k.wide_pair(0)
        flat = sq.rearrange("p a n -> p (a n)")
        k.act([m], flat, k.bank(0, 4).rearrange("p a n -> p (a n)"), ACT.Square)
        s4 = flat.rearrange("p (t i d) -> p t i d", t=NT, i=2)
        v = k.tt([k.A.done.mark()], k.moe[:, :, :], s4[:, :, 0, :], s4[:, :, 1, :], ALU.add)
        k.act([v], k.moe[:, :, :], k.moe[:, :, :], ACT.Sqrt)

    def layer2(self):
        k = self
        k.open_layer(k.nT2, 32)
        k.latent_attention()
        k.local_attention()
        k.magnitude()
        k.meet()
        for t in range(NT):
            m = k.tr((), k.bank(t // 4)[:, (t % 4) * P:(t % 4 + 1) * P], k.sT[:, t * P:(t + 1) * P],
                     signal=(t == NT - 1))
        k.close_R(k.bank(0, 2).rearrange("p a (t d) -> p (a t) d", d=D), k.moe[:, :, :])

    HEADS, DH = 16, 64

    def layer3_prepare(self):
        k, io, nc = self, self.io, self.nc
        H = k.HEADS
        c = Counter(self.prog, "load_l3", 16)

        k.gam, k.bet = k.sb("gam", [P, D]), k.sb("bet", [P, D])
        k.load(c, k.gam[:, :], io["L3_g"].partition_broadcast(P))
        k.load(c, k.bet[:, :], io["L3_b"].partition_broadcast(P))
        k.mscale = k.sb("mscale", [P, 1])
        k.load(c, k.mscale[:, :], io["L3_scale"].partition_broadcast(P))
        k.mu3 = k.sb("mu3", [D, 256])
        k.load(c, k.mu3[:, :], io["L3_mu"].rearrange("d e s -> d (e s)"))
        k.w1s, k.w2s = k.sb("w1s", [D, H, 32]), k.sb("w2s", [32, H, D])
        k.load(c, k.w1s[:, :, :], io["L3_w1"].rearrange("e d h -> d e h"), eng=k.A)
        k.load(c, k.w2s[:, :, :], io["L3_w2"].rearrange("e h d -> h e d"), eng=k.A)
        k.b1s, k.b2s = k.sb("b1s", [32, H]), k.sb("b2s", [D, H])
        k.load(c, k.b1s[:, :], io["L3_b1T"])
        k.load(c, k.b2s[:, :], io["L3_b2T"])
        par = k.sb("par", [H, 6])
        k.load(c, par[:, :], io["L3_par"])
        om = k.scratch[:, 0, 0, 0:512]
        k.load(c, om, io["L3_omega"].rearrange("h d -> (h d)").partition_broadcast(P))
        k.meet()
        sq, nrm = k.scratch[:, 1, 0, 0:256], k.scratch[:, 2, 0, 0:256]
        v = k.tt((), sq, k.mu3[:, :], k.mu3[:, :], ALU.mult)
        m = k.mm([v], k.bank(0)[:, 0:256], k.ones[:, :], sq, signal=True)
        v = k.ts([m], nrm, k.bank(0)[:, 0:256], 1e-24, None, ALU.max)
        a = k.act([v], nrm, nrm, ACT.Sqrt)
        k.V.do([a], nc.vector.reciprocal, nrm, nrm)
        k.tt((), k.mu3[:, :], k.mu3[:, :], nrm, ALU.mult)

        k.cosT = k.sb("cosT", [P, TPB, H, 32])
        k.sinT = k.sb("sinT", [P, TPB, H, 3, 32])
        tok = k.sb("tok", [P, TPB])
        g = k.G.do((), nc.gpsimd.iota, tok[:, :], pattern=[[P, TPB]], base=0, channel_multiplier=1,
                   allow_small_or_imprecise_dtypes=True)
        ang, turns = k.scratch[:, 1, 0, 0:512], k.scratch[:, 2, 0, 0:512]
        s, co = k.scratch[:, 3, 0, 0:512], k.scratch[:, 4, 0, 0:512]
        for t in range(TPB):
            k.ts([g], ang, om, tok[:, t:t + 1])
            k.sincos(ang, s, co, turns)
            k.copy((), k.cosT[:, t, :, :], co.rearrange("p (h d) -> p h d", d=32))
            s3 = s.rearrange("p (h d) -> p h d", d=32)
            for i, f in enumerate((1.0, -1.0, 1.0)):
                last = k.ts([k.A.done.mark()], k.sinT[:, t, :, i, :], s3, f)
            k.A.wait(last)

        k.coef = k.sb("coef", [P, H])
        layer = k.scope
        with ExitStack() as k.scope:
            k.head_tables(par)
        k.scope = layer
        k.ident_b0 = k.sb("zero", [P, 512], BF16)
        k.fill(k.ident_b0[:, :], 0.0)
        k.backwards = k.sb("backwards", [P, P])
        k.fill(k.backwards[:, :], 0.0)
        k.keep_where(k.backwards[:, :], ALU.not_equal, 1.0, 1 - P, [[1, P]], 1)
        k.nT3 = k.sb("nT3", [D, B, S])
        k.slotT = k.sb("slotT", [D, B, 256])
        k.hs = k.sb("hs", [32, H, 32])
        k.so = k.sb("so", [P, B, 2, D])
        k.small3 = [k.sb(f"small3_{i}", [P, NT, 16]) for i in range(3)]
        k.one3 = [k.sb(f"one3_{i}", [P, NT]) for i in range(3)]
        sizes = dict(qkv=2 * 1536, a=1024, b=1024, sq=1024, qT=512, kT=512, y=1280, pt=1280)
        spare = dict(a=k.aT[:, :], kT=k.sT[:, 0:512], qT=k.sT[:, 512:1024])
        other = k.sb("lane3", [P, sum(w for n, w in sizes.items() if n not in spare)])
        flat = k.scratch.rearrange("p i b s -> p (i b s)")
        k.lanes3 = []
        for b, mem in enumerate((flat, other)):
            t, at = {}, 0
            for n, w in sizes.items():
                if b == 1 and n in spare:
                    t[n] = spare[n]
                    continue
                t[n] = mem[:, at:at + w]
                at += w
            t["qkv"] = (t["qkv"][:, 0:1536], t["qkv"][:, 1536:3072])
            t["ek"] = bass.AP(tensor=t["b"].tensor, offset=t["b"].offset,
                              ap=[list(t["b"].ap[0]), [1, 1280]])
            t["nn"], t["qn"] = k.sb(f"nn3_{b}", [P, 2, 4, 2]), k.sb(f"qn3_{b}", [P, 2, 4])
            for n in ("mx", "sum"):
                t[n] = k.sb(f"{n}3_{b}", [P, 4])
            k.lanes3.append(t)
        k.head = [dict(w=k.sb(f"w3_{j}", [D, 3, P]), et=k.sb(f"et3_{j}", [P, 512]),
                       tb=k.sb(f"tb3_{j}", [P, 3, 512]),
                       front=k.lasting_counter(f"front{j}"), back=k.lasting_counter(f"back{j}"))
                  for j in range(2)]
        for j in range(2):
            k.load_front(j, j)
            k.load_back(j, j)

    def lasting_counter(self, name):
        c = Counter(self.prog, name, 16)
        self.prog.counters.remove(c)
        return c

    def head_tables(self, par):
        k, nc, H, X = self, self.nc, self.HEADS, 640
        a, e, v, w = (k.sb(f"ht{i}", [H, X]) for i in range(4))
        ar, er, vr, wr = (t[:, :] for t in (a, e, v, w))
        sp = k.sb("sp", [H, 4])
        u, o = k.sb("spu", [H, 4]), k.sb("spo", [H, 4])
        hp = k.sb("hp", [H, 8])
        mu, vs, nu, coef, icoef, rvn, half, tmp = (hp[:, i:i + 1] for i in range(8))
        raw = par[:, 1:5]
        q = k.stt((), u[:, :], raw, -1.0, raw, ALU.mult, ALU.max)
        q = k.act([q], u[:, :], u[:, :], ACT.Exp, scale=-1.0)
        k.ts([q], o[:, :], u[:, :], 1.0, None, ALU.add)
        q = k.act([k.V.done.mark()], sp[:, :], o[:, :], ACT.Ln)
        k.ts([q], o[:, :], o[:, :], 1.0, None, ALU.subtract)
        z = k.sb("spz", [H, 4])
        k.ts((), z[:, :], o[:, :], 0.0, None, ALU.is_equal)
        k.tt((), sp[:, :], sp[:, :], z[:, :], ALU.add)
        k.tt((), o[:, :], o[:, :], z[:, :], ALU.add)
        k.V.do((), nc.vector.reciprocal, o[:, :], o[:, :])
        k.tt((), sp[:, :], sp[:, :], o[:, :], ALU.mult)
        k.tt((), sp[:, :], sp[:, :], u[:, :], ALU.mult)
        q = k.stt((), sp[:, :], raw, 0.0, sp[:, :], ALU.max, ALU.add)
        q = k.act([q], mu, par[:, 0:1], ACT.Exp, scale=-1.0)
        k.ts([q], mu, mu, 1.0, None, ALU.add)
        k.V.do((), nc.vector.reciprocal, mu, mu)
        k.ts((), mu, mu, 1e-4, None, ALU.add)
        k.ts((), tmp, mu, 2.0)
        k.V.do((), nc.vector.reciprocal, tmp, tmp)
        k.tt((), vs, sp[:, 0:1], tmp, ALU.mult)
        k.tt((), half, sp[:, 1:2], sp[:, 2:3], ALU.add)
        k.copy((), nu, sp[:, 3:4])
        k.ts((), coef, nu, float(k.DH), -0.5, ALU.add, ALU.mult)
        k.tt((), coef, coef, par[:, 5:6], ALU.mult)
        k.stt((), tmp, coef, -1.0, coef, ALU.mult, ALU.max)
        k.ts((), tmp, tmp, 1e-8, None, ALU.is_lt)
        k.stt((), icoef, tmp, -1.0, coef, ALU.mult, ALU.mult)
        k.tt((), coef, coef, icoef, ALU.add)
        k.stt((), coef, tmp, 1e-8, coef, ALU.mult, ALU.add)
        k.V.do((), nc.vector.reciprocal, icoef, coef)
        q = k.G.do((), nc.gpsimd.iota, ar, pattern=[[-1, X]], base=512, channel_multiplier=0,
                   allow_small_or_imprecise_dtypes=True)
        q = k.stt([q], vr, ar, -1.0, ar, ALU.mult, ALU.max)
        k.ts([q], vr, vr, mu, -1.0, ALU.mult, ALU.mult)
        k.ts((), vr, vr, -30.0, None, ALU.max)
        future = k.sb("future", [H, X])
        k.ts((), future[:, :], ar, 0.0, -1e28, ALU.is_lt, ALU.mult)
        q = k.act([k.V.done.mark()], er, vr, ACT.Exp)
        k.ts([q], wr, vr, 1 / 8, 1.0, ALU.mult, ALU.add)
        for n in range(7, 1, -1):
            k.tt((), wr, wr, vr, ALU.mult)
            k.ts((), wr, wr, 1 / n, 1.0, ALU.mult, ALU.add)
        k.tt((), wr, wr, vr, ALU.mult)
        near = ar
        k.ts((), near, vr, -0.25, None, ALU.is_gt)
        k.ts((), vr, er, 1.0, None, ALU.subtract)
        k.tt((), wr, wr, vr, ALU.subtract)
        k.tt((), wr, wr, near, ALU.mult)
        k.tt((), er, er, wr, ALU.add)
        k.tt((), wr, wr, vr, ALU.add)
        k.stt((), vr, wr, 2.0, wr, ALU.add, ALU.mult)
        k.ts((), vr, vr, -1.0)
        k.ts((), vr, vr, vs, half, ALU.mult, ALU.add)
        k.V.do((), nc.vector.reciprocal, wr, er)
        k.ts((), ar, vr, nu)
        k.V.do((), nc.vector.reciprocal, ar, ar)
        k.tt((), ar, ar, er, ALU.mult)
        q = k.act([k.V.done.mark()], vr, vr, ACT.Ln)
        k.stt([q], vr, vr, -0.5 * k.DH, future[:, :], ALU.mult, ALU.add)
        k.ts((), vr, vr, icoef)
        q = k.V.done.mark()
        rows = nc.dram_tensor("head_rows", (H + 2, 4, X), F32).ap()
        cf = nc.dram_tensor("head_coef", (1, H + 2), F32).ap()
        k.c_rows = Counter(k.prog, "store_rows", 16)
        for i, t in enumerate((w, a, v, e)):
            k.load(k.c_rows, rows[0:H, i, :], t[:, :], need=[q])
            k.load(k.c_rows, rows[H:H + 2, i, :], t[0:2, :])
        k.load(k.c_rows, cf[0, 0:H], coef)
        k.load(k.c_rows, cf[0, H:H + 2], hp[0:2, 3:4])
        k.meet()
        k.rows = rows
        k.wvo = nc.dram_tensor("head_wvo", (H + 2, D, D), F32).ap()
        wv, wo, wvo = (k.scratch.rearrange("p i b s -> p (i b s)")[:, i * 2048:(i + 1) * 2048]
                       .rearrange("p (h c) -> p h c", c=D) for i in range(3))
        c = Counter(k.prog, "load_wvo", 16)
        c_out = Counter(k.prog, "store_wvo", 16)
        k.load(c, wv, k.io["L3_WvT"].rearrange("h r d -> r h d"))
        k.load(c, wo, k.io["L3_Wo"].rearrange("h r d -> r h d"), eng=k.A)
        for h in range(H):
            m = k.mm([c.mark()], k.bank(h // 4)[:, (h % 4) * P:(h % 4 + 1) * P], wv[:, h, :],
                     wo[:, h, :], signal=(h % 4 == 3))
        a = k.copy([m], wvo, k.bank(0, 4).rearrange("p a (t c) -> p (a t) c", c=D), k.A)
        k.load(c_out, k.wvo[0:H].rearrange("h d c -> d h c"), wvo, need=[a])
        k.load(c_out, k.wvo[H:H + 2].rearrange("h d c -> d h c"), wvo[:, 0:2, :])
        c = Counter(k.prog, "load_coef", 16)
        k.load(c, k.coef[:, :], cf[0, 0:H].partition_broadcast(P))
        k.meet()

    FRONT_LOADS, BACK_LOADS = 3, 1

    def spread(self, h, first, n):
        row = self.rows[bass.ds(h, 1), first, 1:2]
        return bass.AP(tensor=row.tensor, offset=row.offset, ap=[[1, P], [640, n], [1, 512]])

    def load_front(self, j, h):
        k, t = self, self.head[j]
        k.load(t["front"], t["w"][:, 0:2, :], k.io["L3_Wqk"][bass.ds(h, 1)]
               .rearrange("a d i c -> d (a i) c"))
        k.load(t["front"], t["w"][:, 2:3, :], k.wvo[bass.ds(h, 1)].rearrange("a d c -> d a c"))
        k.load(t["front"], t["et"][:, :], k.spread(h, 3, 1))

    def load_back(self, j, h):
        k, t = self, self.head[j]
        k.load(t["back"], t["tb"][:, :, :], k.spread(h, 0, 3))

    def soft_mixture(self):
        k, H = self, self.HEADS
        xn = k.normed
        k.normalize((), k.n, xn)
        g8 = [P, NT, D]
        k.tt((), xn[:, :, :], xn[:, :, :], k.gam[:, :].unsqueeze(1).broadcast_to(g8), ALU.mult)
        v = k.tt((), xn[:, :, :], xn[:, :, :], k.bet[:, :].unsqueeze(1).broadcast_to(g8), ALU.add)
        ss, r, tot = (t[:, :] for t in k.one3)
        xu = k.moe
        a = k.act([v], xu[:, :, :], xn[:, :, :], ACT.Square)
        v = k.reduce([a], ss, xu[:, :, :], ALU.add)
        k.ts([v], r, ss, 1e-24, None, ALU.max, eng=k.G)
        k.tt((), r, r, k.minus_half[:, 0:NT], ALU.pow, eng=k.G)
        q = k.ts((), r, r, k.mscale[:, 0:1], eng=k.G)
        for t in range(NT):
            v = k.ts([q], xu[:, t, :], xn[:, t, :], r[:, t:t + 1])
        xuT = k.hT
        for t in range(NT):
            m = k.tr([v], k.bank(6 + t // 4)[:, (t % 4) * P:(t % 4 + 1) * P], xu[:, t, :],
                     signal=(t % 4 == 3))
            if t % 4 == 3:
                a = k.copy([m], xuT[:, (t // 4) * S:(t // 4 + 1) * S], k.bank(6 + t // 4), k.A)
        for t in range(NT):
            m = k.mm([a], k.bank(t // 2)[:, (t % 2) * 256:(t % 2 + 1) * 256],
                     xuT[:, t * P:(t + 1) * P], k.mu3[:, :], signal=(t == NT - 1))
        combine, dsp, dspT, cT = (k.wide_pair(2 * i) for i in range(4))
        cmb = combine.rearrange("p a (t c) -> p (a t) c", c=256)
        lg = k.bank(0, 4).rearrange("p a (t c) -> p (a t) c", t=2)
        v = k.reduce([m], ss, lg, ALU.max)
        v = k.ts((), ss, ss, -1.0)
        for t in range(NT):
            c = k.act([v], cmb[:, t, :], lg[:, t, :], ACT.Exp, bias=ss[:, t:t + 1],
                      accum_out=tot[:, t:t + 1])
        v = k.V.do([c], k.nc.vector.reciprocal, tot, tot)
        for t in range(NT):
            v = k.ts((), cmb[:, t, :], cmb[:, t, :], tot[:, t:t + 1])
        for h in range(2):
            for b in range(B):
                m = k.mm([a, k.A.done.mark()], k.bank(4 + 2 * h + b),
                         k.mu3[:, h * P:(h + 1) * P], xuT[:, b * S:(b + 1) * S], signal=True)
        smx, ssum = (t[:, 0, 0:4] for t in k.small3[0:2])
        k.reduce([m], smx, k.bank(4, 4), ALU.max)
        v = k.ts((), smx, smx, -1.0)
        for h in range(2):
            for b in range(B):
                i = 2 * h + b
                w = k.act([v], dspT[:, h, b * S:(b + 1) * S], k.bank(4 + i), ACT.Exp,
                          bias=smx[:, i:i + 1], accum_out=ssum[:, i:i + 1])
        k.V.do([w], k.nc.vector.reciprocal, ssum, ssum)
        for h in range(2):
            for b in range(B):
                i = 2 * h + b
                v = k.ts((), dspT[:, h, b * S:(b + 1) * S], dspT[:, h, b * S:(b + 1) * S],
                         ssum[:, i:i + 1])
        dsp = dsp.rearrange("p a (t c) -> p (a t) c", c=256)
        d = [k.A.done.mark(), v]
        for t in range(NT):
            bank = k.bank(t // 2)
            for h in range(2):
                m = k.tr(d, bank[:, (t % 2) * 256 + h * P:(t % 2) * 256 + (h + 1) * P],
                         dspT[:, h, t * P:(t + 1) * P], signal=(h == 1 and t % 2 == 1))
            if t % 2:
                v = k.copy([m], dsp[:, t - 1:t + 1, :].rearrange("p t c -> p (t c)"), bank,
                           k.A if t // 2 % 2 else k.V)
        for b in range(B):
            for t in range(TPB):
                m = k.mm([k.V.done.mark(), k.A.done.mark()], k.bank(4)[:, b * 256:(b + 1) * 256],
                         xn[:, b * TPB + t, :], dsp[:, b * TPB + t, :], start=(t == 0), stop=(t == TPB - 1),
                         signal=(t == TPB - 1))
        a = k.copy([m], k.slotT.rearrange("p b s -> p (b s)"), k.bank(4), k.A)
        for e in range(H):
            m = k.mm([a], k.bank(5)[0:32, e * 32:(e + 1) * 32], k.w1s[:, e, :],
                     k.slotT[:, :, e * 16:(e + 1) * 16], signal=(e == H - 1))
        v = k.tt([m], k.hs[:, :, :], k.bank(5)[0:32, :].rearrange("p (e c) -> p e c", c=32),
                 k.b1s[:, :].unsqueeze(2).broadcast_to([32, H, 32]), ALU.add)
        a = k.act([v], k.hs[:, :, :], k.hs[:, :, :], ACT.Gelu)
        for e in range(H):
            m = k.mm([a], k.bank(4)[:, e * 32:(e + 1) * 32], k.w2s[:, e, :], k.hs[:, e, :],
                     signal=(e == H - 1))
        for b in range(B):
            v = k.tt([m], k.slotT[:, b, :].rearrange("p (e s) -> p e s", s=16),
                     k.bank(4).rearrange("p (e b s) -> p b e s", b=B, s=16)[:, b],
                     k.b2s[:, :].unsqueeze(2).broadcast_to([D, H, 16]), ALU.add)
        for b in range(B):
            for h in range(2):
                m = k.tr([v], k.bank(5)[:, (2 * b + h) * P:(2 * b + h + 1) * P],
                         k.slotT[:, b, h * P:(h + 1) * P], signal=(b == 1 and h == 1))
        a = k.copy([m], k.so.rearrange("p b h d -> p (b h d)"), k.bank(5), k.A)
        for h in range(2):
            for t in range(NT):
                m = k.tr([v], k.bank(2 * h + t // 4)[:, (t % 4) * P:(t % 4 + 1) * P],
                         cmb[:, t, h * P:(h + 1) * P], signal=(t % 4 == 3))
                if t % 4 == 3:
                    w = k.copy([m], cT[:, h, (t // 4) * S:(t // 4 + 1) * S], k.bank(2 * h + t // 4),
                               k.A if t // 4 else k.V)
        for t in range(NT):
            for h in range(2):
                m = k.mm([a, w, k.A.done.mark(), k.V.done.mark()],
                         k.bank(6 + t // 4)[:, (t % 4) * P:(t % 4 + 1) * P],
                         cT[:, h, t * P:(t + 1) * P], k.so[:, t // 4, h, :], start=(h == 0),
                         stop=(h == 1), signal=(t == NT - 1 and h == 1))
        k.copy([m], k.moe.rearrange("p (a t) d -> p a (t d)", a=2), k.bank(6, 2), k.A)

    def head_front(self, b, u, h, m, free):
        k, t, hd = self, self.lanes3[b], self.head[u % 2]
        bank = k.bank(4 * b)
        for e in (k.T, k.V):
            e.e.wait_ge(hd["front"].sem, 16 * k.FRONT_LOADS * (1 + u // 2))
        w, et = hd["w"].rearrange("d i c -> d (i c)"), hd["et"]
        v4 = t["qkv"][u % 2].rearrange("p (t c) -> p t c", t=4)
        own = free.get("banks_f", ())
        for i in range(4):
            mm = k.mm(own, bank[:, 0:384], k.nT3[:, b, i * P:(i + 1) * P], w, signal=True)
            own = [k.copy([mm, ASIDE], v4[:, i, :], bank[:, 0:384], k.A)]
            yield
        m["v"] = own
        a4, b4 = (t[n].rearrange("p (t c) -> p t c", t=4) for n in "ab")
        cs = k.cosT[:, :, bass.ds(h, 1), :].rearrange("p t a d -> p t (a d)")
        v = k.tt([*own, ASIDE], a4.rearrange("p t (r d) -> p t r d", d=32),
                 v4[:, :, 0:256].rearrange("p t (r d) -> p t r d", d=32),
                 cs.unsqueeze(2).broadcast_to([P, 4, 8, 32]), ALU.mult, k.G)
        sn = k.sinT[:, :, bass.ds(h, 1), :, :].rearrange("p t a i d -> p t (a i d)")
        q4 = v4[:, :, 0:256].rearrange("p t (i c) -> p t i c", i=2)
        r4 = t["b"].rearrange("p (t i c) -> p t i c", t=4, i=2)
        both = [P, 4, 2, 64]
        k.tt([*own, free.get("ek"), ASIDE], r4[:, :, :, 0:64], q4[:, :, :, 64:128],
             sn[:, :, 32:96].unsqueeze(2).broadcast_to(both), ALU.mult)
        v = k.tt([ASIDE], r4[:, :, :, 64:128], q4[:, :, :, 0:64],
                 sn[:, :, 0:64].unsqueeze(2).broadcast_to(both), ALU.mult)
        r = k.tt([v], t["a"], t["a"], t["b"], ALU.add, k.G)
        for i in range(4):
            for c in range(2):
                nn = k.act([*own, free.get("ek"), ASIDE], t["sq"][:, (2 * i + c) * P:(2 * i + c + 1) * P],
                           v4[:, i, c * P:(c + 1) * P], ACT.Square,
                           accum_out=t["nn"][:, u % 2, i, c:c + 1])
        yield
        mm = k.mm([nn], bank[:, 0:4], k.backwards[:, :], t["nn"][:, u % 2, :, 0], signal=True)
        qn = k.copy([mm, ASIDE], t["qn"][:, u % 2, :], bank[:, 0:4], k.A)
        for jj in range(4):
            m["ek"] = k.ts([nn, r, ASIDE],
                           t["ek"][:, k.AT_KEY[jj]:k.AT_KEY[jj + 1]], et[:, jj * P:512],
                           t["nn"][:, u % 2, jj, 1:2])
        yield
        qk = []
        need = [r, qn]
        for i, (n, f) in enumerate((("qT", -2.0), ("kT", 1.0))):
            for tt in range(4):
                mm = k.tr(need, bank[:, tt * P:(tt + 1) * P], a4[:, tt, i * P:(i + 1) * P],
                          signal=(tt == 3))
            out = t[n].rearrange("p (t c) -> p t c", t=4)
            if n == "qT":
                out = view(out[:, 0, P - 1:P], [[P, 4], [-1, P]])
            need = [k.act([mm, free.get("qk"), ASIDE], out,
                          bank.rearrange("p (t c) -> p t c", t=4), ACT.Identity, scale=f)]
            qk += need
            if i == 0:
                yield
        m["qk"] = qk
        m["qn"] = qn
        free["banks_f"] = need

    AT_QUERY = [0, 128, 384, 768, 1280]
    AT_KEY = [0, 512, 896, 1152, 1280]

    def head_back(self, b, u, m, free):
        k, t, hd, nc = self, self.lanes3[b], self.head[u % 2], self.nc
        bk = [k.bank(4 * b + 1 + i) for i in range(3)]
        at, pat, tb = k.AT_QUERY, k.AT_KEY, hd["tb"]
        v4 = t["qkv"][u % 2].rearrange("p (t c) -> p t c", t=4)
        k.V.e.wait_ge(hd["back"].sem, 16 * k.BACK_LOADS * (1 + u // 2))
        qn = m["qn"]
        need = [*m["qk"], m["ek"]]
        scored, ln, exp, flipped = {}, {}, {}, {}

        def y_of(i):
            return t["y"][:, at[i]:at[i + 1]]

        def cols(i):
            return slice(384 - i * P, 512)

        def scores(i):
            y, wd = y_of(i), (i + 1) * P
            ps = bk[i % 2][:, 0:wd]
            k.mm([*need, free.get(f"scores{i % 2}")], ps, t["qT"][:, i * P:(i + 1) * P],
                 t["kT"][:, 0:wd], stop=False)
            for jj in range(i + 1):
                c = pat[jj] + (3 - i) * P
                mm = k.tr((), ps[:, jj * P:(jj + 1) * P], t["ek"][:, c:c + P], start=False,
                          signal=(jj == i))
            free[f"scores{i % 2}"] = k.stt([mm, qn, free.get(f"y{i}"), ASIDE], y,
                                           tb[:, 0, cols(i)], t["qn"][:, u % 2, i:i + 1], ps,
                                           ALU.mult, ALU.add)
            v = k.stt((), y, y, 0.0, tb[:, 1, cols(i)], ALU.max, ALU.mult)
            ln[i] = k.act([v, ASIDE], y, y, ACT.Ln, bias=1.0)
            free["ek"] = free["qk"] = mm

        def softmax(i):
            y, mx = y_of(i), t["mx"][:, i:i + 1]
            k.V.do([ln[i], ASIDE], nc.vector.tensor_tensor_reduce, y, y, tb[:, 2, cols(i)],
                   k.coef_u[:, u:u + 1], -3e38, ALU.add, ALU.max, mx)
            v = k.ts((), mx, mx, -1.0)
            exp[i] = k.act([v, ASIDE], y, y, ACT.Exp, bias=mx, accum_out=t["sum"][:, i:i + 1])

        def flip(i):
            for jj in range(i + 1):
                mm = k.tr([exp[i], free.get("flip")], bk[2][:, jj * P:(jj + 1) * P],
                          y_of(i)[:, jj * P:(jj + 1) * P], signal=(jj == i))
            free[f"y{i}"] = mm
            flipped[i] = k.copy([mm, free.get(f"pt{i}"), ASIDE], t["pt"][:, at[i]:at[i + 1]],
                                bk[2][:, 0:(i + 1) * P], k.A if i != 2 else k.V)
            k.V.do([exp[i], ASIDE], nc.vector.reciprocal, t["sum"][:, i:i + 1],
                   t["sum"][:, i:i + 1])

        def values(i):
            for jj in range(i + 1):
                c = at[i] + jj * P
                mm = k.mm([flipped[i], *m["v"]], bk[2][:, 0:P], t["pt"][:, c:c + P],
                          v4[:, jj, 256:384], start=(jj == 0), stop=(jj == i), signal=(jj == i))
            free[f"pt{i}"] = mm
            n = k.n[:, b * TPB + i, :]
            free["flip"] = k.stt([mm], n, bk[2][:, 0:P], t["sum"][:, i:i + 1], n, ALU.mult,
                                 ALU.add)

        steps = ((0, scores), (3, values), (2, flip), (1, softmax))
        for slot in range(4 + 3):
            for behind, step in steps:
                if 0 <= slot - behind < 4:
                    step(3 - (slot - behind))
            if slot < 6:
                yield
        m["done"] = [k.T.done.mark(), k.V.done.mark()]

    ORDER3 = "bfBF"
    ROUND = 4

    def attention(self):
        k = self
        k.coef_u = k.small3[0][:, 0, 0:k.ROUND]
        k.meet()
        k.A.do((), k.nc.scalar.preload_act_table_set, "natural_log_exp_and_others")
        k.fill(k.n[:, :, :], 0.0)

        def body(i):
            first = i * k.ROUND
            k.copy((), k.coef_u, k.coef[:, bass.ds(first, k.ROUND)])

            def passed(kind, u, marks):
                for m in marks:
                    k.Y.wait(*((*m["qk"], m["ek"]) if kind == "front" else m["done"]))
                if u >= k.ROUND - 2:
                    k.Y.e.sem_clear(k.head[u % 2][kind].sem)
                (k.load_front if kind == "front" else k.load_back)(u % 2, first + u + 2)

            pipeline(k.ORDER3, k.ROUND,
                     lambda b, u, m, free: k.head_front(b, u, first + u, m, free),
                     k.head_back, passed, lead=4, first_stages=4, offset=0)

        k.prog.loop_over("heads", k.HEADS // k.ROUND, body)
        for b in range(B):
            for i in range(4):
                k.mm((), k.bank(6 + b)[:, i * P:(i + 1) * P], k.backwards[:, :],
                     k.n[:, b * TPB + i, :], signal=(i == 3))

    def layer3(self):
        k = self
        k.open_layer(k.nT3, 0)
        k.soft_mixture()
        k.attention()
        k.close_R(k.bank(6, 2).rearrange("p a (t d) -> p (a t) d", d=D), k.moe[:, :, :])

    def run(self, layers):
        k, p = self, self.prog
        with ExitStack() as k.scope:
            k.constants()
            k.norm_scratch()
            k.xs = k.sb("xs", [P, SEQS * TPB, D])
            load_x, store_x = Counter(p, "load_x", 16), Counter(p, "store_x", 16)
            for b in range(SEQS):
                k.load(load_x, k.xs[:, b * TPB:(b + 1) * TPB, :],
                       k.io["x"][b].rearrange("(t p) d -> p t d", p=P))
            k.x, k.n, k.sR, k.moe = (k.sb(n, [P, NT, D]) for n in ("x", "n", "sR", "moe"))
            k.sT, k.hT, k.aT = (k.sb(n, [D, N]) for n in ("sT", "hT", "aT"))
            k.scratch = k.sb("scratch", [D, 11, B, 1 + S])
            k.wide = [k.scratch[:, i, :, :] for i in range(11)]
            whole = k.scope
            for i in range(layers):
                with ExitStack() as k.scope:
                    prepare, layer = ((k.layer0_prepare, k.layer0), (k.layer1_prepare, k.layer1),
                                      (k.layer2_prepare, k.layer2), (k.layer3_prepare, k.layer3))[i]
                    prepare()

                    def chunk(c):
                        k.chunk = c
                        k.copy((), k.x[:, :, :], k.xs[:, bass.ds(c * NT, NT), :], k.A)
                        k.meet()
                        layer()

                    p.loop_over(f"layer{i}", CHUNKS, chunk)
                    if i == 3:
                        for head in k.head:
                            k.Y.e.wait_ge(head["front"].sem, 16 * k.FRONT_LOADS)
                            k.Y.e.wait_ge(head["back"].sem, 16 * k.BACK_LOADS)
                k.scope = whole
            for b in range(SEQS):
                k.load(store_x, k.io["out"][b].rearrange("(t p) d -> p t d", p=P),
                       k.xs[:, b * TPB:(b + 1) * TPB, :])
            k.Y.wait(store_x.mark())


def build(nc, inputs):
    io = {n: nc.dram_tensor("in_" + n, a.shape, mybir.dt.from_np(a.dtype), kind="ExternalInput").ap()
          for n, a in inputs.items()}
    io["out"] = nc.dram_tensor("out_0", (SEQS, S, D), F32, kind="ExternalOutput").ap()
    k = Kernel(nc, io)
    k.run(LAYERS)


def lay_out_more(a, r, c):
    for i in (1, 3, 2):
        w = np.concatenate([a[f"L1_ffn_w{i}"], a[f"L1_ffn_sw{i}"]])
        r[f"L1_w{i}T"] = w.transpose(0, 2, 1)
    r["L1_routerT"] = a["L1_ffn_router_w"].T
    r["L1_eb"] = a["L1_ffn_expert_bias"]
    for n in ("Wk", "Wv", "Wr", "Wo"):
        r["L1_" + n] = a["L1_attn_" + n]
    for n, m in (("td", "time_decay"), ("tf", "time_first"), ("tmk", "time_mix_key"),
                 ("tmv", "time_mix_value"), ("tmr", "time_mix_receptance")):
        r["L1_" + n] = a["L1_attn_" + m]
    for n in ("wq", "wk", "wv", "wgq", "wgk", "wgv"):
        r["L2_" + n] = a["L2_attn_" + n]
    r["L2_rout"] = a["L2_attn_r_out_w"]
    r["L2_wout"] = a["L2_attn_w_out"]
    r["L2_gl"] = a["L2_attn_gate_local_w"].reshape(-1)
    r["L2_gr"] = a["L2_attn_gate_remote_w"].reshape(-1)
    for n, m in (("theta", "theta"), ("phi", "phi"), ("thetan", "theta_noise"), ("phin", "phi_noise")):
        r["L2_" + n] = a["L2_ffn_" + m]
    w = np.stack([a[f"L3_attn_W{n}"].reshape(D, 2, 16, 64) for n in "qk"])
    w = w.transpose(3, 1, 0, 2, 4).reshape(16, D, 2, P)
    r["L3_Wqk"] = np.concatenate([w, w[:2]])
    r["L3_WvT"] = a["L3_attn_Wv"].reshape(D, 2, 16, 64).transpose(2, 1, 3, 0).reshape(16, P, D)
    r["L3_Wo"] = a["L3_attn_Wo"].reshape(2, 16, 64, D).transpose(1, 0, 2, 3).reshape(16, P, D)
    r["L3_par"] = np.stack([a["L3_attn_" + n] for n in (
        "mu_raw", "sigma_raw", "eta_raw", "gamma_raw", "nu_raw", "tau")], axis=1)
    r["L3_omega"] = a["L3_attn_omega"]
    r["L3_g"], r["L3_b"] = a["L3_ffn_ln_gamma"], a["L3_ffn_ln_beta"]
    r["L3_scale"] = a["L3_ffn_scale"]
    r["L3_mu"], r["L3_w1"], r["L3_w2"] = (a["L3_ffn_" + n] for n in ("mu", "w1", "w2"))
    r["L3_b1T"], r["L3_b2T"] = a["L3_ffn_b1"].T, a["L3_ffn_b2"].T


def lay_out(a):
    c = np.ascontiguousarray
    r = {"x": a["L0_attn_x"]}
    for n in "qkvo":
        r[f"L0_W{n}T"] = c(a[f"L0_attn_W{n}"].T)
        r[f"L0_b{n}"] = a[f"L0_attn_b{n}"]
    r["L0_qT"] = c(a["L0_ffn_qweights"].transpose(0, 2, 1))
    r["L0_scT"] = c(np.repeat(a["L0_ffn_scales"], 16, axis=2).transpose(0, 2, 1))
    r["L0_la"] = a["L0_ffn_lora_a"]
    r["L0_lbT"] = c(a["L0_ffn_lora_b"].transpose(0, 2, 1))
    r["L0_fb"] = a["L0_ffn_biases"]
    r["L0_fbT"] = c(a["L0_ffn_biases"].T)
    r["L0_lngT"] = c(a["L0_ffn_ln_gamma"].T)
    r["L0_lnbT"] = c(a["L0_ffn_ln_beta"].T)
    lay_out_more(a, r, c)
    return {k: c(v) for k, v in r.items()}


def kernel(**inputs):
    import concourse.bacc as bacc
    from concourse.bass_utils import run_bass_kernel_spmd as run

    nc = bacc.Bacc("TRN2", target_bir_lowering=False, num_devices=1)
    arrays = lay_out({k: np.asarray(v) for k, v in inputs.items()})
    build(nc, arrays)
    r = run(nc, [{"in_" + n: v for n, v in arrays.items()}], core_ids=[0])
    return r.results[0]["out_0"]
```

```python
from contextlib import ExitStack

import numpy as np

import concourse.bass as bass
import concourse.mybir as mybir
from concourse.alu_op_type import AluOpType as ALU

F32 = mybir.dt.float32
BF16 = mybir.dt.bfloat16
I32 = mybir.dt.int32
ACT = mybir.ActivationFunctionType
AX = mybir.AxisListType

LAYERS = 4
P = 128
D = 128
SEQS, S = 8, 512
B = 2
CHUNKS = SEQS // B
N = B * S
NT = N // P
TPB = S // P
ASIDE = "aside"
MASKED = -1e30


class Counter:

    def __init__(self, prog, name, step=1):
        self.prog, self.name, self.step, self.count = prog, name, step, 0
        self.sem = prog.nc.alloc_semaphore(name)
        prog.counters.append(self)

    def mark(self):
        return (self, self.prog.era, self.count)

    def next(self):
        self.count += self.step
        return self.mark()


class Program:

    def __init__(self, nc):
        self.nc, self.era, self.counters, self.engines = nc, 0, [], []

    def new_era(self):
        for e in self.engines:
            for c in self.counters:
                e.wait(c.mark())
        self.nc.all_engine_barrier(sem_only=True)
        for c in self.counters:
            if c.count:
                self.engines[0].e.sem_clear(c.sem)
        self.nc.all_engine_barrier(sem_only=True)
        self.era += 1
        for c in self.counters:
            c.count = 0
        for e in self.engines:
            e.waited = {}

    def loop_over(self, name, n, body):
        self.new_era()
        with self.nc.Fori(0, n) as i:
            body(i)
            self.new_era()


class Engine:

    def __init__(self, prog, eng, name, in_order):
        self.prog, self.e, self.in_order = prog, eng, in_order
        self.done = Counter(prog, name)
        self.waited = {}
        prog.engines.append(self)

    def wait(self, *marks):
        for mark in marks:
            if mark is None or mark is ASIDE:
                continue
            counter, era, count = mark
            if era != self.prog.era or count <= self.waited.get(counter, 0):
                continue
            self.e.wait_ge(counter.sem, count)
            self.waited[counter] = count

    def do(self, need, fn, *args, **kw):
        self.wait(*need)
        if self.in_order and ASIDE not in need:
            self.wait(self.done.mark())
        fn(*args, **kw).then_inc(self.done.sem, 1)
        return self.done.next()

    def quiet(self, need, fn, *args, **kw):
        self.wait(*need)
        fn(*args, **kw)


def interleave(*lanes):
    lanes = [iter(x) for x in lanes]
    while lanes:
        for lane in list(lanes):
            try:
                next(lane)
            except StopIteration:
                lanes.remove(lane)


def pipeline(order, units, front, back, passed=None, lead=0, first_stages=1,
             offset=0):
    marks = [[{} for _ in range(units)] for _ in range(B)]
    free = [{} for _ in range(B)]
    through = {"front": [0] * B, "back": [0] * B}
    stage, running = {}, {}

    def may_go(kind, b):
        u, key = through[kind][b], (kind, b)
        if kind == "back":
            return u < through["front"][b]
        if key not in running:
            ahead = passed is not None and u - 2 >= min(through["front"])
            return u < units and u - 1 <= through["back"][b] and not ahead
        return (u == 0 or through["back"][b] == u or stage[key] < first_stages
                or stage.get(("back", b), 0) >= lead)

    while min(through["back"]) < units:
        for c in order:
            kind, b = ("front" if c in "fF" else "back"), int(c in "FB")
            if b and offset > 0:
                offset -= 1
                continue
            if not may_go(kind, b):
                continue
            key, u = (kind, b), through[kind][b]
            if key not in running:
                running[key] = (front if kind == "front" else back)(b, u, marks[b][u], free[b])
                stage[key] = 0
            stage[key] += 1
            if next(running[key], "end") != "end":
                continue
            del running[key], stage[key]
            through[kind][b] += 1
            if passed and min(through[kind]) == u + 1:
                passed(kind, u, [m[u] for m in marks])


def view(ap, dims, offset=0):
    return bass.AP(tensor=ap.tensor, offset=ap.offset + offset, ap=[list(ap.ap[0])] + dims)


class Kernel:
    def __init__(self, nc, io):
        self.nc, self.io = nc, io
        self.prog = Program(nc)
        p = self.prog
        self.T = Engine(p, nc.tensor, "pe", False)
        self.V = Engine(p, nc.vector, "dve", True)
        self.A = Engine(p, nc.scalar, "act", True)
        self.G = Engine(p, nc.gpsimd, "pool", True)
        self.Y = Engine(p, nc.sync, "sp", False)
        self.engines = [self.T, self.V, self.A, self.G, self.Y]
        self.ps = nc.alloc_psum_tensor("banks", [P, 8, 512], F32)

    def sb(self, name, shape, dt=F32):
        return self.scope.enter_context(self.nc.sbuf_tensor(name, shape, dt))

    def wide_pair(self, i):
        w = self.scratch
        a = w[:, i, 0, 0:1]
        return bass.AP(tensor=a.tensor, offset=a.offset,
                       ap=[list(a.ap[0]), [N, 2], [1, N]])

    def bank(self, k, n=1):
        return self.ps[:, k, :] if n == 1 else self.ps[:, k:k + n, :]

    def meet(self):
        for e in self.engines:
            for c in self.prog.counters:
                e.wait(c.mark())

    def load(self, group, out, src, need=(), eng=None):
        e = eng or self.Y
        e.wait(*need)
        e.e.dma_start(out, src).then_inc(group.sem, 16)
        return group.next()

    def mm(self, need, out, lhsT, rhs, start=True, stop=True, signal=False, **kw):
        f = self.T.do if signal else self.T.quiet
        return f(need, self.nc.tensor.matmul, out, lhsT, rhs, start=start, stop=stop,
                 skip_group_check=True, **kw)

    def tr(self, need, out, in_, signal=False, start=True, ident=None):
        k = in_.shape[0]
        f = self.T.do if signal else self.T.quiet
        i = self.ident if ident is None else ident
        return f(need, self.nc.tensor.matmul, out, in_, i[0:k, 0:k], start=start, stop=True,
                 is_transpose=True, skip_group_check=True)

    def act(self, need, out, in_, func, **kw):
        return self.A.do(need, self.nc.scalar.activation, out, in_, func, **kw)

    def tt(self, need, out, a, b, op, eng=None):
        e = eng or self.V
        return e.do(need, e.e.tensor_tensor, out, a, b, op)

    def ts(self, need, out, a, s1, s2=None, op0=ALU.mult, op1=None, eng=None):
        e = eng or self.V
        if op1 is None:
            return e.do(need, e.e.tensor_scalar, out, a, s1, None, op0)
        return e.do(need, e.e.tensor_scalar, out, a, s1, s2, op0, op1)

    def stt(self, need, out, a, s, b, op0, op1):
        return self.V.do(need, self.nc.vector.scalar_tensor_tensor, out, a, s, b, op0, op1)

    def copy(self, need, out, in_, eng=None):
        e = eng or self.V
        if e is self.A:
            return self.act(need, out, in_, ACT.Identity)
        return e.do(need, e.e.tensor_copy, out, in_)

    def reduce(self, need, out, in_, op, axis=AX.X):
        return self.V.do(need, self.nc.vector.tensor_reduce, out, in_, axis, op)

    def fill(self, out, value, eng=None):
        e = eng or self.G
        return e.do((), e.e.memset, out, value)

    def keep_where(self, ap, op, fill, base, pattern, mult):
        return self.G.do((), self.nc.gpsimd.affine_select, out=ap, in_=ap, compare_op=op,
                         fill=fill, base=base, pattern=pattern, channel_multiplier=mult)

    def constants(self):
        self.ident = self.sb("ident", [P, P])
        self.identb = self.sb("identb", [P, P], BF16)
        self.ones = self.sb("ones", [P, P])
        self.minus_half = self.sb("minus_half", [P, 16])
        self.fill(self.ident[:, :], 0.0)
        self.keep_where(self.ident[:, :], ALU.not_equal, 1.0, 0, [[-1, P]], 1)
        self.fill(self.identb[:, :], 0.0)
        self.keep_where(self.identb[:, :], ALU.not_equal, 1.0, 0, [[-1, P]], 1)
        self.fill(self.ones[:, :], 1.0)
        self.fill(self.minus_half[:, :], -0.5)

    def rsqrt(self, need, out, in_, eps):
        n = in_.shape[1]
        self.ts(need, out, in_, eps, None, ALU.add, eng=self.G)
        return self.tt((), out, out, self.minus_half[:, 0:n], ALU.pow, eng=self.G)

    def norm_scratch(self):
        self.bn = self.sb("bn", [P, NT, 6])
        self.mv = self.sb("mv", [P, NT, 2])
        self.rstd = self.sb("rstd", [P, NT])
        self.normed = self.sb("normed", [P, NT, D])

    def normalize(self, need, src, out, tiles=range(NT), eps=1e-5):
        v = self.nc.vector
        for n, t in enumerate(tiles):
            self.V.do([*need, ASIDE if n else None], v.bn_stats, self.bn[:, t, :], src[:, t, :])
        for n, t in enumerate(tiles):
            m = self.V.do([ASIDE if n else None], v.bn_aggr, self.mv[:, t, :], self.bn[:, t, :])
        span = slice(tiles[0], tiles[-1] + 1)
        r = self.rsqrt([m], self.rstd[:, span], self.mv[:, span, 1], eps)
        for t in tiles:
            m = self.ts([r, ASIDE], out[:, t, :], src[:, t, :], self.mv[:, t, 0:1],
                        self.rstd[:, t:t + 1], ALU.subtract, ALU.mult)
        return m


    def window_mask(self, name, w, heads):
        m = self.sb(name, [P, 2 * w], BF16)
        self.fill(m[:, :], 0.0)
        for h in range(heads):
            q = m[h * w:(h + 1) * w, :]
            self.keep_where(q, ALU.is_ge, MASKED, -1, [[1, 2 * w]], -1)
            self.keep_where(q, ALU.is_ge, MASKED, w, [[-1, 2 * w]], 1)
        first = self.sb(name + "_first", [P, 2 * w], BF16)
        self.copy((), first[:, :], m[:, :], self.G)
        self.fill(first[:, 0:w], MASKED)
        return m, first

    def head_select(self, name, q, scale):
        m = self.sb(name, [P, 4, q])
        self.fill(m[:, :, :], scale)
        for g in range(4):
            part = m[32 * g:32 * g + 32, :, :]
            self.keep_where(part, ALU.is_ge, 0.0, 0, [[-8, 4], [0, q]], 1)
            self.keep_where(part, ALU.is_ge, 0.0, 7, [[8, 4], [0, q]], -1)
        return m

    def l0_load(self):
        io = self.io
        self.c_w0 = Counter(self.prog, "load_w0", 16)
        self.w0 = self.sb("w0", [D, 3, D])
        for i, n in enumerate(("WqT", "WkT", "WvT")):
            self.load(self.c_w0, self.w0[:, i, :], io["L0_" + n])
        self.wo0 = self.sb("wo0", [64, 2, D])
        for hp in range(2):
            src = io["L0_WoT"].rearrange("(g hp d) o -> hp g d o", hp=2, d=8)[hp]
            for g in range(8):
                self.load(self.c_w0, self.wo0[8 * g:8 * g + 8, hp, :], src[g], eng=self.A)
        self.b0 = self.sb("b0", [D, 4])
        self.bv0 = self.sb("bv0", [P, D])
        for i, n in enumerate(("bq", "bk", "bo")):
            self.load(self.c_w0, self.b0[:, i:i + 1], io["L0_" + n].rearrange("(a b) -> a b", b=1))
        self.load(self.c_w0, self.bv0[:, :], io["L0_bv"].partition_broadcast(P))

    def l0_attention_prepare(self):
        W = 64
        self.sel0 = self.head_select("sel0", W, 8 ** -0.5)
        self.mask0_rest, self.mask0_first = self.window_mask("mask0_rest", W, 2)
        self.mask0 = self.sb("mask0", [P, 2 * W], BF16)
        self.kT0 = self.sb("kT0", [D, B, W + S])
        self.fill(self.kT0[:, :, 0:W], 0.0)
        self.qT0 = self.sb("qT0", [D, B, S])
        self.v0 = self.sb("v0", [P, B, S // W, 16, 9])
        self.fill(self.v0[:, :, :, :, 8:9], 1.0)
        self.oT0 = self.sb("oT0", [64, B, 2, S])
        self.lanes0 = lanes = []
        for b in range(B):
            t = dict(
                kt=self.sb(f"kt0_{b}", [D, 2 * W]), qx=self.sb(f"qx0_{b}", [D, 4, W]),
                mx=self.sb(f"mx0_{b}", [P, 8]), p=self.sb(f"p0_{b}", [P, 2, 8, P]),
                pt=self.sb(f"pt0_{b}", [P, 8, P]), r=self.sb(f"r0_{b}", [P, 8]),
                o=self.sb(f"o0_{b}", [P, 16, 8]))
            self.fill(t["o"][:, :, :], 0.0)
            lanes.append(t)

    ORDER0 = "fbBFF"
    WINDOWS = 4

    def l0_window_front(self, b, u, i, m, free):
        k, W, t = self, 64, self.lanes0[b]
        mask = k.mask0 if u == 0 else k.mask0_rest
        sc = k.bank(4 * b, 2)
        kt = k.copy([free.get("scores")], t["kt"][:, :], k.kT0[:, b, bass.ds(i * W, 2 * W)], k.G)
        q = k.tt([free.get("scores"), ASIDE], t["qx"][:, :, :],
                 k.qT0[:, b, bass.ds(i * W, W)].unsqueeze(1).broadcast_to([P, 4, W]),
                 k.sel0[:, :, :], ALU.mult)
        yield
        for half in range(2):
            k.mm([free.get("sub")], sc[:, half, :], k.identb[:, :],
                 mask[:, :].unsqueeze(1).broadcast_to([P, 4, 2 * W]), stop=False)
        done = {}
        for g in (0, 2, 1, 3):
            rows = slice(32 * g, 32 * g + 32)
            for pair in range(2):
                c = (g % 2 * 2 + pair) * P
                mm = k.mm([kt, q, done.get(g - 1)], sc[:, g // 2, c:c + P],
                          t["qx"][rows, 2 * pair:2 * pair + 2, :], t["kt"][rows, :],
                          start=False, signal=(pair == 1))
            done[g] = mm
        m["mask"] = free["scores"] = mm
        yield
        s3 = sc.rearrange("p a (g t) -> p (a g) t", t=P)
        p = t["p"][:, u % 2, :, :]
        k.reduce([mm, ASIDE], t["mx"][:, :], s3, ALU.max)
        d = free["sub"] = k.tt((), p, s3, t["mx"][:, :].unsqueeze(2).broadcast_to([P, 8, P]),
                               ALU.subtract)
        m["exp"] = k.act([d, ASIDE], p, p, ACT.Exp)

    def l0_window_back(self, b, u, i, m, free):
        k, W, t = self, 64, self.lanes0[b]
        bk = [k.bank(4 * b + 2 + j) for j in range(2)]
        c = []
        for gp in range(8):
            mm = k.tr([m["exp"], free.get("oT")], bk[gp // 4][:, (gp % 4) * P:(gp % 4 + 1) * P],
                      t["p"][:, u % 2, gp, :], signal=(gp % 4 == 3))
            if gp % 4 == 3:
                c.append(k.copy([mm, ASIDE], t["pt"][:, gp - 3:gp + 1, :], bk[gp // 4],
                                k.V if gp == 7 else k.A))
        yield
        tail = bk[0]
        for gp in range(8):
            mm = k.mm(c, tail[:, gp * 18:gp * 18 + 18], t["pt"][:, gp, :],
                      k.v0[:, b, bass.ds(i, 1), 2 * gp:2 * gp + 2, :]
                      .rearrange("p w h c -> p (w h c)"), signal=(gp == 7))
        for hp in range(2):
            rows = slice(64 * hp, 64 * hp + 64)
            pv = tail[rows, 0:144].rearrange("p (g c) -> p g c", c=18)[:, :, 9 * hp:9 * hp + 9]
            k.V.do([mm, ASIDE], k.nc.vector.reciprocal, t["r"][rows, :], pv[:, :, 8])
        for hp in range(2):
            rows = slice(64 * hp, 64 * hp + 64)
            pv = tail[rows, 0:144].rearrange("p (g c) -> p g c", c=18)[:, :, 9 * hp:9 * hp + 9]
            o = k.tt([ASIDE] if hp else (), t["o"][rows, 0:8, :], pv[:, :, 0:8],
                     t["r"][rows, :].unsqueeze(2).broadcast_to([64, 8, 8]), ALU.mult)
        yield
        mm = k.tr([o], bk[1][:, 0:P], t["o"][:, :, :].rearrange("p g d -> p (g d)"), signal=True)
        free["oT"] = k.copy([mm, ASIDE], k.oT0[:, b, :, bass.ds(i * W, W)],
                            bk[1][0:64, 0:P].rearrange("p (h q) -> p h q", h=2), k.A)

    def l0_attention(self):
        W, k = 64, self
        k.copy((), k.mask0[:, :], k.mask0_first[:, :])
        for b in range(B):
            x = k.nT0[:, b, W:W + S]
            for i, out in enumerate((k.qT0[:, b, :], k.kT0[:, b, W:W + S])):
                m = k.mm((), k.bank(4 * b + i), k.w0[:, i, :], x, signal=True)
                k.act([m], out, k.bank(4 * b + i), ACT.Identity, bias=k.b0[:, i:i + 1])
            for w in range(S // W):
                m = k.mm((), k.bank(4 * b + 2 + w // 4)[:, (w % 4) * P:(w % 4 + 1) * P],
                         k.nT0[:, b, w * W:w * W + 2 * W], k.w0[:, 2, :], signal=(w % 4 == 3))
                if w % 4 == 3:
                    k.tt([m, ASIDE], k.v0[:, b, w - 3:w + 1, :, 0:8],
                         k.bank(4 * b + 2 + w // 4).rearrange("p (w h d) -> p w h d", w=4, d=8),
                         k.bv0.rearrange("p (h d) -> p h d", d=8).unsqueeze(1)
                         .broadcast_to([P, 4, 16, 8]), ALU.add)
        k.meet()

        def body(i):
            at = i * k.WINDOWS

            def passed(kind, u, marks):
                if kind == "front" and u == 0:
                    k.copy([m["mask"] for m in marks], k.mask0[:, :], k.mask0_rest[:, :])

            pipeline(k.ORDER0, k.WINDOWS,
                     lambda b, u, m, free: k.l0_window_front(b, u, at + u, m, free),
                     lambda b, u, m, free: k.l0_window_back(b, u, at + u, m, free), passed)

        k.prog.loop_over("l0_attention", S // W // k.WINDOWS, body)
        for b in range(B):
            for hp in range(2):
                m = k.mm((), k.bank(b), k.wo0[:, hp, :], k.oT0[:, b, hp, :], start=(hp == 0),
                         stop=(hp == 1), signal=(hp == 1))
            k.act([m], k.sT[:, b * S:(b + 1) * S], k.bank(b), ACT.Identity, bias=k.b0[:, 2:3])

    def l0_ffn_load(self):
        io, p = self.io, self.prog
        self.c_q = Counter(p, "load_q", 16)
        self.c_f0 = Counter(p, "load_f0", 16)
        self.q0 = self.sb("q0", [D, 6, D], I32)
        self.sc0 = self.sb("sc0", [D, 6, D])
        self.la0, self.lb0 = self.sb("la0", [32, 6, D]), self.sb("lb0", [32, 6, D])
        self.load(self.c_q, self.q0[:, :, :], io["L0_qT"].rearrange("i d o -> d i o"), eng=self.A)
        self.load(self.c_q, self.sc0[:, :, :], io["L0_scT"].rearrange("i d o -> d i o"), eng=self.A)
        self.load(self.c_q, self.la0[:, :, :], io["L0_la"].rearrange("i r d -> r i d"), eng=self.A)
        self.load(self.c_q, self.lb0[:, :, :], io["L0_lbT"].rearrange("i r o -> r i o"), eng=self.A)
        self.fb_row = self.sb("fb_row", [1, 3, D])
        self.fb_col = self.sb("fb_col", [D, 6])
        self.ln_g0, self.ln_b0 = self.sb("ln_g0", [D, 3]), self.sb("ln_b0", [D, 3])
        self.load(self.c_f0, self.fb_row[:, :, :],
                  io["L0_fb"].rearrange("(j two) o -> two j o", two=2)[0:1], eng=self.A)
        self.load(self.c_f0, self.fb_col[:, :], io["L0_fbT"], eng=self.A)
        self.load(self.c_f0, self.ln_g0[:, :], io["L0_lngT"], eng=self.A)
        self.load(self.c_f0, self.ln_b0[:, :], io["L0_lnbT"], eng=self.A)

    def l0_ffn_weights(self):
        k = self
        self.wf0 = self.sb("wf0", [D, 6, D])
        k.ts([k.c_q.mark()], k.wf0[:, :, :], k.q0[:, :, :], 1 / 7.5, -1.0, ALU.mult, ALU.add)
        k.tt((), k.wf0[:, :, :], k.wf0[:, :, :], k.sc0[:, :, :], ALU.mult)
        for i in range(6):
            m = k.mm([k.c_q.mark()], k.bank(i // 4)[:, (i % 4) * P:(i % 4 + 1) * P], k.la0[:, i, :],
                     k.lb0[:, i, :], signal=(i in (3, 5)))
            if i == 3:
                k.tt([m], k.wf0[:, 0:4, :], k.wf0[:, 0:4, :],
                     k.bank(0).rearrange("p (i o) -> p i o", o=P), ALU.add)
        return k.tt([m], k.wf0[:, 4:6, :], k.wf0[:, 4:6, :],
                    k.bank(1)[:, 0:256].rearrange("p (i o) -> p i o", o=P), ALU.add)

    def l0_ffn(self):
        k = self

        def lane(b):
            tiles, c = range(b * TPB, (b + 1) * TPB), slice(b * S, (b + 1) * S)
            y, flipped, out = k.bank(b), k.bank(2 + b), k.bank(4 + b)
            y8 = k.bank(0, 2).rearrange("p a (t d) -> p (a t) d", d=D)
            h, last = k.nT0[:, b, 64:64 + S], k.c_f0.mark()
            for blk in range(3):
                w1, w2 = k.wf0[:, 2 * blk, :], k.wf0[:, 2 * blk + 1, :]
                k.mm([last], y, k.ones[0:1, :],
                     k.fb_row[:, blk, :].unsqueeze(1).broadcast_to([1, 4, D]), stop=False)
                for t in range(TPB):
                    m = k.mm((), y[:, t * P:(t + 1) * P], h[:, t * P:(t + 1) * P], w1, start=False,
                             signal=(t == TPB - 1))
                yield
                m = k.normalize([m], y8, k.normed, tiles)
                yield
                for t in range(TPB):
                    m = k.tr([m], flipped[:, t * P:(t + 1) * P], k.normed[:, b * TPB + t, :],
                             signal=(t == TPB - 1))
                g = k.act([m], k.aT[:, c], flipped, ACT.Gelu, bias=k.ln_b0[:, blk:blk + 1],
                          scale=k.ln_g0[:, blk:blk + 1])
                yield
                m = k.mm([g], out, w2, k.aT[:, c], signal=True)
                last = k.stt([m], k.hT[:, c], out, k.fb_col[:, 2 * blk + 1:2 * blk + 2], h, ALU.add,
                             ALU.add)
                h = k.hT[:, c]
                yield

        interleave(*(lane(b) for b in range(B)))

    def close_T(self, s, h):
        k = self
        k.meet()
        for half in range(2):
            c = slice(half * S, (half + 1) * S)
            a = k.act((), k.aT[:, c], h[:, c], ACT.Tanh, scale=0.5)
            v = k.stt([a], k.aT[:, c], k.aT[:, c], 1.0, h[:, c], ALU.add, ALU.mult)
            v = k.stt((), k.aT[:, c], k.aT[:, c], 0.5, s[:, c], ALU.mult, ALU.mult)
            for t in range(4):
                m = k.tr([v], k.bank(half)[:, t * P:(t + 1) * P],
                         k.aT[:, half * S + t * P:half * S + (t + 1) * P], signal=(t == 3))
            v = k.tt([m], k.xs[:, bass.ds(k.chunk * NT + 4 * half, 4), :],
                     k.x[:, 4 * half:4 * half + 4, :],
                     k.bank(half).rearrange("p (t d) -> p t d", d=D), ALU.add)
        k.meet()

    def close_R(self, s, f):
        k = self
        k.meet()
        t = k.normed
        a = k.act((), t[:, :, :], f, ACT.Tanh, scale=0.5)
        k.stt([a], t[:, :, :], t[:, :, :], 1.0, f, ALU.add, ALU.mult)
        k.stt((), t[:, :, :], t[:, :, :], 0.5, s, ALU.mult, ALU.mult)
        k.tt((), k.xs[:, bass.ds(k.chunk * NT, NT), :], k.x[:, :, :], t[:, :, :], ALU.add)
        k.meet()

    def open_layer(self, out, pad):
        k = self
        for b in range(B):
            m = k.normalize((), k.x, k.n, range(b * TPB, (b + 1) * TPB))
            for t in range(TPB):
                mm = k.tr([m], k.bank(b)[:, t * P:(t + 1) * P], k.n[:, b * TPB + t, :],
                          signal=(t == 3))
            k.copy([mm], out[:, b, pad:pad + S], k.bank(b), k.A)
        k.meet()

    def layer0_prepare(self):
        k = self
        k.l0_load()
        k.l0_ffn_load()
        k.nT0 = k.sb("nT0", [D, B, 64 + S])
        k.fill(k.nT0[:, :, 0:64], 0.0)
        k.l0_attention_prepare()
        k.l0_ffn_weights()

    def layer0(self):
        k = self
        k.open_layer(k.nT0, 64)
        k.l0_ffn()
        k.meet()
        k.l0_attention()
        k.close_T(k.sT, k.hT)

    def layer1_prepare(self):
        k, io = self, self.io
        c = Counter(self.prog, "load_l1", 16)
        k.w1 = k.sb("w1", [D, 10, 256])
        k.w3 = k.sb("w3", [D, 10, 256])
        k.w2 = k.sb("w2", [P, 10, 2, D])
        k.load(c, k.w1[:, :, :], io["L1_w1T"].rearrange("e d h -> d e h"))
        k.load(c, k.w3[:, :, :], io["L1_w3T"].rearrange("e d h -> d e h"), eng=k.A)
        k.load(c, k.w2[:, :, :, :], io["L1_w2T"].rearrange("e (m p) d -> p e m d", p=P))
        k.router = k.sb("router", [D, 8])
        k.router_b = k.sb("router_b", [1, 8])
        k.load(c, k.router[:, :], io["L1_routerT"])
        k.load(c, k.router_b[:, :], io["L1_eb"].rearrange("(a b) -> a b", a=1))
        k.rw = k.sb("rw", [D, 3, D])
        k.rwo = k.sb("rwo", [D, D])
        k.rp = k.sb("rp", [D, 5])
        for i, n in enumerate("kvr"):
            k.load(c, k.rw[:, i, :], io[f"L1_W{n}"], eng=k.A)
        k.load(c, k.rwo[:, :], io["L1_Wo"])
        for i, n in enumerate(("td", "tf", "tmk", "tmv", "tmr")):
            k.load(c, k.rp[:, i:i + 1], io["L1_" + n].rearrange("(a b) -> a b", b=1), eng=k.A)
        k.meet()
        k.td = k.sb("td", [D, 1])
        k.act((), k.td[:, :], k.rp[:, 0:1], ACT.Exp)
        k.ts([k.A.done.mark()], k.td[:, :], k.td[:, :], -1.0)
        k.rw_now, k.rw_before = k.sb("rw_now", [D, 3, D]), k.sb("rw_before", [D, 3, D])
        k.rest = k.sb("rest", [D, 3])
        k.ts((), k.rest[:, :], k.rp[:, 2:5], -1.0, 1.0, ALU.mult, ALU.add)
        for i in range(3):
            k.ts((), k.rw_now[:, i, :], k.rw[:, i, :], k.rp[:, 2 + i:3 + i])
            k.ts((), k.rw_before[:, i, :], k.rw[:, i, :], k.rest[:, i:i + 1])
        k.nT1 = k.sb("nT1", [D, B, 1 + S])
        k.fill(k.nT1[:, :, 0:1], 0.0)
        k.rank = k.sb("rank", [P, NT, 8])
        k.G.do((), k.nc.gpsimd.iota, k.rank[:, :, :], pattern=[[0, NT], [-1, 8]], base=8,
               channel_multiplier=0, allow_small_or_imprecise_dtypes=True)
        k.cw = k.sb("cw", [P, NT, 8])
        k.gated = k.sb("gated", [P, 2, S])
        k.hidden = k.sb("hidden", [P, 2, 2, N])
        k.route_scratch = [k.sb(f"route{i}", [P, NT, 8]) for i in range(4)]
        k.route_top = k.sb("route_top", [P, NT, 4])

    def time_mixing(self):
        k = self
        w = [x[:, :, :] for x in k.wide]
        kT, vT, rT, mx, num, den, mo, e1, e2, f1, f2 = w[:11]
        cols, prev = slice(1, 1 + S), slice(0, S)
        for b in range(B):
            marks = []
            for i in range(3):
                k.mm((), k.bank(2 * i + b), k.rw_now[:, i, :], k.nT1[:, b, cols], stop=False)
                marks.append(k.mm((), k.bank(2 * i + b), k.rw_before[:, i, :], k.nT1[:, b, prev],
                                  start=False, signal=True))
            k.act([marks[0]], kT[:, b, cols], k.bank(b), ACT.Identity)
            k.act([marks[1]], vT[:, b, cols], k.bank(2 + b), ACT.Identity)
            a = k.act([marks[2]], rT[:, b, cols], k.bank(4 + b), ACT.Tanh, scale=0.5)
        k.projected = a
        yield
        K, Vv, R = kT[:, :, cols], vT[:, :, cols], rT[:, :, cols]
        k.V.do((), k.nc.vector.memset, mx[:, :, 0:1], -1e38)
        k.V.do((), k.nc.vector.memset, num[:, :, 0:1], 0.0)
        k.V.do((), k.nc.vector.memset, den[:, :, 0:1], 0.0)
        scan = k.nc.vector.tensor_tensor_scan
        for b in range(B):
            v = k.V.do([a], scan, mx[:, b, cols], k.td[:, 0:1].broadcast_to([D, S]), kT[:, b, cols],
                       -1e38, ALU.add, ALU.max)
            yield
        mp, mn = mx[:, :, prev], mx[:, :, cols]
        F1, F2, E1, E2, MO = (x[:, :, cols] for x in (f1, f2, e1, e2, mo))
        g = k.tt([v], F2, K, mn, ALU.subtract, k.G)
        yield
        v = k.stt((), F1, mp, k.td[:, 0:1], mn, ALU.add, ALU.subtract)
        yield
        x2 = k.act([g], F2, F2, ACT.Exp)
        x1 = k.act([v], F1, F1, ACT.Exp)
        yield
        v = k.stt((), MO, K, k.rp[:, 1:2], mp, ALU.add, ALU.max)
        yield
        g = k.tt([v, x2], E1, F2, Vv, ALU.mult, k.G)
        yield
        v = k.stt((), E2, K, k.rp[:, 1:2], MO, ALU.add, ALU.subtract)
        yield
        y2 = k.act([v], E2, E2, ACT.Exp)
        yield
        for b in range(B):
            k.V.do([g, x1], scan, num[:, b, cols], f1[:, b, cols], e1[:, b, cols], 0.0,
                   ALU.mult, ALU.add)
            yield
            v = k.V.do([x2], scan, den[:, b, cols], f1[:, b, cols], f2[:, b, cols], 0.0,
                       ALU.mult, ALU.add)
            yield
        g = k.tt([v], MO, mp, MO, ALU.subtract, k.G)
        yield
        y1 = k.act([g], E1, MO, ACT.Exp)
        yield
        g = k.tt([y2, v], F2, E2, Vv, ALU.mult, k.G)
        yield
        k.tt([y1, g], F1, E1, num[:, :, prev], ALU.mult)
        yield
        k.tt((), F1, F1, F2, ALU.add)
        yield
        k.tt((), MO, E1, den[:, :, prev], ALU.mult)
        yield
        k.tt((), MO, MO, E2, ALU.add)
        yield
        k.V.do((), k.nc.vector.reciprocal, MO, MO)
        yield
        k.tt((), F1, F1, MO, ALU.mult)
        yield
        k.stt((), F1, R, 1.0, F1, ALU.add, ALU.mult)
        yield
        k.mixed = k.ts((), F1, F1, 0.5)

    def route(self):
        k = self
        z = k.bank(7)[:, 0:NT * 8]
        k.mm((), z, k.ones[0:1, :], k.router_b[:, :].unsqueeze(1).broadcast_to([1, NT, 8]), stop=False)
        for t in range(NT):
            m = k.mm((), z[:, 8 * t:8 * t + 8], k.nT1[:, t // 4, 1 + (t % 4) * P:1 + (t % 4 + 1) * P],
                     k.router[:, :], start=False, signal=(t == NT - 1))
        top = k.route_top
        l, c, one, two = (x[:, :, :] for x in k.route_scratch)
        full = [P, NT, 8]

        def col(i):
            return top[:, :, i:i + 1].broadcast_to(full)

        def first_largest(out, j):
            k.reduce((), top[:, :, j], l, ALU.max)
            k.tt((), c, l, col(j), ALU.is_ge)
            k.tt((), c, c, k.rank[:, :, :], ALU.mult)
            k.reduce((), top[:, :, 2], c, ALU.max)
            k.tt((), out, c, col(2), ALU.is_equal)

        k.logits_read = k.copy([m], l, z.rearrange("p (t e) -> p t e", e=8))
        first_largest(one, 0)
        k.stt((), l, one, -3e38, l, ALU.mult, ALU.add)
        first_largest(two, 1)
        v = k.tt((), top[:, :, 2], top[:, :, 1], top[:, :, 0], ALU.subtract)
        a = k.act([v], top[:, :, 2], top[:, :, 2], ACT.Exp)
        k.ts([a], top[:, :, 3], top[:, :, 2], 1.0, None, ALU.add)
        k.V.do((), k.nc.vector.reciprocal, top[:, :, 3], top[:, :, 3])
        k.tt((), one, one, col(3), ALU.mult)
        k.tt((), top[:, :, 3], top[:, :, 3], top[:, :, 2], ALU.mult)
        k.tt((), two, two, col(3), ALU.mult)
        v = k.tt((), k.cw[:, :, :], one, two, ALU.add)
        return k.ts((), k.cw[:, :, :], k.cw[:, :, :], 0.5)

    def experts(self):
        k = self
        t, g = k.gated, k.hidden
        free = {}
        acc_done, y_done, unit, pending = None, {}, 0, None

        def outputs(e):
            nonlocal acc_done
            marks = []
            for i in range(NT):
                for m in range(2):
                    mk = k.mm([acc_done, g_done[e]], k.bank(6 + i // 4)[:, (i % 4) * P:(i % 4 + 1) * P],
                              g[:, e % 2, m, i * P:(i + 1) * P], k.w2[:, e, m, :], start=(m == 0),
                              stop=(m == 1), signal=(m == 1 and i % 4 == 3))
                if i % 4 == 3:
                    marks.append(mk)
            y_done[e] = marks[1]
            y = k.bank(6, 2).rearrange("p a (t d) -> p (a t) d", d=D)
            if e >= 8:
                acc_done = k.stt([marks[1]], k.moe[:, :, :], y, 0.5, k.moe[:, :, :], ALU.mult, ALU.add)
                return
            for i in range(NT):
                need = [marks[i // 4]]
                if e == 0:
                    acc_done = k.ts(need, k.moe[:, i, :], y[:, i, :], k.cw[:, i, e:e + 1])
                else:
                    acc_done = k.stt(need, k.moe[:, i, :], y[:, i, :], k.cw[:, i, e:e + 1],
                                     k.moe[:, i, :], ALU.mult, ALU.add)

        g_done = {}
        for e in range(10):
            for b in range(B):
                x = k.nT1[:, b, 1:1 + S]
                for m in range(2):
                    p = unit % 3
                    h1, h3, ts_ = k.bank(2 * p), k.bank(2 * p + 1), t[:, unit % 2, :]
                    k.mm([free.get(p)], h1, k.w1[:, e, m * P:(m + 1) * P], x)
                    mk = k.mm((), h3, k.w3[:, e, m * P:(m + 1) * P], x, signal=True)
                    a = k.act([mk, free.get(("t", unit % 2))], ts_, h1, ACT.Tanh, scale=0.5)
                    v = k.stt([a], ts_, ts_, 1.0, h1, ALU.add, ALU.mult)
                    v = k.tt([y_done.get(e - 2)], g[:, e % 2, m, b * S:(b + 1) * S], ts_, h3,
                             ALU.mult)
                    free[p] = free["t", unit % 2] = v
                    unit += 1
                    yield
            g_done[e] = v
            if e:
                outputs(e - 1)
        outputs(9)
        for i in range(NT):
            k.mm([acc_done, k.mixed], k.bank(6 + i // 4)[:, (i % 4) * P:(i % 4 + 1) * P],
                 k.wide[9][:, i // 4, 1 + (i % 4) * P:1 + (i % 4 + 1) * P], k.rwo[:, :],
                 signal=(i == NT - 1))

    def layer1(self):
        k = self
        k.open_layer(k.nT1, 1)
        mixing = k.time_mixing()
        next(mixing)
        k.route()
        k.T.wait(k.projected, k.logits_read)
        interleave(k.experts(), mixing)
        k.close_R(k.bank(6, 2).rearrange("p a (t d) -> p (a t) d", d=D), k.moe[:, :, :])

    def sincos(self, ang, sin, cos, turns):
        k = self
        two_pi = 2 * np.pi
        c1 = 6.28125
        c2 = float(np.round((two_pi - c1) * 2.0 ** 20) / 2.0 ** 20)
        c3 = two_pi - c1 - c2
        nearest = 1.5 * 2.0 ** 23
        k.ts((), turns, ang, 1 / two_pi, nearest, ALU.mult, ALU.add)
        k.ts((), turns, turns, nearest, None, ALU.subtract)
        k.stt((), ang, turns, -c1, ang, ALU.mult, ALU.add)
        k.stt((), ang, turns, -c2, ang, ALU.mult, ALU.add)
        k.stt((), ang, turns, -c3, ang, ALU.mult, ALU.add)
        pi = float(np.nextafter(np.float32(np.pi), np.float32(0)))
        v = k.ts((), ang, ang, pi, -pi, ALU.min, ALU.max)
        k.act([v], sin, ang, ACT.Sin)
        a = k.act((), cos, ang, ACT.Sin, scale=0.5)
        k.tt([a], cos, cos, cos, ALU.mult)
        return k.ts((), cos, cos, -2.0, 1.0, ALU.mult, ALU.add)

    def layer2_prepare(self):
        k, io = self, self.io
        c = Counter(self.prog, "load_l2", 16)
        W = 32
        k.wqkv2 = k.sb("wqkv2", [D, 3, D])
        for i, n in enumerate("qkv"):
            k.load(c, k.wqkv2[:, i, :], io["L2_w" + n])
        k.wg2 = k.sb("wg2", [D, 3, 64])
        for i, n in enumerate("qkv"):
            k.load(c, k.wg2[:, i, :], io["L2_wg" + n], eng=k.A)
        k.rout2 = k.sb("rout2", [64, D])
        k.load(c, k.rout2[:, :], io["L2_rout"])
        k.wout2 = k.sb("wout2", [D, D])
        k.load(c, k.wout2[:, :], io["L2_wout"])
        k.wout2_hp = k.sb("wout2_hp", [32, 4, D])
        src = io["L2_wout"].rearrange("(g hp d) o -> g hp d o", hp=4, d=8)
        for g in range(4):
            k.load(c, k.wout2_hp[8 * g:8 * g + 8, :, :], src[g].rearrange("hp d o -> d hp o"), eng=k.A)
        k.gate_w = k.sb("gate_w", [D, 2])
        k.load(c, k.gate_w[:, 0:1], io["L2_gl"].rearrange("(a b) -> a b", b=1))
        k.load(c, k.gate_w[:, 1:2], io["L2_gr"].rearrange("(a b) -> a b", b=1))
        k.trig = k.sb("trig", [D, 2, D])
        noise = k.scratch[:, 0, 0, 0:256].rearrange("p (i o) -> p i o", i=2)
        k.load(c, k.trig[:, 0, :], io["L2_theta"])
        k.load(c, k.trig[:, 1, :], io["L2_phi"])
        k.load(c, noise[:, 0, :], io["L2_thetan"])
        k.load(c, noise[:, 1, :], io["L2_phin"])
        k.meet()
        k.tt((), k.trig[:, :, :], k.trig[:, :, :], noise, ALU.add)
        s, co, tu, an = (k.scratch[:, i, 0, 0:256] for i in range(1, 5))
        k.copy((), an, k.trig.rearrange("p i o -> p (i o)"))
        k.sincos(an, s, co, tu)
        k.copy((), k.trig[:, 0, :], co[:, 0:D])
        k.copy((), k.trig[:, 1, :], s[:, D:2 * D])
        k.ts((), k.wout2[:, :], k.wout2[:, :], 0.5)
        k.ts((), k.wout2_hp[:, :, :], k.wout2_hp[:, :, :], 0.5)
        k.sel2 = k.head_select("sel2", W, 8 ** -0.5)
        rest, first = k.window_mask("mask2w", W, 4)
        k.mask2_rest, k.mask2_first = (k.sb("mask2" + n, [P, 4, 2 * W], BF16)
                                       for n in ("_rest", "_first"))
        k.copy((), k.mask2_rest[:, :, :], rest[:, :].unsqueeze(1).broadcast_to([P, 4, 2 * W]), k.G)
        k.copy((), k.mask2_first[:, :, :], k.mask2_rest[:, :, :], k.G)
        k.copy((), k.mask2_first[:, 0, :], first[:, :], k.G)
        k.glw = k.sb("glw", [D, 4])
        k.fill(k.glw[:, :], 1.0)
        k.keep_where(k.glw[:, :], ALU.is_ge, 0.0, 0, [[-32, 4]], 1)
        k.keep_where(k.glw[:, :], ALU.is_ge, 0.0, 31, [[32, 4]], -1)
        k.ts((), k.glw[:, :], k.glw[:, :], k.gate_w[:, 0:1], eng=k.G)
        k.grw = k.sb("grw", [D, 16, 8])
        k.fill(k.grw[:, :, :], 1.0)
        k.keep_where(k.grw[:, :, :], ALU.is_ge, 0.0, 0, [[-8, 16], [0, 8]], 1)
        k.keep_where(k.grw[:, :, :], ALU.is_ge, 0.0, 7, [[8, 16], [0, 8]], -1)
        k.ts((), k.grw[:, :, :], k.grw[:, :, :], k.gate_w[:, 1:2], eng=k.G)
        k.selg = k.sb("selg", [64, 8, 64])
        k.fill(k.selg[:, :, :], 1.0)
        k.keep_where(k.selg[:, :, :], ALU.is_ge, 0.0, 0, [[-8, 8], [0, 64]], 1)
        k.keep_where(k.selg[:, :, :], ALU.is_ge, 0.0, 7, [[8, 8], [0, 64]], -1)
        k.maskg = k.sb("maskg", [P, TPB, 64], BF16)
        k.fill(k.maskg[:, :, :], 0.0)
        k.keep_where(k.maskg[:, :, :], ALU.is_ge, MASKED, 0, [[P, TPB], [-8, 64]], 1)
        k.half2 = k.sb("half2", [P, 2, 9])
        k.fill(k.half2[:, :, :], 1.0)
        k.keep_where(k.half2[:, :, :], ALU.is_ge, 0.0, 0, [[-64, 2], [0, 9]], 1)
        k.keep_where(k.half2[:, :, :], ALU.is_ge, 0.0, 63, [[64, 2], [0, 9]], -1)
        k.quad2 = k.sb("quad2", [P, 4, 9])
        k.fill(k.quad2[:, :, :], 1.0)
        k.keep_where(k.quad2[:, :, :], ALU.is_ge, 0.0, 0, [[-32, 4], [0, 9]], 1)
        k.keep_where(k.quad2[:, :, :], ALU.is_ge, 0.0, 31, [[32, 4], [0, 9]], -1)
        k.nT2 = k.sb("nT2", [D, B, W + S])
        k.fill(k.nT2[:, :, 0:W], 0.0)
        k.pool2 = k.sb("pool2", [D, B, 2, 64])
        k.gk2 = k.sb("gk2", [64, B, 8, 64])
        k.gv2 = k.sb("gv2", [P, B, 4, 2, 9])
        for b in range(B):
            k.copy((), k.gv2[:, b, :, :, 8:9], k.half2[:, :, 8:9].unsqueeze(1)
                   .broadcast_to([P, 4, 2, 1]), k.G)
        k.lanes2g = [dict(mx=k.sb(f"mx2g_{b}", [P, 8]), p=k.sb(f"p2g_{b}", [P, 8, 64]),
                          pt=k.sb(f"pt2g_{b}", [P, 4, P]), o=k.sb(f"o2g_{b}", [P, 8, 8]))
                     for b in range(4)]
        k.kT2 = k.sb("kT2", [D, B, W + S])
        k.fill(k.kT2[:, :, 0:W], 0.0)
        k.v2 = k.sb("v2", [P, B, 2 * TPB, 16, 9])
        k.fill(k.v2[:, :, :, :, 8:9], 1.0)
        k.oT2 = k.sb("oT2", [32, B, 4, S])
        k.lanes2 = []
        for b in range(B):
            t = dict(qx=k.sb(f"qx2_{b}", [D, 2, 4, 4, W]),
                     mx=k.sb(f"mx2_{b}", [P, 16]), r=k.sb(f"r2_{b}", [P, 16]),
                     p=k.sb(f"p2_{b}", [P, 2, 8, P]), pt=k.sb(f"pt2_{b}", [P, 8, P]),
                     gate=k.sb(f"gate2_{b}", [P, 16]), ox=k.sb(f"ox2_{b}", [P, 16, 36]),
                     os=k.sb(f"os2_{b}", [P, 16, 9]), o=k.sb(f"o2_{b}", [P, 4, 4, 8]))
            k.lanes2.append(t)

    def latent_attention(self):
        k = self
        qT, gr, gq, rem = (k.wide[i] for i in range(4))
        for b in range(B):
            x = k.nT2[:, b, 32:32 + S]
            m = k.mm((), k.bank(b), k.wqkv2[:, 0, :], x, signal=True)
            a = k.copy([m], qT[:, b, 0:S], k.bank(b), k.A)
            m = k.mm([a], k.bank(b), k.grw.rearrange("p h d -> p (h d)"), qT[:, b, 0:S], signal=True)
            k.act([m], gr[:, b, 0:S], k.bank(b), ACT.Tanh, scale=0.5)
            m = k.mm((), k.bank(2 + b)[0:64, :], k.wg2[:, 0, :], x, signal=True)
            k.act([m], gq[0:64, b, 0:S], k.bank(2 + b)[0:64, :], ACT.Identity, scale=8 ** -0.5)
            k.reduce((), k.pool2[:, b, 0, :], x.rearrange("p (n c) -> p n c", c=8), ALU.add)
        v = k.ts((), k.pool2[:, :, 0, :], k.pool2[:, :, 0, :], 1 / 8)
        v = k.copy((), k.pool2[:, :, 1, :], k.pool2[:, :, 0, :])
        for b in range(B):
            m = k.mm([v], k.bank(4)[0:64, b * 64:b * 64 + 64], k.wg2[:, 1, :], k.pool2[:, b, 0, :])
            m = k.mm((), k.bank(4)[:, 256 + b * 64:320 + b * 64],
                     k.pool2[:, b, :, :].rearrange("p i n -> p (i n)"), k.wg2[:, 2, :],
                     signal=True)
        for b in range(B):
            k.tt([m], k.gk2[:, b, :, :], k.bank(4)[0:64, b * 64:b * 64 + 64].unsqueeze(1)
                 .broadcast_to([64, 8, 64]), k.selg[:, :, :], ALU.mult)
            gv = k.tt((), k.gv2[:, b, :, :, 0:8], k.bank(4)[:, 256 + b * 64:320 + b * 64]
                      .rearrange("p (a h d) -> p a h d", a=4, h=2),
                      k.half2[:, :, 0:8].unsqueeze(1).broadcast_to([P, 4, 2, 8]), ALU.mult)
        k.meet()

        def lane(n, tiles):
            t = k.lanes2g[n]
            sc, small = k.bank(2 * n), k.bank(2 * n + 1)
            free = None
            for tile in tiles:
                cols = slice((tile % 4) * P, (tile % 4 + 1) * P)
                b = tile // 4
                k.mm([free], sc, k.identb[:, :], k.maskg[:, tile % 4, :].unsqueeze(1)
                     .broadcast_to([P, 8, 64]), stop=False)
                m = k.mm((), sc, gq[0:64, b, cols], k.gk2[:, b, :, :].rearrange("p h n -> p (h n)"),
                         start=False, signal=True)
                s3 = sc.rearrange("p (h n) -> p h n", n=64)
                k.reduce([m, ASIDE], t["mx"][:, :], s3, ALU.max)
                v = k.tt((), t["p"][:, :, :], s3, t["mx"][:, :].unsqueeze(2).broadcast_to([P, 8, 64]),
                         ALU.subtract)
                a = k.act([v, ASIDE], t["p"][:, :, :], t["p"][:, :, :], ACT.Exp)
                yield
                for pair in range(4):
                    m = k.tr([a], sc[:, pair * P:(pair + 1) * P],
                             t["p"][:, 2 * pair:2 * pair + 2, :].rearrange("p h n -> p (h n)"),
                             signal=(pair == 3))
                a = k.copy([m, ASIDE], t["pt"].rearrange("p a n -> p (a n)"), sc, k.A)
                yield
                for pair in range(4):
                    m = k.mm([a], small[:, pair * 18:pair * 18 + 18], t["pt"][:, pair, :],
                             k.gv2[:, b, pair, :, :].rearrange("p h c -> p (h c)"),
                             signal=(pair == 3))
                o = small[:, 0:72].rearrange("p (h c) -> p h c", c=9)
                k.V.do([m, ASIDE], k.nc.vector.reciprocal, t["mx"][:, :], o[:, :, 8])
                v = k.tt((), t["o"][:, :, :], o[:, :, 0:8],
                         t["mx"][:, :].unsqueeze(2).broadcast_to([P, 8, 8]), ALU.mult)
                yield
                m = k.tr([v], small[0:64, 128:256], t["o"][:, :, :].rearrange("p h d -> p (h d)"),
                         signal=True)
                free = k.copy([m, ASIDE], rem[0:64, b, cols], small[0:64, 128:256], k.A)
                yield

        interleave(*(lane(n, (2 * n, 2 * n + 1)) for n in range(4)))
        k.meet()
        for b in range(B):
            m = k.mm((), k.bank(b), k.rout2[:, :], rem[0:64, b, 0:S], signal=True)
            v = k.stt([m], gr[:, b, 0:S], gr[:, b, 0:S], 1.0, k.bank(b), ALU.add, ALU.mult)
            m = k.mm([v], k.bank(2 + b), k.wout2[:, :], gr[:, b, 0:S], signal=True)
            k.copy([m], k.sT[:, b * S:(b + 1) * S], k.bank(2 + b), k.A)

    ORDER2 = "FFbffFB"
    def l2_tile_front(self, b, i, m, free):
        k, W, t = self, 32, self.lanes2[b]
        mask = k.mask2_rest if i else k.mask2_first
        sc, qx = k.bank(4 * b, 2), t["qx"][:, i % 2]
        q = k.tt([free.get("gate"), ASIDE], qx, k.wide[0][:, b, i * P:(i + 1) * P]
                 .rearrange("p (j q) -> p j q", j=4).unsqueeze(2).broadcast_to([P, 4, 4, W]),
                 k.sel2[:, :, :].unsqueeze(1).broadcast_to([P, 4, 4, W]), ALU.mult)
        m["q"] = q
        yield
        for half in range(2):
            k.mm([free.get("sub")], sc[:, half, :], k.identb[:, :],
                 mask.rearrange("p j t -> p (j t)").unsqueeze(1).broadcast_to([P, 2, 8 * W]),
                 stop=False)
        done = {}
        for g in (0, 2, 1, 3):
            rows = slice(32 * g, 32 * g + 32)
            for j in range(4):
                c = (g % 2 * 4 + j) * 2 * W
                mm = k.mm([q, done.get(g - 1)], sc[:, g // 2, c:c + 2 * W],
                          qx[rows, j, :, :].rearrange("p h q -> p (h q)"),
                          k.kT2[rows, b, i * P + j * W:i * P + (j + 2) * W], start=False, signal=(j == 3))
            done[g] = mm
        yield
        s3 = sc.rearrange("p a (g t) -> p (a g) t", t=2 * W)
        k.reduce([mm, ASIDE], t["mx"][:, :], s3, ALU.max)
        p = t["p"][:, i % 2, :, :]
        d = free["sub"] = k.tt((), p.rearrange("p a (g t) -> p (a g) t", t=2 * W), s3,
                               t["mx"][:, :].unsqueeze(2).broadcast_to([P, 16, 2 * W]),
                               ALU.subtract)
        m["exp"] = k.act([d, ASIDE], p, p, ACT.Exp)

    def l2_tile_back(self, b, i, m, free):
        k, W, t = self, 32, self.lanes2[b]
        bk = [k.bank(4 * b + 2 + j) for j in range(2)]
        c = []
        for gj in range(8):
            mm = k.tr([m["exp"], free.get("oT"), free.get("banks")],
                      bk[gj // 4][:, (gj % 4) * P:(gj % 4 + 1) * P], t["p"][:, i % 2, gj, :],
                      signal=(gj % 4 == 3))
            if gj % 4 == 3:
                c.append(k.copy([mm, ASIDE], t["pt"][:, gj - 3:gj + 1, :], bk[gj // 4],
                                k.V if gj == 7 else k.A))
        yield
        for j in range(4):
            off = 288 + (j % 2) * 8 + j // 2
            mm = k.mm([m["q"], c[0]], bk[0][:, off:off + 7:2],
                      t["qx"][:, i % 2, j, :, :].rearrange("p h q -> p (h q)"), k.glw[:, :],
                      signal=(j == 3))
        ga = k.act([mm, ASIDE], t["gate"][:, :], bk[0][:, 288:304], ACT.Tanh,
                   scale=0.5 * 8 ** 0.5)
        for par, bank in ((1, bk[1]), (0, bk[0])):
            rows = slice(64 * par, 64 * par + 64)
            for gj in range(8):
                g, jp = gj // 2, gj % 2
                mm = k.mm([*c, ga if par == 0 else None], bank[:, gj * 36:gj * 36 + 36],
                          t["pt"][rows, gj, :],
                          k.v2[rows, b, 2 * i + jp, 4 * g:4 * g + 4, :].rearrange("p h c -> p (h c)"),
                          signal=(gj == 7))
            x = k.tt([mm, ASIDE], t["ox"][:, 8 * par:8 * par + 8, :], bank[:, 0:288]
                     .rearrange("p (g c) -> p g c", c=36),
                     k.quad2.rearrange("p h c -> p (h c)").unsqueeze(1).broadcast_to([P, 8, 36]),
                     ALU.mult)
        yield
        k.reduce((), t["os"][:, :, :], t["ox"].rearrange("p g (h c) -> p g c h", c=9), ALU.add)
        k.V.do((), k.nc.vector.reciprocal, t["r"][:, :], t["os"][:, :, 8])
        k.stt([ga], t["r"][:, :], t["gate"][:, :], 1.0, t["r"][:, :], ALU.add, ALU.mult)
        for par in range(2):
            gs = slice(8 * par, 8 * par + 8)
            o = k.tt([ASIDE] if par else (),
                     t["o"].rearrange("p (jp par) g d -> p par g jp d", par=2)[:, par],
                     t["os"][:, gs, 0:8].rearrange("p (g jp) d -> p g jp d", jp=2),
                     t["r"][:, gs].rearrange("p (g jp) -> p g jp", jp=2).unsqueeze(3)
                     .broadcast_to([P, 4, 2, 8]), ALU.mult)
        yield
        for j in range(4):
            mm = k.tr([o], bk[1][0:32, j * P:(j + 1) * P],
                      t["o"][:, j, :, :].rearrange("p g d -> p (g d)"), signal=(j == 3))
        free["banks"] = x
        free["oT"] = k.copy([mm, ASIDE], k.oT2[:, b, :, i * P:(i + 1) * P]
                            .rearrange("p h (j q) -> p h j q", j=4),
                            bk[1][0:32, :].rearrange("p (j h q) -> p h j q", j=4, h=4), k.A)

    def local_attention(self):
        k, W = self, 32
        k.meet()
        xv = k.scratch[:, 1:3, :, :].rearrange("p i b s -> p (i b s)")[:, 0:B * 1024]
        for b in range(B):
            n = k.nT2[:, b, 0:1]
            x = k.copy((), xv[:, b * 1024:(b + 1) * 1024].rearrange("p (j t) -> p j t", t=2 * W),
                       view(n, [[W, 4 * TPB], [1, 2 * W]]), (k.V, k.A)[b])
            m = k.mm((), k.bank(4 * b), k.wqkv2[:, 1, :], k.nT2[:, b, W:W + S], signal=True)
            k.copy([m], k.kT2[:, b, W:W + S], k.bank(4 * b), k.A)
            for j in range(2 * TPB):
                c = b * 1024 + j * P
                bank = k.bank(4 * b + 2 + j // 4)
                m = k.mm([x], bank[:, (j % 4) * P:(j % 4 + 1) * P], xv[:, c:c + P],
                         k.wqkv2[:, 2, :], signal=(j % 4 == 3))
                if j % 4 == 3:
                    k.copy([m], k.v2[:, b, j - 3:j + 1, :, 0:8],
                           bank.rearrange("p (w h d) -> p w h d", w=4, d=8), (k.V, k.A)[b])
        k.meet()

        pipeline(k.ORDER2, TPB, k.l2_tile_front, k.l2_tile_back)
        for b in range(B):
            for h in range(4):
                m = k.mm([k.A.done.mark(), k.V.done.mark()], k.bank(b), k.wout2_hp[:, h, :], k.oT2[:, b, h, :], start=(h == 0),
                         stop=(h == 3), signal=(h == 3))
            dst = k.sT[:, b * S:(b + 1) * S]
            k.tt([m], dst, dst, k.bank(b), ALU.add)

    def magnitude(self):
        k = self
        for t in range(NT):
            m = k.mm([k.V.done.mark()], k.bank(t // 2)[:, (t % 2) * 256:(t % 2 + 1) * 256],
                     k.nT2[:, t // 4, 32 + (t % 4) * P:32 + (t % 4 + 1) * P],
                     k.trig.rearrange("p i o -> p (i o)"), signal=(t == NT - 1))
        sq = k.wide_pair(0)
        flat = sq.rearrange("p a n -> p (a n)")
        k.act([m], flat, k.bank(0, 4).rearrange("p a n -> p (a n)"), ACT.Square)
        s4 = flat.rearrange("p (t i d) -> p t i d", t=NT, i=2)
        v = k.tt([k.A.done.mark()], k.moe[:, :, :], s4[:, :, 0, :], s4[:, :, 1, :], ALU.add)
        k.act([v], k.moe[:, :, :], k.moe[:, :, :], ACT.Sqrt)

    def layer2(self):
        k = self
        k.open_layer(k.nT2, 32)
        k.latent_attention()
        k.local_attention()
        k.magnitude()
        k.meet()
        for t in range(NT):
            m = k.tr((), k.bank(t // 4)[:, (t % 4) * P:(t % 4 + 1) * P], k.sT[:, t * P:(t + 1) * P],
                     signal=(t == NT - 1))
        k.close_R(k.bank(0, 2).rearrange("p a (t d) -> p (a t) d", d=D), k.moe[:, :, :])

    HEADS, DH = 16, 64

    def layer3_prepare(self):
        k, io, nc = self, self.io, self.nc
        H = k.HEADS
        c = Counter(self.prog, "load_l3", 16)

        k.gam, k.bet = k.sb("gam", [P, D]), k.sb("bet", [P, D])
        k.load(c, k.gam[:, :], io["L3_g"].partition_broadcast(P))
        k.load(c, k.bet[:, :], io["L3_b"].partition_broadcast(P))
        k.mscale = k.sb("mscale", [P, 1])
        k.load(c, k.mscale[:, :], io["L3_scale"].partition_broadcast(P))
        k.mu3 = k.sb("mu3", [D, 256])
        k.load(c, k.mu3[:, :], io["L3_mu"].rearrange("d e s -> d (e s)"))
        k.w1s, k.w2s = k.sb("w1s", [D, H, 32]), k.sb("w2s", [32, H, D])
        k.load(c, k.w1s[:, :, :], io["L3_w1"].rearrange("e d h -> d e h"), eng=k.A)
        k.load(c, k.w2s[:, :, :], io["L3_w2"].rearrange("e h d -> h e d"), eng=k.A)
        k.b1s, k.b2s = k.sb("b1s", [32, H]), k.sb("b2s", [D, H])
        k.load(c, k.b1s[:, :], io["L3_b1T"])
        k.load(c, k.b2s[:, :], io["L3_b2T"])
        par = k.sb("par", [H, 6])
        k.load(c, par[:, :], io["L3_par"])
        om = k.scratch[:, 0, 0, 0:512]
        k.load(c, om, io["L3_omega"].rearrange("h d -> (h d)").partition_broadcast(P))
        k.meet()
        sq, nrm = k.scratch[:, 1, 0, 0:256], k.scratch[:, 2, 0, 0:256]
        v = k.tt((), sq, k.mu3[:, :], k.mu3[:, :], ALU.mult)
        m = k.mm([v], k.bank(0)[:, 0:256], k.ones[:, :], sq, signal=True)
        v = k.ts([m], nrm, k.bank(0)[:, 0:256], 1e-24, None, ALU.max)
        a = k.act([v], nrm, nrm, ACT.Sqrt)
        k.V.do([a], nc.vector.reciprocal, nrm, nrm)
        k.tt((), k.mu3[:, :], k.mu3[:, :], nrm, ALU.mult)

        k.cosT = k.sb("cosT", [P, TPB, H, 32])
        k.sinT = k.sb("sinT", [P, TPB, H, 3, 32])
        tok = k.sb("tok", [P, TPB])
        g = k.G.do((), nc.gpsimd.iota, tok[:, :], pattern=[[P, TPB]], base=0, channel_multiplier=1,
                   allow_small_or_imprecise_dtypes=True)
        ang, turns = k.scratch[:, 1, 0, 0:512], k.scratch[:, 2, 0, 0:512]
        s, co = k.scratch[:, 3, 0, 0:512], k.scratch[:, 4, 0, 0:512]
        for t in range(TPB):
            k.ts([g], ang, om, tok[:, t:t + 1])
            k.sincos(ang, s, co, turns)
            k.copy((), k.cosT[:, t, :, :], co.rearrange("p (h d) -> p h d", d=32))
            s3 = s.rearrange("p (h d) -> p h d", d=32)
            for i, f in enumerate((1.0, -1.0, 1.0)):
                last = k.ts([k.A.done.mark()], k.sinT[:, t, :, i, :], s3, f)
            k.A.wait(last)

        k.coef = k.sb("coef", [P, H])
        layer = k.scope
        with ExitStack() as k.scope:
            k.head_tables(par)
        k.scope = layer
        k.ident_b0 = k.sb("zero", [P, 512], BF16)
        k.fill(k.ident_b0[:, :], 0.0)
        k.backwards = k.sb("backwards", [P, P])
        k.fill(k.backwards[:, :], 0.0)
        k.keep_where(k.backwards[:, :], ALU.not_equal, 1.0, 1 - P, [[1, P]], 1)
        k.nT3 = k.sb("nT3", [D, B, S])
        k.slotT = k.sb("slotT", [D, B, 256])
        k.hs = k.sb("hs", [32, H, 32])
        k.so = k.sb("so", [P, B, 2, D])
        k.small3 = [k.sb(f"small3_{i}", [P, NT, 16]) for i in range(3)]
        k.one3 = [k.sb(f"one3_{i}", [P, NT]) for i in range(3)]
        sizes = dict(qkv=2 * 1536, a=1024, b=1024, sq=1024, qT=512, kT=512, y=1280, pt=1280)
        spare = dict(a=k.aT[:, :], kT=k.sT[:, 0:512], qT=k.sT[:, 512:1024])
        other = k.sb("lane3", [P, sum(w for n, w in sizes.items() if n not in spare)])
        flat = k.scratch.rearrange("p i b s -> p (i b s)")
        k.lanes3 = []
        for b, mem in enumerate((flat, other)):
            t, at = {}, 0
            for n, w in sizes.items():
                if b == 1 and n in spare:
                    t[n] = spare[n]
                    continue
                t[n] = mem[:, at:at + w]
                at += w
            t["qkv"] = (t["qkv"][:, 0:1536], t["qkv"][:, 1536:3072])
            t["ek"] = bass.AP(tensor=t["b"].tensor, offset=t["b"].offset,
                              ap=[list(t["b"].ap[0]), [1, 1280]])
            t["nn"], t["qn"] = k.sb(f"nn3_{b}", [P, 2, 4, 2]), k.sb(f"qn3_{b}", [P, 2, 4])
            for n in ("mx", "sum"):
                t[n] = k.sb(f"{n}3_{b}", [P, 4])
            k.lanes3.append(t)
        k.head = [dict(w=k.sb(f"w3_{j}", [D, 3, P]), et=k.sb(f"et3_{j}", [P, 512]),
                       tb=k.sb(f"tb3_{j}", [P, 3, 512]),
                       front=k.lasting_counter(f"front{j}"), back=k.lasting_counter(f"back{j}"))
                  for j in range(2)]
        for j in range(2):
            k.load_front(j, j)
            k.load_back(j, j)

    def lasting_counter(self, name):
        c = Counter(self.prog, name, 16)
        self.prog.counters.remove(c)
        return c

    def head_tables(self, par):
        k, nc, H, X = self, self.nc, self.HEADS, 640
        a, e, v, w = (k.sb(f"ht{i}", [H, X]) for i in range(4))
        ar, er, vr, wr = (t[:, :] for t in (a, e, v, w))
        sp = k.sb("sp", [H, 4])
        u, o = k.sb("spu", [H, 4]), k.sb("spo", [H, 4])
        hp = k.sb("hp", [H, 8])
        mu, vs, nu, coef, icoef, rvn, half, tmp = (hp[:, i:i + 1] for i in range(8))
        raw = par[:, 1:5]
        q = k.stt((), u[:, :], raw, -1.0, raw, ALU.mult, ALU.max)
        q = k.act([q], u[:, :], u[:, :], ACT.Exp, scale=-1.0)
        k.ts([q], o[:, :], u[:, :], 1.0, None, ALU.add)
        q = k.act([k.V.done.mark()], sp[:, :], o[:, :], ACT.Ln)
        k.ts([q], o[:, :], o[:, :], 1.0, None, ALU.subtract)
        z = k.sb("spz", [H, 4])
        k.ts((), z[:, :], o[:, :], 0.0, None, ALU.is_equal)
        k.tt((), sp[:, :], sp[:, :], z[:, :], ALU.add)
        k.tt((), o[:, :], o[:, :], z[:, :], ALU.add)
        k.V.do((), nc.vector.reciprocal, o[:, :], o[:, :])
        k.tt((), sp[:, :], sp[:, :], o[:, :], ALU.mult)
        k.tt((), sp[:, :], sp[:, :], u[:, :], ALU.mult)
        q = k.stt((), sp[:, :], raw, 0.0, sp[:, :], ALU.max, ALU.add)
        q = k.act([q], mu, par[:, 0:1], ACT.Exp, scale=-1.0)
        k.ts([q], mu, mu, 1.0, None, ALU.add)
        k.V.do((), nc.vector.reciprocal, mu, mu)
        k.ts((), mu, mu, 1e-4, None, ALU.add)
        k.ts((), tmp, mu, 2.0)
        k.V.do((), nc.vector.reciprocal, tmp, tmp)
        k.tt((), vs, sp[:, 0:1], tmp, ALU.mult)
        k.tt((), half, sp[:, 1:2], sp[:, 2:3], ALU.add)
        k.copy((), nu, sp[:, 3:4])
        k.ts((), coef, nu, float(k.DH), -0.5, ALU.add, ALU.mult)
        k.tt((), coef, coef, par[:, 5:6], ALU.mult)
        k.stt((), tmp, coef, -1.0, coef, ALU.mult, ALU.max)
        k.ts((), tmp, tmp, 1e-8, None, ALU.is_lt)
        k.stt((), icoef, tmp, -1.0, coef, ALU.mult, ALU.mult)
        k.tt((), coef, coef, icoef, ALU.add)
        k.stt((), coef, tmp, 1e-8, coef, ALU.mult, ALU.add)
        k.V.do((), nc.vector.reciprocal, icoef, coef)
        q = k.G.do((), nc.gpsimd.iota, ar, pattern=[[-1, X]], base=512, channel_multiplier=0,
                   allow_small_or_imprecise_dtypes=True)
        q = k.stt([q], vr, ar, -1.0, ar, ALU.mult, ALU.max)
        k.ts([q], vr, vr, mu, -1.0, ALU.mult, ALU.mult)
        k.ts((), vr, vr, -30.0, None, ALU.max)
        future = k.sb("future", [H, X])
        k.ts((), future[:, :], ar, 0.0, -1e28, ALU.is_lt, ALU.mult)
        q = k.act([k.V.done.mark()], er, vr, ACT.Exp)
        k.ts([q], wr, vr, 1 / 8, 1.0, ALU.mult, ALU.add)
        for n in range(7, 1, -1):
            k.tt((), wr, wr, vr, ALU.mult)
            k.ts((), wr, wr, 1 / n, 1.0, ALU.mult, ALU.add)
        k.tt((), wr, wr, vr, ALU.mult)
        near = ar
        k.ts((), near, vr, -0.25, None, ALU.is_gt)
        k.ts((), vr, er, 1.0, None, ALU.subtract)
        k.tt((), wr, wr, vr, ALU.subtract)
        k.tt((), wr, wr, near, ALU.mult)
        k.tt((), er, er, wr, ALU.add)
        k.tt((), wr, wr, vr, ALU.add)
        k.stt((), vr, wr, 2.0, wr, ALU.add, ALU.mult)
        k.ts((), vr, vr, -1.0)
        k.ts((), vr, vr, vs, half, ALU.mult, ALU.add)
        k.V.do((), nc.vector.reciprocal, wr, er)
        k.ts((), ar, vr, nu)
        k.V.do((), nc.vector.reciprocal, ar, ar)
        k.tt((), ar, ar, er, ALU.mult)
        q = k.act([k.V.done.mark()], vr, vr, ACT.Ln)
        k.stt([q], vr, vr, -0.5 * k.DH, future[:, :], ALU.mult, ALU.add)
        k.ts((), vr, vr, icoef)
        q = k.V.done.mark()
        rows = nc.dram_tensor("head_rows", (H + 2, 4, X), F32).ap()
        cf = nc.dram_tensor("head_coef", (1, H + 2), F32).ap()
        k.c_rows = Counter(k.prog, "store_rows", 16)
        for i, t in enumerate((w, a, v, e)):
            k.load(k.c_rows, rows[0:H, i, :], t[:, :], need=[q])
            k.load(k.c_rows, rows[H:H + 2, i, :], t[0:2, :])
        k.load(k.c_rows, cf[0, 0:H], coef)
        k.load(k.c_rows, cf[0, H:H + 2], hp[0:2, 3:4])
        k.meet()
        k.rows = rows
        k.wvo = nc.dram_tensor("head_wvo", (H + 2, D, D), F32).ap()
        wv, wo, wvo = (k.scratch.rearrange("p i b s -> p (i b s)")[:, i * 2048:(i + 1) * 2048]
                       .rearrange("p (h c) -> p h c", c=D) for i in range(3))
        c = Counter(k.prog, "load_wvo", 16)
        c_out = Counter(k.prog, "store_wvo", 16)
        k.load(c, wv, k.io["L3_WvT"].rearrange("h r d -> r h d"))
        k.load(c, wo, k.io["L3_Wo"].rearrange("h r d -> r h d"), eng=k.A)
        for h in range(H):
            m = k.mm([c.mark()], k.bank(h // 4)[:, (h % 4) * P:(h % 4 + 1) * P], wv[:, h, :],
                     wo[:, h, :], signal=(h % 4 == 3))
        a = k.copy([m], wvo, k.bank(0, 4).rearrange("p a (t c) -> p (a t) c", c=D), k.A)
        k.load(c_out, k.wvo[0:H].rearrange("h d c -> d h c"), wvo, need=[a])
        k.load(c_out, k.wvo[H:H + 2].rearrange("h d c -> d h c"), wvo[:, 0:2, :])
        c = Counter(k.prog, "load_coef", 16)
        k.load(c, k.coef[:, :], cf[0, 0:H].partition_broadcast(P))
        k.meet()

    FRONT_LOADS, BACK_LOADS = 3, 1

    def spread(self, h, first, n):
        row = self.rows[bass.ds(h, 1), first, 1:2]
        return bass.AP(tensor=row.tensor, offset=row.offset, ap=[[1, P], [640, n], [1, 512]])

    def load_front(self, j, h):
        k, t = self, self.head[j]
        k.load(t["front"], t["w"][:, 0:2, :], k.io["L3_Wqk"][bass.ds(h, 1)]
               .rearrange("a d i c -> d (a i) c"))
        k.load(t["front"], t["w"][:, 2:3, :], k.wvo[bass.ds(h, 1)].rearrange("a d c -> d a c"))
        k.load(t["front"], t["et"][:, :], k.spread(h, 3, 1))

    def load_back(self, j, h):
        k, t = self, self.head[j]
        k.load(t["back"], t["tb"][:, :, :], k.spread(h, 0, 3))

    def soft_mixture(self):
        k, H = self, self.HEADS
        combine, dispatch, dspT, cT = (k.wide_pair(2 * i) for i in range(4))

        def lane(b):
            bank = [k.bank(4 * b + i) for i in range(4)]
            T4, c = slice(b * TPB, (b + 1) * TPB), slice(b * S, (b + 1) * S)
            tiles = range(b * TPB, (b + 1) * TPB)
            xn, xu, shape = k.normed, k.moe, [P, TPB, D]
            k.normalize((), k.n, xn, tiles)
            yield
            k.tt((), xn[:, T4, :], xn[:, T4, :], k.gam[:, :].unsqueeze(1).broadcast_to(shape),
                 ALU.mult)
            v = k.tt((), xn[:, T4, :], xn[:, T4, :], k.bet[:, :].unsqueeze(1).broadcast_to(shape),
                     ALU.add)
            ss, r, tot = (t[:, T4] for t in k.one3)
            a = k.act([v], xu[:, T4, :], xn[:, T4, :], ACT.Square)
            yield
            v = k.reduce([a], ss, xu[:, T4, :], ALU.add)
            k.ts([v], r, ss, 1e-24, None, ALU.max, eng=k.G)
            k.tt((), r, r, k.minus_half[:, 0:TPB], ALU.pow, eng=k.G)
            q = k.ts((), r, r, k.mscale[:, 0:1], eng=k.G)
            yield
            for i in tiles:
                v = k.ts([q, ASIDE], xu[:, i, :], xn[:, i, :], k.one3[1][:, i:i + 1])
            for n, i in enumerate(tiles):
                m = k.tr([v], bank[2][:, n * P:(n + 1) * P], xu[:, i, :], signal=(n == TPB - 1))
            a = k.copy([m], k.hT[:, c], bank[2], k.A)
            yield
            for n, i in enumerate(tiles):
                m = k.mm([a], bank[n // 2][:, (n % 2) * 256:(n % 2 + 1) * 256],
                         k.hT[:, i * P:(i + 1) * P], k.mu3[:, :], signal=(n == TPB - 1))
            for h in range(2):
                mt = k.mm((), bank[2 + h], k.mu3[:, h * P:(h + 1) * P], k.hT[:, c], signal=True)
            yield
            cmb = combine.rearrange("p a (t c) -> p (a t) c", c=256)[:, T4, :]
            lg = k.bank(4 * b, 2).rearrange("p a (t c) -> p (a t) c", t=2)
            k.reduce([m, ASIDE], ss, lg, ALU.max)
            v = k.ts((), ss, ss, -1.0)
            for n in range(TPB):
                w = k.act([v, ASIDE], cmb[:, n, :], lg[:, n, :], ACT.Exp, bias=ss[:, n:n + 1],
                          accum_out=tot[:, n:n + 1])
            smx, ssum = (t[:, b, 0:2] for t in k.small3[0:2])
            k.reduce([mt, ASIDE], smx, k.bank(4 * b + 2, 2), ALU.max)
            v = k.ts((), smx, smx, -1.0)
            for h in range(2):
                x = k.act([v, ASIDE], dspT[:, h, c], bank[2 + h], ACT.Exp, bias=smx[:, h:h + 1],
                          accum_out=ssum[:, h:h + 1])
            yield
            k.V.do([x], k.nc.vector.reciprocal, ssum, ssum)
            k.V.do([w, ASIDE], k.nc.vector.reciprocal, tot, tot)
            v = k.V.done.mark()
            for h in range(2):
                x = k.ts([v, ASIDE], dspT[:, h, c], dspT[:, h, c], ssum[:, h:h + 1])
            for n in range(TPB):
                y = k.ts([ASIDE], cmb[:, n, :], cmb[:, n, :], tot[:, n:n + 1])
            dsp = dispatch.rearrange("p a (t c) -> p (a t) c", c=256)[:, T4, :]
            dc = []
            for n, i in enumerate(tiles):
                for h in range(2):
                    m = k.tr([x], bank[n // 2][:, (n % 2) * 256 + h * P:(n % 2) * 256 + (h + 1) * P],
                             dspT[:, h, i * P:(i + 1) * P], signal=(h == 1 and n % 2 == 1))
                if n % 2:
                    dc.append(k.copy([m, ASIDE], dsp[:, n - 1:n + 1, :].rearrange("p t c -> p (t c)"),
                                     bank[n // 2], k.A))
            yield
            for n, i in enumerate(tiles):
                m = k.mm(dc, bank[2][:, 0:256], xn[:, i, :], dsp[:, n, :], start=(n == 0),
                         stop=(n == TPB - 1), signal=(n == TPB - 1))
            slot = k.slotT[:, b, :]
            a = k.copy([m], slot, bank[2][:, 0:256], k.A)
            cc = []
            for h in range(2):
                for n in range(TPB):
                    m = k.tr([y], bank[h][:, n * P:(n + 1) * P], cmb[:, n, h * P:(h + 1) * P],
                             signal=(n == TPB - 1))
                cc.append(k.copy([m, ASIDE], cT[:, h, c], bank[h], k.V if h else k.A))
            yield
            hs = k.hs[:, :, b * 16:(b + 1) * 16]
            for e in range(H):
                m = k.mm([a], bank[3][0:32, e * 16:(e + 1) * 16], k.w1s[:, e, :],
                         slot[:, e * 16:(e + 1) * 16], signal=(e == H - 1))
            v = k.tt([m], hs, bank[3][0:32, 0:256].rearrange("p (e c) -> p e c", c=16),
                     k.b1s[:, :].unsqueeze(2).broadcast_to([32, H, 16]), ALU.add)
            a = k.act([v], hs, hs, ACT.Gelu)
            yield
            for e in range(H):
                m = k.mm([a], bank[2][:, e * 16:(e + 1) * 16], k.w2s[:, e, :], hs[:, e, :],
                         signal=(e == H - 1))
            v = k.tt([m], slot.rearrange("p (e s) -> p e s", s=16),
                     bank[2][:, 0:256].rearrange("p (e s) -> p e s", s=16),
                     k.b2s[:, :].unsqueeze(2).broadcast_to([D, H, 16]), ALU.add)
            yield
            for h in range(2):
                m = k.tr([v], bank[3][:, h * P:(h + 1) * P], slot[:, h * P:(h + 1) * P],
                         signal=(h == 1))
            a = k.copy([m], k.so[:, b, :, :].rearrange("p h d -> p (h d)"), bank[3][:, 0:256], k.A)
            yield
            for n, i in enumerate(tiles):
                for h in range(2):
                    m = k.mm([a, *cc], bank[2][:, n * P:(n + 1) * P], cT[:, h, i * P:(i + 1) * P],
                             k.so[:, b, h, :], start=(h == 0), stop=(h == 1),
                             signal=(n == TPB - 1 and h == 1))
            k.copy([m], k.moe[:, T4, :].rearrange("p t d -> p (t d)"), bank[2], k.A)

        interleave(*(lane(b) for b in range(B)))

    def head_front(self, b, u, h, m, free):
        k, t, hd = self, self.lanes3[b], self.head[u % 2]
        bank = k.bank(4 * b)
        for e in (k.T, k.V):
            e.e.wait_ge(hd["front"].sem, 16 * k.FRONT_LOADS * (1 + u // 2))
        w, et = hd["w"].rearrange("d i c -> d (i c)"), hd["et"]
        v4 = t["qkv"][u % 2].rearrange("p (t c) -> p t c", t=4)
        own = free.get("banks_f", ())
        for i in range(4):
            mm = k.mm(own, bank[:, 0:384], k.nT3[:, b, i * P:(i + 1) * P], w, signal=True)
            own = [k.copy([mm, ASIDE], v4[:, i, :], bank[:, 0:384], k.A)]
            yield
        m["v"] = own
        a4, b4 = (t[n].rearrange("p (t c) -> p t c", t=4) for n in "ab")
        cs = k.cosT[:, :, bass.ds(h, 1), :].rearrange("p t a d -> p t (a d)")
        v = k.tt([*own, ASIDE], a4.rearrange("p t (r d) -> p t r d", d=32),
                 v4[:, :, 0:256].rearrange("p t (r d) -> p t r d", d=32),
                 cs.unsqueeze(2).broadcast_to([P, 4, 8, 32]), ALU.mult, k.G)
        sn = k.sinT[:, :, bass.ds(h, 1), :, :].rearrange("p t a i d -> p t (a i d)")
        q4 = v4[:, :, 0:256].rearrange("p t (i c) -> p t i c", i=2)
        r4 = t["b"].rearrange("p (t i c) -> p t i c", t=4, i=2)
        both = [P, 4, 2, 64]
        k.tt([*own, free.get("ek"), ASIDE], r4[:, :, :, 0:64], q4[:, :, :, 64:128],
             sn[:, :, 32:96].unsqueeze(2).broadcast_to(both), ALU.mult)
        v = k.tt([ASIDE], r4[:, :, :, 64:128], q4[:, :, :, 0:64],
                 sn[:, :, 0:64].unsqueeze(2).broadcast_to(both), ALU.mult)
        r = k.tt([v], t["a"], t["a"], t["b"], ALU.add, k.G)
        for i in range(4):
            for c in range(2):
                nn = k.act([*own, free.get("ek"), ASIDE], t["sq"][:, (2 * i + c) * P:(2 * i + c + 1) * P],
                           v4[:, i, c * P:(c + 1) * P], ACT.Square,
                           accum_out=t["nn"][:, u % 2, i, c:c + 1])
        yield
        mm = k.mm([nn], bank[:, 0:4], k.backwards[:, :], t["nn"][:, u % 2, :, 0], signal=True)
        qn = k.copy([mm, ASIDE], t["qn"][:, u % 2, :], bank[:, 0:4], k.A)
        for jj in range(4):
            m["ek"] = k.ts([nn, r, ASIDE],
                           t["ek"][:, k.AT_KEY[jj]:k.AT_KEY[jj + 1]], et[:, jj * P:512],
                           t["nn"][:, u % 2, jj, 1:2])
        yield
        qk = []
        need = [r, qn]
        for i, (n, f) in enumerate((("qT", -2.0), ("kT", 1.0))):
            for tt in range(4):
                mm = k.tr(need, bank[:, tt * P:(tt + 1) * P], a4[:, tt, i * P:(i + 1) * P],
                          signal=(tt == 3))
            out = t[n].rearrange("p (t c) -> p t c", t=4)
            if n == "qT":
                out = view(out[:, 0, P - 1:P], [[P, 4], [-1, P]])
            need = [k.act([mm, free.get("qk"), ASIDE], out,
                          bank.rearrange("p (t c) -> p t c", t=4), ACT.Identity, scale=f)]
            qk += need
            if i == 0:
                yield
        m["qk"] = qk
        m["qn"] = qn
        free["banks_f"] = need

    AT_QUERY = [0, 128, 384, 768, 1280]
    AT_KEY = [0, 512, 896, 1152, 1280]

    def head_back(self, b, u, m, free):
        k, t, hd, nc = self, self.lanes3[b], self.head[u % 2], self.nc
        bk = [k.bank(4 * b + 1 + i) for i in range(3)]
        at, pat, tb = k.AT_QUERY, k.AT_KEY, hd["tb"]
        v4 = t["qkv"][u % 2].rearrange("p (t c) -> p t c", t=4)
        k.V.e.wait_ge(hd["back"].sem, 16 * k.BACK_LOADS * (1 + u // 2))
        qn = m["qn"]
        need = [*m["qk"], m["ek"]]
        scored, ln, exp, flipped = {}, {}, {}, {}

        def y_of(i):
            return t["y"][:, at[i]:at[i + 1]]

        def cols(i):
            return slice(384 - i * P, 512)

        def scores(i):
            y, wd = y_of(i), (i + 1) * P
            ps = bk[i % 2][:, 0:wd]
            k.mm([*need, free.get(f"scores{i % 2}")], ps, t["qT"][:, i * P:(i + 1) * P],
                 t["kT"][:, 0:wd], stop=False)
            for jj in range(i + 1):
                c = pat[jj] + (3 - i) * P
                mm = k.tr((), ps[:, jj * P:(jj + 1) * P], t["ek"][:, c:c + P], start=False,
                          signal=(jj == i))
            free[f"scores{i % 2}"] = k.stt([mm, qn, free.get(f"y{i}"), ASIDE], y,
                                           tb[:, 0, cols(i)], t["qn"][:, u % 2, i:i + 1], ps,
                                           ALU.mult, ALU.add)
            v = k.stt((), y, y, 0.0, tb[:, 1, cols(i)], ALU.max, ALU.mult)
            ln[i] = k.act([v, ASIDE], y, y, ACT.Ln, bias=1.0)
            free["ek"] = free["qk"] = mm

        def softmax(i):
            y, mx = y_of(i), t["mx"][:, i:i + 1]
            k.V.do([ln[i], ASIDE], nc.vector.tensor_tensor_reduce, y, y, tb[:, 2, cols(i)],
                   k.coef_u[:, u:u + 1], -3e38, ALU.add, ALU.max, mx)
            v = k.ts((), mx, mx, -1.0)
            exp[i] = k.act([v, ASIDE], y, y, ACT.Exp, bias=mx, accum_out=t["sum"][:, i:i + 1])

        def flip(i):
            for jj in range(i + 1):
                mm = k.tr([exp[i], free.get("flip")], bk[2][:, jj * P:(jj + 1) * P],
                          y_of(i)[:, jj * P:(jj + 1) * P], signal=(jj == i))
            free[f"y{i}"] = mm
            flipped[i] = k.copy([mm, free.get(f"pt{i}"), ASIDE], t["pt"][:, at[i]:at[i + 1]],
                                bk[2][:, 0:(i + 1) * P], k.A if i != 2 else k.V)
            k.V.do([exp[i], ASIDE], nc.vector.reciprocal, t["sum"][:, i:i + 1],
                   t["sum"][:, i:i + 1])

        def values(i):
            for jj in range(i + 1):
                c = at[i] + jj * P
                mm = k.mm([flipped[i], *m["v"]], bk[2][:, 0:P], t["pt"][:, c:c + P],
                          v4[:, jj, 256:384], start=(jj == 0), stop=(jj == i), signal=(jj == i))
            free[f"pt{i}"] = mm
            n = k.n[:, b * TPB + i, :]
            free["flip"] = k.stt([mm], n, bk[2][:, 0:P], t["sum"][:, i:i + 1], n, ALU.mult,
                                 ALU.add)

        steps = ((0, scores), (3, values), (2, flip), (1, softmax))
        for slot in range(4 + 3):
            for behind, step in steps:
                if 0 <= slot - behind < 4:
                    step(3 - (slot - behind))
            if slot < 6:
                yield
        m["done"] = [k.T.done.mark(), k.V.done.mark()]

    ORDER3 = "bfBF"
    ROUND = 8

    def attention(self):
        k = self
        k.coef_u = k.small3[0][:, 0, 0:k.ROUND]
        k.meet()
        k.A.do((), k.nc.scalar.preload_act_table_set, "natural_log_exp_and_others")
        k.fill(k.n[:, :, :], 0.0)

        def body(i):
            first = i * k.ROUND
            k.copy((), k.coef_u, k.coef[:, bass.ds(first, k.ROUND)])

            def passed(kind, u, marks):
                for m in marks:
                    k.Y.wait(*((*m["qk"], m["ek"]) if kind == "front" else m["done"]))
                if u >= k.ROUND - 2:
                    k.Y.e.sem_clear(k.head[u % 2][kind].sem)
                (k.load_front if kind == "front" else k.load_back)(u % 2, first + u + 2)

            pipeline(k.ORDER3, k.ROUND,
                     lambda b, u, m, free: k.head_front(b, u, first + u, m, free),
                     k.head_back, passed, lead=4, first_stages=4, offset=0)

        k.prog.loop_over("heads", k.HEADS // k.ROUND, body)
        for b in range(B):
            for i in range(4):
                k.mm((), k.bank(6 + b)[:, i * P:(i + 1) * P], k.backwards[:, :],
                     k.n[:, b * TPB + i, :], signal=(i == 3))

    def layer3(self):
        k = self
        k.open_layer(k.nT3, 0)
        k.soft_mixture()
        k.attention()
        k.close_R(k.bank(6, 2).rearrange("p a (t d) -> p (a t) d", d=D), k.moe[:, :, :])

    def run(self, layers):
        k, p = self, self.prog
        with ExitStack() as k.scope:
            k.constants()
            k.norm_scratch()
            k.xs = k.sb("xs", [P, SEQS * TPB, D])
            load_x, store_x = Counter(p, "load_x", 16), Counter(p, "store_x", 16)
            for b in range(SEQS):
                k.load(load_x, k.xs[:, b * TPB:(b + 1) * TPB, :],
                       k.io["x"][b].rearrange("(t p) d -> p t d", p=P))
            k.x, k.n, k.sR, k.moe = (k.sb(n, [P, NT, D]) for n in ("x", "n", "sR", "moe"))
            k.sT, k.hT, k.aT = (k.sb(n, [D, N]) for n in ("sT", "hT", "aT"))
            k.scratch = k.sb("scratch", [D, 11, B, 1 + S])
            k.wide = [k.scratch[:, i, :, :] for i in range(11)]
            whole = k.scope
            for i in range(layers):
                with ExitStack() as k.scope:
                    prepare, layer = ((k.layer0_prepare, k.layer0), (k.layer1_prepare, k.layer1),
                                      (k.layer2_prepare, k.layer2), (k.layer3_prepare, k.layer3))[i]
                    prepare()

                    def chunk(c):
                        k.chunk = c
                        k.copy((), k.x[:, :, :], k.xs[:, bass.ds(c * NT, NT), :], k.A)
                        k.meet()
                        layer()

                    p.loop_over(f"layer{i}", CHUNKS, chunk)
                    if i == 3:
                        for head in k.head:
                            k.Y.e.wait_ge(head["front"].sem, 16 * k.FRONT_LOADS)
                            k.Y.e.wait_ge(head["back"].sem, 16 * k.BACK_LOADS)
                k.scope = whole
            for b in range(SEQS):
                k.load(store_x, k.io["out"][b].rearrange("(t p) d -> p t d", p=P),
                       k.xs[:, b * TPB:(b + 1) * TPB, :])
            k.Y.wait(store_x.mark())


def build(nc, inputs):
    io = {n: nc.dram_tensor("in_" + n, a.shape, mybir.dt.from_np(a.dtype), kind="ExternalInput").ap()
          for n, a in inputs.items()}
    io["out"] = nc.dram_tensor("out_0", (SEQS, S, D), F32, kind="ExternalOutput").ap()
    k = Kernel(nc, io)
    k.run(LAYERS)


def lay_out_more(a, r, c):
    for i in (1, 3, 2):
        w = np.concatenate([a[f"L1_ffn_w{i}"], a[f"L1_ffn_sw{i}"]])
        r[f"L1_w{i}T"] = w.transpose(0, 2, 1)
    r["L1_routerT"] = a["L1_ffn_router_w"].T
    r["L1_eb"] = a["L1_ffn_expert_bias"]
    for n in ("Wk", "Wv", "Wr", "Wo"):
        r["L1_" + n] = a["L1_attn_" + n]
    for n, m in (("td", "time_decay"), ("tf", "time_first"), ("tmk", "time_mix_key"),
                 ("tmv", "time_mix_value"), ("tmr", "time_mix_receptance")):
        r["L1_" + n] = a["L1_attn_" + m]
    for n in ("wq", "wk", "wv", "wgq", "wgk", "wgv"):
        r["L2_" + n] = a["L2_attn_" + n]
    r["L2_rout"] = a["L2_attn_r_out_w"]
    r["L2_wout"] = a["L2_attn_w_out"]
    r["L2_gl"] = a["L2_attn_gate_local_w"].reshape(-1)
    r["L2_gr"] = a["L2_attn_gate_remote_w"].reshape(-1)
    for n, m in (("theta", "theta"), ("phi", "phi"), ("thetan", "theta_noise"), ("phin", "phi_noise")):
        r["L2_" + n] = a["L2_ffn_" + m]
    w = np.stack([a[f"L3_attn_W{n}"].reshape(D, 2, 16, 64) for n in "qk"])
    w = w.transpose(3, 1, 0, 2, 4).reshape(16, D, 2, P)
    r["L3_Wqk"] = np.concatenate([w, w[:2]])
    r["L3_WvT"] = a["L3_attn_Wv"].reshape(D, 2, 16, 64).transpose(2, 1, 3, 0).reshape(16, P, D)
    r["L3_Wo"] = a["L3_attn_Wo"].reshape(2, 16, 64, D).transpose(1, 0, 2, 3).reshape(16, P, D)
    r["L3_par"] = np.stack([a["L3_attn_" + n] for n in (
        "mu_raw", "sigma_raw", "eta_raw", "gamma_raw", "nu_raw", "tau")], axis=1)
    r["L3_omega"] = a["L3_attn_omega"]
    r["L3_g"], r["L3_b"] = a["L3_ffn_ln_gamma"], a["L3_ffn_ln_beta"]
    r["L3_scale"] = a["L3_ffn_scale"]
    r["L3_mu"], r["L3_w1"], r["L3_w2"] = (a["L3_ffn_" + n] for n in ("mu", "w1", "w2"))
    r["L3_b1T"], r["L3_b2T"] = a["L3_ffn_b1"].T, a["L3_ffn_b2"].T


def lay_out(a):
    c = np.ascontiguousarray
    r = {"x": a["L0_attn_x"]}
    for n in "qkvo":
        r[f"L0_W{n}T"] = c(a[f"L0_attn_W{n}"].T)
        r[f"L0_b{n}"] = a[f"L0_attn_b{n}"]
    r["L0_qT"] = c(a["L0_ffn_qweights"].transpose(0, 2, 1))
    r["L0_scT"] = c(np.repeat(a["L0_ffn_scales"], 16, axis=2).transpose(0, 2, 1))
    r["L0_la"] = a["L0_ffn_lora_a"]
    r["L0_lbT"] = c(a["L0_ffn_lora_b"].transpose(0, 2, 1))
    r["L0_fb"] = a["L0_ffn_biases"]
    r["L0_fbT"] = c(a["L0_ffn_biases"].T)
    r["L0_lngT"] = c(a["L0_ffn_ln_gamma"].T)
    r["L0_lnbT"] = c(a["L0_ffn_ln_beta"].T)
    lay_out_more(a, r, c)
    return {k: c(v) for k, v in r.items()}


def kernel(**inputs):
    import concourse.bacc as bacc
    from concourse.bass_utils import run_bass_kernel_spmd as run

    nc = bacc.Bacc("TRN2", target_bir_lowering=False, num_devices=1)
    arrays = lay_out({k: np.asarray(v) for k, v in inputs.items()})
    build(nc, arrays)
    r = run(nc, [{"in_" + n: v for n, v in arrays.items()}], core_ids=[0])
    return r.results[0]["out_0"]
```
